# Optimizing a Trainium2 kernel written in Bass

```python
import numpy as np
import jax
import jax.numpy as jnp

def _softmax(x, axis=-1):
    return jax.nn.softmax(x, axis=axis)

def _gelu(x):
    return jax.nn.gelu(x, approximate=True)

def _silu(x):
    return jax.nn.silu(x)

def _sigmoid(x):
    return jax.nn.sigmoid(x)

def _layernorm(x, axis=-1, eps=1e-05):
    m = jnp.mean(x, axis=axis, keepdims=True)
    v = jnp.var(x, axis=axis, keepdims=True)
    return (x - m) / jnp.sqrt(v + eps)

def _scatter_add(tgt, idx, src, axis=0):
    return tgt.at[idx].add(src)

def _segment_sum(src, seg, n):
    return jax.ops.segment_sum(src, seg, n)
kernel_name = 'mk_seq_postln_d4_jaxref_r8_c793d2'

def setup_inputs(seed: int=0):
    np.random.seed(seed)
    _w = jnp.asarray

    def _L0_attn_setup():
        import jax, jax.numpy as jnp
        import numpy as np
        N_HEAD = 16
        key = jax.random.key(seed)
        ks = jax.random.split(key, 10)
        C = 128
        B, T = (4, 1024)
        s = 1.0 / np.sqrt(C)
        return {'x': jax.random.normal(ks[0], (B, T, C), dtype=jnp.float32), 'Wq': jax.random.normal(ks[1], (C, C), dtype=jnp.float32) * s, 'bq': jax.random.normal(ks[2], (C,), dtype=jnp.float32) * s, 'Wk': jax.random.normal(ks[3], (C, C), dtype=jnp.float32) * s, 'bk': jax.random.normal(ks[4], (C,), dtype=jnp.float32) * s, 'Wv': jax.random.normal(ks[5], (C, C), dtype=jnp.float32) * s, 'bv': jax.random.normal(ks[6], (C,), dtype=jnp.float32) * s, 'Wp': jax.random.normal(ks[7], (C, C), dtype=jnp.float32) * s, 'bp': jax.random.normal(ks[8], (C,), dtype=jnp.float32) * s}
    _L0_attn_in = _L0_attn_setup()

    def _L0_ffn_setup():
        import jax, jax.numpy as jnp
        import numpy as np
        N_EMBD = 128
        N_STATE = 512
        key = jax.random.key(seed)
        k_x, k_w1, k_b1, k_w2, k_b2 = jax.random.split(key, 5)
        x = jax.random.normal(k_x, (4, 256, N_EMBD), dtype=jnp.float32)
        w1 = jax.random.normal(k_w1, (N_EMBD, N_STATE), dtype=jnp.float32) * (1.0 / np.sqrt(N_EMBD))
        b1 = jax.random.normal(k_b1, (N_STATE,), dtype=jnp.float32) * 0.02
        w2 = jax.random.normal(k_w2, (N_STATE, N_EMBD), dtype=jnp.float32) * (1.0 / np.sqrt(N_STATE))
        b2 = jax.random.normal(k_b2, (N_EMBD,), dtype=jnp.float32) * 0.02
        return {'x': x, 'w1': w1, 'b1': b1, 'w2': w2, 'b2': b2}
    _L0_ffn_in = _L0_ffn_setup()

    def _L1_attn_setup():
        import jax, jax.numpy as jnp
        import numpy as np
        D_MODEL = 128
        N_HEADS = 16
        D_K = 64
        key = jax.random.key(seed)
        k0, k1, k2, k3, k4 = jax.random.split(key, 5)
        B, S = (4, 512)
        std = 0.02
        x = jax.random.normal(k0, (B, S, D_MODEL), dtype=jnp.float32)
        W_q = std * jax.random.normal(k1, (N_HEADS * D_K, D_MODEL), dtype=jnp.float32)
        W_k = std * jax.random.normal(k2, (N_HEADS * D_K, D_MODEL), dtype=jnp.float32)
        W_v = std * jax.random.normal(k3, (N_HEADS * D_K, D_MODEL), dtype=jnp.float32)
        W_o = std * jax.random.normal(k4, (D_MODEL, N_HEADS * D_K), dtype=jnp.float32)
        return {'x': x, 'W_q': W_q, 'W_k': W_k, 'W_v': W_v, 'W_o': W_o}
    _L1_attn_in = _L1_attn_setup()

    def _L1_ffn_setup():
        import jax, jax.numpy as jnp
        import numpy as np
        B, S, H, F, E, K = (4, 256, 128, 448, 8, 2)
        CAP_FACTOR = 1.25

        def _moe_forward(hidden_states, gate_w, w1, w2, w3):
            b, s, h = hidden_states.shape
            dtype = hidden_states.dtype
            x = hidden_states.reshape(-1, h)
            router_logits = x @ gate_w.T
            expert_weights = jax.nn.softmax(router_logits.astype(jnp.float32), axis=1)
            _, selected_experts = jax.lax.top_k(expert_weights, K)
            top_k_idx = selected_experts.reshape(b, s, K)
            probs = expert_weights.reshape(b, s, E)
            capacity = int(s * K / E * CAP_FACTOR)
            expert_mask = jax.nn.one_hot(top_k_idx, E, dtype=jnp.int32)
            mask_fused = expert_mask.reshape(b, s * K, E)
            count_fused = jnp.cumsum(mask_fused, axis=1)
            count = count_fused.reshape(b, s, K, E)
            trunc_mask = expert_mask * (count <= capacity).astype(jnp.int32)
            combined_mask = trunc_mask.sum(axis=2)
            masked_probs = probs * combined_mask
            pos_fused = mask_fused * count_fused
            pos = pos_fused.reshape(b, s, K, E)
            combined_pos = pos.sum(axis=2) * combined_mask
            pos_in_cap = jax.nn.one_hot(combined_pos, capacity + 1, dtype=jnp.int32)
            combine_mask = masked_probs[..., None] * pos_in_cap
            combine_mask = combine_mask[..., 1:].astype(dtype)
            dispatch_mask = (combine_mask != 0).astype(dtype)
            dispatch = jnp.einsum('bsm,bsec->ebcm', hidden_states, dispatch_mask)
            h1 = jnp.einsum('ebcm,emh->ebch', dispatch, w1)
            h3 = jnp.einsum('ebcm,emh->ebch', dispatch, w3)
            expert_out = jnp.einsum('ebch,ehm->ebcm', jax.nn.silu(h1) * h3, w2)
            final = jnp.einsum('ebcm,bsec->bsm', expert_out, combine_mask)
            return final
        key = jax.random.key(seed)
        k1, k2, k3, k4, k5 = jax.random.split(key, 5)
        s_h = 1.0 / np.sqrt(H)
        s_f = 1.0 / np.sqrt(F)
        return {'hidden_states': jax.random.normal(k1, (B, S, H), dtype=jnp.float32), 'gate_w': jax.random.normal(k2, (E, H), dtype=jnp.float32) * s_h, 'w1': jax.random.normal(k3, (E, H, F), dtype=jnp.float32) * s_h, 'w2': jax.random.normal(k4, (E, F, H), dtype=jnp.float32) * s_f, 'w3': jax.random.normal(k5, (E, H, F), dtype=jnp.float32) * s_h}
    _L1_ffn_in = _L1_ffn_setup()

    def _L2_attn_setup():
        import jax, jax.numpy as jnp
        import numpy as np
        import math
        D_MODEL = 128
        D_STATE = 64
        DT_MIN, DT_MAX = (0.001, 0.1)
        key = jax.random.key(seed)
        ks = jax.random.split(key, 8)
        x = jax.random.normal(ks[0], (2, 512, D_MODEL), dtype=jnp.float32)
        lim = 1.0 / math.sqrt(D_MODEL)
        Win = jax.random.uniform(ks[1], (D_MODEL, D_MODEL), minval=-lim, maxval=lim, dtype=jnp.float32)
        bin_ = jax.random.uniform(ks[2], (D_MODEL,), minval=-lim, maxval=lim, dtype=jnp.float32)
        Wout = jax.random.uniform(ks[3], (D_MODEL, D_MODEL), minval=-lim, maxval=lim, dtype=jnp.float32)
        bout = jax.random.uniform(ks[4], (D_MODEL,), minval=-lim, maxval=lim, dtype=jnp.float32)
        A_log = jnp.broadcast_to(jnp.log(jnp.arange(1, D_STATE + 1, dtype=jnp.float32)), (D_MODEL, D_STATE))
        B = 0.1 * jax.random.normal(ks[5], (D_MODEL, D_STATE), dtype=jnp.float32)
        C = 0.1 * jax.random.normal(ks[6], (D_MODEL, D_STATE), dtype=jnp.float32)
        Dp = jnp.ones((D_MODEL,), dtype=jnp.float32)
        log_dt = jax.random.uniform(ks[7], (D_MODEL,), dtype=jnp.float32) * (math.log(DT_MAX) - math.log(DT_MIN)) + math.log(DT_MIN)
        dt = jnp.exp(log_dt)
        return {'x': x, 'Win': Win, 'bin_': bin_, 'A_log': A_log, 'B': B, 'C': C, 'Dp': Dp, 'dt': dt, 'Wout': Wout, 'bout': bout}
    _L2_attn_in = _L2_attn_setup()

    def _L2_ffn_setup():
        import jax, jax.numpy as jnp
        import numpy as np
        LN_EPS = 0.001
        EPS = 1e-05
        QB = 128.0

        def ste_round(x):
            return x + jax.lax.stop_gradient(jnp.round(x) - x)
        key = jax.random.key(seed)
        k1, k2 = jax.random.split(key)
        x = jax.random.normal(k1, (4, 1024, 128), dtype=jnp.float32)
        weight = jax.random.normal(k2, (128, 128), dtype=jnp.float32) * 0.02
        ln_gamma = jnp.ones((128,), dtype=jnp.float32)
        ln_beta = jnp.zeros((128,), dtype=jnp.float32)
        return {'x': x, 'weight': weight, 'ln_gamma': ln_gamma, 'ln_beta': ln_beta}
    _L2_ffn_in = _L2_ffn_setup()

    def _L3_attn_setup():
        import jax, jax.numpy as jnp
        from jax import lax
        import numpy as np
        D_MODEL = 128
        D_STATE = 64
        D_CONV = 4
        EXPAND = 2
        HEADDIM = 64
        D_INNER = EXPAND * D_MODEL
        NHEADS = D_INNER // HEADDIM
        CHUNK = 64
        CONV_DIM = D_INNER + 2 * D_STATE
        D_IN_PROJ = 2 * D_INNER + 2 * D_STATE + NHEADS
        B_SZ = 4
        SEQLEN = 256
        EPS = 1e-05

        def _silu(x):
            return x * jax.nn.sigmoid(x)

        def _segsum(x):
            T = x.shape[-1]
            xe = jnp.broadcast_to(x[..., None], x.shape + (T,))
            strict_lower = jnp.tril(jnp.ones((T, T), bool), -1)
            xe = jnp.where(strict_lower, xe, 0.0)
            s = jnp.cumsum(xe, axis=-2)
            lower = jnp.tril(jnp.ones((T, T), bool), 0)
            return jnp.where(lower, s, -jnp.inf)
        key = jax.random.key(seed)
        ks = jax.random.split(key, 5)
        u = jax.random.normal(ks[0], (B_SZ, SEQLEN, D_MODEL), jnp.float32)
        W_in = jax.random.normal(ks[1], (D_IN_PROJ, D_MODEL), jnp.float32) * 0.02
        conv_w = jax.random.normal(ks[2], (CONV_DIM, 1, D_CONV), jnp.float32) * 0.2
        conv_b = jnp.zeros((CONV_DIM,), jnp.float32)
        dt_bias = jax.random.uniform(ks[3], (NHEADS,), jnp.float32, -1.0, 1.0)
        A_log = jnp.log(jnp.linspace(1.0, float(NHEADS), NHEADS)).astype(jnp.float32)
        D = jnp.ones((NHEADS,), jnp.float32)
        norm_w = jnp.ones((D_INNER,), jnp.float32)
        W_out = jax.random.normal(ks[4], (D_MODEL, D_INNER), jnp.float32) * 0.02
        return dict(u=u, W_in=W_in, conv_w=conv_w, conv_b=conv_b, dt_bias=dt_bias, A_log=A_log, D=D, norm_w=norm_w, W_out=W_out)
    _L3_attn_in = _L3_attn_setup()

    def _L3_ffn_setup():
        import jax, jax.numpy as jnp
        import numpy as np
        DIM = 128

        def _reference_tuple_inner(x, W_r, W_k, W_v, mu_r, mu_k):
            B, T, C = x.shape
            x_prev = jnp.concatenate([jnp.zeros((B, 1, C), x.dtype), x[:, :-1, :]], axis=1)
            xr = mu_r * x + (1.0 - mu_r) * x_prev
            xk = mu_k * x + (1.0 - mu_k) * x_prev
            r = jax.nn.sigmoid(jnp.einsum('btc,dc->btd', xr, W_r))
            k = jnp.einsum('btc,dc->btd', xk, W_k)
            k_act = jnp.square(jax.nn.relu(k))
            out = r * jnp.einsum('btc,dc->btd', k_act, W_v)
            new_state = x[:, -1, :]
            return (out, new_state)
        key = jax.random.key(seed)
        ks = jax.random.split(key, 6)
        B, T, C = (8, 256, DIM)
        x = jax.random.normal(ks[0], (B, T, C), dtype=jnp.float32)
        s = 1.0 / np.sqrt(C)
        W_r = jax.random.uniform(ks[1], (C, C), jnp.float32, -s, s)
        W_k = jax.random.uniform(ks[2], (C, C), jnp.float32, -s, s)
        W_v = jax.random.uniform(ks[3], (C, C), jnp.float32, -s, s)
        mu_r = jax.random.uniform(ks[4], (C,), jnp.float32)
        mu_k = jax.random.uniform(ks[5], (C,), jnp.float32)
        return {'x': x, 'W_r': W_r, 'W_k': W_k, 'W_v': W_v, 'mu_r': mu_r, 'mu_k': mu_k}
    _L3_ffn_in = _L3_ffn_setup()
    _d = {'L0_attn_x': _L0_attn_in['x'], 'L0_attn_Wq': _L0_attn_in['Wq'], 'L0_attn_bq': _L0_attn_in['bq'], 'L0_attn_Wk': _L0_attn_in['Wk'], 'L0_attn_bk': _L0_attn_in['bk'], 'L0_attn_Wv': _L0_attn_in['Wv'], 'L0_attn_bv': _L0_attn_in['bv'], 'L0_attn_Wp': _L0_attn_in['Wp'], 'L0_attn_bp': _L0_attn_in['bp'], 'L0_ffn_w1': _L0_ffn_in['w1'], 'L0_ffn_b1': _L0_ffn_in['b1'], 'L0_ffn_w2': _L0_ffn_in['w2'], 'L0_ffn_b2': _L0_ffn_in['b2'], 'L1_attn_W_q': _L1_attn_in['W_q'], 'L1_attn_W_k': _L1_attn_in['W_k'], 'L1_attn_W_v': _L1_attn_in['W_v'], 'L1_attn_W_o': _L1_attn_in['W_o'], 'L1_ffn_gate_w': _L1_ffn_in['gate_w'], 'L1_ffn_w1': _L1_ffn_in['w1'], 'L1_ffn_w2': _L1_ffn_in['w2'], 'L1_ffn_w3': _L1_ffn_in['w3'], 'L2_attn_Win': _L2_attn_in['Win'], 'L2_attn_bin_': _L2_attn_in['bin_'], 'L2_attn_A_log': _L2_attn_in['A_log'], 'L2_attn_B': _L2_attn_in['B'], 'L2_attn_C': _L2_attn_in['C'], 'L2_attn_Dp': _L2_attn_in['Dp'], 'L2_attn_dt': _L2_attn_in['dt'], 'L2_attn_Wout': _L2_attn_in['Wout'], 'L2_attn_bout': _L2_attn_in['bout'], 'L2_ffn_weight': _L2_ffn_in['weight'], 'L2_ffn_ln_gamma': _L2_ffn_in['ln_gamma'], 'L2_ffn_ln_beta': _L2_ffn_in['ln_beta'], 'L3_attn_W_in': _L3_attn_in['W_in'], 'L3_attn_conv_w': _L3_attn_in['conv_w'], 'L3_attn_conv_b': _L3_attn_in['conv_b'], 'L3_attn_dt_bias': _L3_attn_in['dt_bias'], 'L3_attn_A_log': _L3_attn_in['A_log'], 'L3_attn_D': _L3_attn_in['D'], 'L3_attn_norm_w': _L3_attn_in['norm_w'], 'L3_attn_W_out': _L3_attn_in['W_out'], 'L3_ffn_W_r': _L3_ffn_in['W_r'], 'L3_ffn_W_k': _L3_ffn_in['W_k'], 'L3_ffn_W_v': _L3_ffn_in['W_v'], 'L3_ffn_mu_r': _L3_ffn_in['mu_r'], 'L3_ffn_mu_k': _L3_ffn_in['mu_k']}
    _x0 = _d['L0_attn_x']
    _d['L0_attn_x'] = jax.random.normal(jax.random.fold_in(jax.random.key(seed), 1), (8, 256, 128), dtype=_x0.dtype)
    del _x0
    return _d

def reference(L0_attn_x, L0_attn_Wq, L0_attn_bq, L0_attn_Wk, L0_attn_bk, L0_attn_Wv, L0_attn_bv, L0_attn_Wp, L0_attn_bp, L0_ffn_w1, L0_ffn_b1, L0_ffn_w2, L0_ffn_b2, L1_attn_W_q, L1_attn_W_k, L1_attn_W_v, L1_attn_W_o, L1_ffn_gate_w, L1_ffn_w1, L1_ffn_w2, L1_ffn_w3, L2_attn_Win, L2_attn_bin_, L2_attn_A_log, L2_attn_B, L2_attn_C, L2_attn_Dp, L2_attn_dt, L2_attn_Wout, L2_attn_bout, L2_ffn_weight, L2_ffn_ln_gamma, L2_ffn_ln_beta, L3_attn_W_in, L3_attn_conv_w, L3_attn_conv_b, L3_attn_dt_bias, L3_attn_A_log, L3_attn_D, L3_attn_norm_w, L3_attn_W_out, L3_ffn_W_r, L3_ffn_W_k, L3_ffn_W_v, L3_ffn_mu_r, L3_ffn_mu_k):

    def _L0_attn_ref(x, Wq, bq, Wk, bk, Wv, bv, Wp, bp):
        import jax, jax.numpy as jnp
        import numpy as np
        N_HEAD = 16
        B, T, C = x.shape
        H = N_HEAD
        d = C // H

        def proj_heads(W, b):
            h = x @ W.T + b
            return h.reshape(B, T, H, d).transpose(0, 2, 1, 3)
        q = proj_heads(Wq, bq)
        k = proj_heads(Wk, bk)
        v = proj_heads(Wv, bv)
        q = jax.nn.softmax(q, axis=-1)
        k = jax.nn.softmax(k, axis=-1)
        k_sum = k.sum(axis=-2, keepdims=True)
        D_inv = 1.0 / (q * k_sum).sum(axis=-1, keepdims=True)
        context = jnp.einsum('bhnd,bhnv->bhdv', k, v)
        out = jnp.einsum('bhqd,bhdv->bhqv', q, context)
        out = out * D_inv + q
        out = out.transpose(0, 2, 1, 3).reshape(B, T, C)
        return out @ Wp.T + bp

    def _L0_ffn_ref(x, w1, b1, w2, b2):
        import jax, jax.numpy as jnp
        import numpy as np
        N_EMBD = 128
        N_STATE = 512
        h = jax.nn.gelu(jnp.einsum('bse,eh->bsh', x, w1) + b1, approximate=False)
        return jnp.einsum('bsh,he->bse', h, w2) + b2

    def _L1_attn_ref(x, W_q, W_k, W_v, W_o):
        import jax, jax.numpy as jnp
        import numpy as np
        D_MODEL = 128
        N_HEADS = 16
        D_K = 64
        B, S, _ = x.shape
        H, Dk = (N_HEADS, D_K)
        q = (x @ W_q.T).reshape(B, S, H, Dk)
        k = (x @ W_k.T).reshape(B, S, H, Dk)
        v = (x @ W_v.T).reshape(B, S, H, Dk)
        scale = 1.0 / jnp.sqrt(jnp.float32(Dk))
        kv = jnp.einsum('bshd,bshe->bhde', k, v)
        attn = jnp.einsum('bshd,bhde->bshe', q, kv) * scale
        out = attn.reshape(B, S, H * Dk) @ W_o.T
        return out

    def _L1_ffn_ref(hidden_states, gate_w, w1, w2, w3):
        import jax, jax.numpy as jnp
        import numpy as np
        B, S, H, F, E, K = (4, 256, 128, 448, 8, 2)
        CAP_FACTOR = 1.25

        def _moe_forward(hidden_states, gate_w, w1, w2, w3):
            b, s, h = hidden_states.shape
            dtype = hidden_states.dtype
            x = hidden_states.reshape(-1, h)
            router_logits = x @ gate_w.T
            expert_weights = jax.nn.softmax(router_logits.astype(jnp.float32), axis=1)
            _, selected_experts = jax.lax.top_k(expert_weights, K)
            top_k_idx = selected_experts.reshape(b, s, K)
            probs = expert_weights.reshape(b, s, E)
            capacity = int(s * K / E * CAP_FACTOR)
            expert_mask = jax.nn.one_hot(top_k_idx, E, dtype=jnp.int32)
            mask_fused = expert_mask.reshape(b, s * K, E)
            count_fused = jnp.cumsum(mask_fused, axis=1)
            count = count_fused.reshape(b, s, K, E)
            trunc_mask = expert_mask * (count <= capacity).astype(jnp.int32)
            combined_mask = trunc_mask.sum(axis=2)
            masked_probs = probs * combined_mask
            pos_fused = mask_fused * count_fused
            pos = pos_fused.reshape(b, s, K, E)
            combined_pos = pos.sum(axis=2) * combined_mask
            pos_in_cap = jax.nn.one_hot(combined_pos, capacity + 1, dtype=jnp.int32)
            combine_mask = masked_probs[..., None] * pos_in_cap
            combine_mask = combine_mask[..., 1:].astype(dtype)
            dispatch_mask = (combine_mask != 0).astype(dtype)
            dispatch = jnp.einsum('bsm,bsec->ebcm', hidden_states, dispatch_mask)
            h1 = jnp.einsum('ebcm,emh->ebch', dispatch, w1)
            h3 = jnp.einsum('ebcm,emh->ebch', dispatch, w3)
            expert_out = jnp.einsum('ebch,ehm->ebcm', jax.nn.silu(h1) * h3, w2)
            final = jnp.einsum('ebcm,bsec->bsm', expert_out, combine_mask)
            return final
        return _moe_forward(hidden_states, gate_w, w1, w2, w3)

    def _L2_attn_ref(x, Win, bin_, A_log, B, C, Dp, dt, Wout, bout):
        import jax, jax.numpy as jnp
        import numpy as np
        import math
        D_MODEL = 128
        D_STATE = 64
        DT_MIN, DT_MAX = (0.001, 0.1)
        b, L, d = x.shape
        x = x @ Win.T + bin_
        u = jnp.transpose(x, (0, 2, 1))
        A = -jnp.exp(-A_log)
        logdA = A * dt[:, None]
        dB = B * dt[:, None]
        t = jnp.arange(L, dtype=x.dtype)
        powers = jnp.exp(logdA[:, :, None] * t)
        k = jnp.einsum('dn,dnl->dl', C * dB, powers)
        n_fft = 2 * L
        k_f = jnp.fft.rfft(k, n=n_fft)
        u_f = jnp.fft.rfft(u, n=n_fft)
        y = jnp.fft.irfft(u_f * k_f[None], n=n_fft)[..., :L]
        y = y + u * Dp[:, None]
        y = jnp.transpose(y, (0, 2, 1))
        return y @ Wout.T + bout

    def _L2_ffn_ref(x, weight, ln_gamma, ln_beta):
        import jax, jax.numpy as jnp
        import numpy as np
        LN_EPS = 0.001
        EPS = 1e-05
        QB = 128.0

        def ste_round(x):
            return x + jax.lax.stop_gradient(jnp.round(x) - x)
        mu = jnp.mean(x, axis=-1, keepdims=True)
        var = jnp.var(x, axis=-1, keepdims=True)
        xn = (x - mu) * jax.lax.rsqrt(var + LN_EPS) * ln_gamma + ln_beta
        beta = jnp.mean(jnp.abs(weight))
        w_q = jnp.clip(ste_round(weight / (beta + EPS)), -1.0, 1.0)
        gamma = jnp.max(jnp.abs(xn))
        xq = jnp.clip(xn * QB / gamma, -QB + EPS, QB - EPS)
        y = jnp.einsum('bsd,du->bsu', xq, w_q)
        return y * (gamma * beta / QB)

    def _L3_attn_ref(u, W_in, conv_w, conv_b, dt_bias, A_log, D, norm_w, W_out):
        import jax, jax.numpy as jnp
        from jax import lax
        import numpy as np
        D_MODEL = 128
        D_STATE = 64
        D_CONV = 4
        EXPAND = 2
        HEADDIM = 64
        D_INNER = EXPAND * D_MODEL
        NHEADS = D_INNER // HEADDIM
        CHUNK = 64
        CONV_DIM = D_INNER + 2 * D_STATE
        D_IN_PROJ = 2 * D_INNER + 2 * D_STATE + NHEADS
        B_SZ = 4
        SEQLEN = 256
        EPS = 1e-05

        def _silu(x):
            return x * jax.nn.sigmoid(x)

        def _segsum(x):
            T = x.shape[-1]
            xe = jnp.broadcast_to(x[..., None], x.shape + (T,))
            strict_lower = jnp.tril(jnp.ones((T, T), bool), -1)
            xe = jnp.where(strict_lower, xe, 0.0)
            s = jnp.cumsum(xe, axis=-2)
            lower = jnp.tril(jnp.ones((T, T), bool), 0)
            return jnp.where(lower, s, -jnp.inf)
        b, s, _ = u.shape
        A = -jnp.exp(A_log)
        zxbcdt = u @ W_in.T
        z = zxbcdt[..., :D_INNER]
        xBC = zxbcdt[..., D_INNER:D_INNER + CONV_DIM]
        dt = jax.nn.softplus(zxbcdt[..., D_INNER + CONV_DIM:] + dt_bias)
        xc = lax.conv_general_dilated(xBC.transpose(0, 2, 1), conv_w, window_strides=(1,), padding=[(D_CONV - 1, 0)], feature_group_count=CONV_DIM, dimension_numbers=('NCH', 'OIH', 'NCH'))
        xBC = _silu(xc.transpose(0, 2, 1) + conv_b)
        x = xBC[..., :D_INNER].reshape(b, s, NHEADS, HEADDIM)
        Bm = xBC[..., D_INNER:D_INNER + D_STATE]
        Cm = xBC[..., D_INNER + D_STATE:]
        nch = s // CHUNK
        xs = (x * dt[..., None]).reshape(b, nch, CHUNK, NHEADS, HEADDIM)
        Ad = (A * dt).reshape(b, nch, CHUNK, NHEADS)
        Br = Bm.reshape(b, nch, CHUNK, D_STATE)
        Cr = Cm.reshape(b, nch, CHUNK, D_STATE)
        A_ch = Ad.transpose(0, 1, 3, 2)
        A_cum = jnp.cumsum(A_ch, axis=-1)
        L = jnp.exp(_segsum(A_ch))
        Y_diag = jnp.einsum('bcln,bcsn,bchls,bcshp->bclhp', Cr, Br, L, xs)
        decay_states = jnp.exp(A_cum[..., -1:] - A_cum)
        states = jnp.einsum('bchl,bcln,bclhp->bchpn', decay_states, Br, xs)
        init = jnp.zeros((b, 1, NHEADS, HEADDIM, D_STATE), xs.dtype)
        states = jnp.concatenate([init, states], axis=1)
        total_decay = jnp.pad(A_cum[..., -1].transpose(0, 2, 1), ((0, 0), (0, 0), (1, 0)))
        decay_chunk = jnp.exp(_segsum(total_decay))
        new_states = jnp.einsum('bhzc,bchpn->bzhpn', decay_chunk, states)
        states = new_states[:, :-1]
        state_decay_out = jnp.exp(A_cum)
        Y_off = jnp.einsum('bcln,bchpn,bchl->bclhp', Cr, states, state_decay_out)
        y = (Y_diag + Y_off).reshape(b, s, NHEADS, HEADDIM)
        y = y + x * D[:, None]
        y = y.reshape(b, s, D_INNER)
        y = y * _silu(z)
        y = y * lax.rsqrt(jnp.mean(y * y, axis=-1, keepdims=True) + EPS) * norm_w
        return y @ W_out.T

    def _L3_ffn_ref(x, W_r, W_k, W_v, mu_r, mu_k):
        import jax, jax.numpy as jnp
        import numpy as np
        DIM = 128

        def _reference_tuple_inner(x, W_r, W_k, W_v, mu_r, mu_k):
            B, T, C = x.shape
            x_prev = jnp.concatenate([jnp.zeros((B, 1, C), x.dtype), x[:, :-1, :]], axis=1)
            xr = mu_r * x + (1.0 - mu_r) * x_prev
            xk = mu_k * x + (1.0 - mu_k) * x_prev
            r = jax.nn.sigmoid(jnp.einsum('btc,dc->btd', xr, W_r))
            k = jnp.einsum('btc,dc->btd', xk, W_k)
            k_act = jnp.square(jax.nn.relu(k))
            out = r * jnp.einsum('btc,dc->btd', k_act, W_v)
            new_state = x[:, -1, :]
            return (out, new_state)
        return _reference_tuple_inner(x, W_r, W_k, W_v, mu_r, mu_k)[0]
    x = L0_attn_x
    x = _layernorm(x + _L0_attn_ref(x, L0_attn_Wq, L0_attn_bq, L0_attn_Wk, L0_attn_bk, L0_attn_Wv, L0_attn_bv, L0_attn_Wp, L0_attn_bp), axis=-1)
    x = _layernorm(x + _L0_ffn_ref(x, L0_ffn_w1, L0_ffn_b1, L0_ffn_w2, L0_ffn_b2), axis=-1)
    x = _layernorm(x + _L1_attn_ref(x, L1_attn_W_q, L1_attn_W_k, L1_attn_W_v, L1_attn_W_o), axis=-1)
    x = _layernorm(x + _L1_ffn_ref(x, L1_ffn_gate_w, L1_ffn_w1, L1_ffn_w2, L1_ffn_w3), axis=-1)
    x = _layernorm(x + _L2_attn_ref(x, L2_attn_Win, L2_attn_bin_, L2_attn_A_log, L2_attn_B, L2_attn_C, L2_attn_Dp, L2_attn_dt, L2_attn_Wout, L2_attn_bout), axis=-1)
    x = _layernorm(x + _L2_ffn_ref(x, L2_ffn_weight, L2_ffn_ln_gamma, L2_ffn_ln_beta), axis=-1)
    x = _layernorm(x + _L3_attn_ref(x, L3_attn_W_in, L3_attn_conv_w, L3_attn_conv_b, L3_attn_dt_bias, L3_attn_A_log, L3_attn_D, L3_attn_norm_w, L3_attn_W_out), axis=-1)
    x = _layernorm(x + _L3_ffn_ref(x, L3_ffn_W_r, L3_ffn_W_k, L3_ffn_W_v, L3_ffn_mu_r, L3_ffn_mu_k), axis=-1)
    return x

_drawn_inputs = setup_inputs


def setup_inputs(seed=0):
    import zlib

    import numpy as np

    out = dict(_drawn_inputs(seed))
    spreads = {'L2_attn_Dp': (1.0, 0.2),
     'L2_ffn_ln_gamma': (1.0, 0.2),
     'L2_ffn_ln_beta': (0.0, 0.574),
     'L3_attn_conv_b': (0.0, 0.1),
     'L3_attn_D': (1.0, 0.6),
     'L3_attn_norm_w': (1.0, 0.2)}
    factors = {'L0_attn_bk': 8.0,
     'L2_attn_A_log': 7.468,
     'L2_attn_dt': 3.753,
     'L3_attn_dt_bias': 8.0,
     'L3_attn_A_log': 8.0,
     'L3_ffn_W_r': 2.902,
     'L3_ffn_mu_r': 6.173}
    for name, (base, spread) in spreads.items():
        noise = np.random.default_rng([zlib.crc32(name.encode()), seed]).standard_normal(out[name].shape)
        drawn = base * np.exp(spread * noise) if base else spread * noise
        out[name] = jnp.asarray(drawn.astype(out[name].dtype))
    for name, factor in factors.items():
        out[name] = (out[name] * factor).astype(out[name].dtype)
    return out
```

```python
from contextlib import ExitStack

import numpy as np
import concourse.bass as bass
from concourse import mybir

ALU = mybir.AluOpType
ACT = mybir.ActivationFunctionType
AX = mybir.AxisListType
F32 = mybir.dt.float32
BF16 = mybir.dt.bfloat16

P = 128
BATCH = 8
SEQ = 256
NTOK = BATCH * SEQ
NT = NTOK // P
NC = 4
CT = NT // NC
CHUNK = CT * P
BANK = 512

HEADS0, HDIM0 = 16, 8
FFN0 = 512
HEADS1, HDIM1 = 16, 64
EXPERTS, EXP_HID, CAP = 8, 448, 80
FB, NFB = 112, 4
SLOTS = BATCH * CAP
HALF_SLOTS = SLOTS // 2
NSTATE = 64
D_INNER, N_HEADS3, HEAD3 = 256, 4, 64
NEG = -1e30
QCLIP = float(np.float32(128.0 - 1e-5))
LEVELS = 8


def fourier_constants():
    t = np.arange(SEQ, dtype=np.float64)[:, None]
    theta = (np.pi / 2 + 2 * np.pi * np.arange(SEQ, dtype=np.float64)[None, :]) / SEQ
    fwd = np.concatenate([np.cos(theta * t), np.sin(theta * t)], axis=1)
    inv = fwd.T / SEQ
    return fwd.astype(np.float32), np.ascontiguousarray(inv).astype(np.float32)


def build(nc, I, fwd_dram, inv_dram, out, levels=LEVELS):
    with ExitStack() as ctx:
        def sb(name, shape, dt=F32):
            return ctx.enter_context(nc.sbuf_tensor(name, shape, dt))

        def sem(name):
            return ctx.enter_context(nc.semaphore(name))

        ps = ctx.enter_context(nc.psum_tensor("ps", [P, 8, BANK], F32))
        x_tok = sb("x_tok", [P, NT, P])
        xT = sb("xT", [P, NTOK])
        wT = sb("wT", [P, 3084])
        ident = sb("ident", [P, P])
        ones = sb("ones", [P, P])
        tri = sb("tri", [P, P])
        identb = sb("identb", [P, P], BF16)
        negmask = sb("negmask", [P, P], BF16)
        mask144 = sb("mask144", [P, 144])
        bias_tok = sb("bias_tok", [P, 3, P])
        bn = sb("bn", [P, NT, 6])
        mv = sb("mv", [P, NT, 2])
        rstd = sb("rstd", [P, NT])
        mhalf = sb("mhalf", [P, NT])
        b1c = sb("b1c", [P, 4])
        iota_slot = sb("iota_slot", [P, CAP])
        iota_part = sb("iota_part", [P, 1])
        iota_l = sb("iota_l", [P, P])
        tie = sb("tie", [P, EXPERTS])
        sel8 = sb("sel8", [EXPERTS, EXPERTS, CAP], BF16)
        sel4 = sb("sel4", [N_HEADS3, N_HEADS3, P])
        posT = sb("posT", [EXPERTS, NTOK], BF16)
        cols = sb("cols", [P, 40])
        A = sb("arena_a", [P, 20900])
        B = sb("arena_b", [P, 21700])

        def carve(arena, at, *dims):
            n = int(np.prod(dims))
            v = arena[:, at:at + n]
            if len(dims) == 1:
                return v
            names = ["a", "b", "c", "d"][:len(dims)]
            return v.rearrange(f"p ({' '.join(names)}) -> p {' '.join(names)}",
                               **{k: d for k, d in zip(names[1:], dims[1:])})

        WQKV, WP, WO1, GATE, WIN, WOUT, W3IN, W3OUT, WR, WK, WV = (
            0, 384, 512, 1536, 1544, 1672, 1800, 2444, 2700, 2828, 2956)

        s_x = sem("x_loaded")
        s_w0 = sem("weights_l0_loaded")
        s_b0 = sem("biases_l0_loaded")
        s_wf = sem("weights_ffn0_loaded")
        s_w1 = sem("weights_l1_loaded")
        s_wr = sem("weights_rest_loaded")
        s_kw = sem("ssm_parameters_loaded")
        s_four = sem("fourier_loaded")
        s_cols = sem("columns_loaded")
        s_const = sem("constants_ready")
        N_CONST = 14
        N_COLS = 16
        s_pool = sem("pool_chain")
        s_dve = sem("dve_chain")
        s_actc = sem("act_chain")
        s_out = sem("layer_out_ready")
        s_xb = sem("bias_added_to_x")
        s_res = sem("residual_in_x_tok")
        s_mv = sem("mean_var_ready")
        s_rstd = sem("rstd_ready")
        s_xtok = sem("x_tok_normalised")
        s_tp = sem("x_transposed_in_psum")
        s_xT = sem("xT_ready")
        s_wtp = sem("weights_transposed")
        s_wev = sem("weights_T_ready")

        w1s = carve(A, 10112, FFN0)
        w2s = carve(A, 10624, 4, P)
        l0w = carve(A, 9216, 4, P)
        l1w = carve(A, 4096, 3, 8, P)
        l1wo = carve(A, 4096 + 3072, 8 * P)

        gate_nat = carve(A, 11200, P)
        win_nat = carve(A, 11328, P)
        wout_nat = carve(A, 11456, P)
        w3in_nat = carve(A, 11584, 5, P)
        w3dt_nat = carve(A, 12224, P)
        w3out_nat = carve(A, 12352, 2 * P)
        wrkv_nat = carve(A, 12608, 3, P)
        N_WR = 9

        wgroups = [
            ([l0w[:, 0, :], l0w[:, 1, :], l0w[:, 2, :], l0w[:, 3, :]], WQKV, s_w0, 64),
            ([l1wo[:, P * k:P * (k + 1)] for k in range(4)], WO1, s_w1, 64),
            ([l1wo[:, P * k:P * (k + 1)] for k in range(4, 8)], WO1 + 512, s_w1, 64),
            ([gate_nat[0:EXPERTS, :], win_nat, wout_nat], GATE, s_wr, 16 * N_WR),
            ([w3in_nat[:, k, :] for k in range(4)], W3IN, s_wr, 16 * N_WR),
            ([w3in_nat[:, 4, :], w3dt_nat[0:N_HEADS3, :]], W3IN + 512, s_wr, 16 * N_WR),
            ([w3out_nat[:, 0:P], w3out_nat[:, P:2 * P], wrkv_nat[:, 0, :], wrkv_nat[:, 1, :]], W3OUT, s_wr, 16 * N_WR),
            ([wrkv_nat[:, 2, :]], WV, s_wr, 16 * N_WR),
        ]

        x_in = I["L0_attn_x"].rearrange("b (t p) c -> p (b t) c", p=P)
        x_out = out.rearrange("b (t p) c -> p (b t) c", p=P)

        qkv = carve(B, 0, NT, 400)
        gmax = carve(B, 6400, NT, 32)
        gsum = carve(B, 6912, NT, 32)
        grec = carve(B, 7424, NT, 32)
        ctxs = carve(B, 7936, BATCH, 144)
        q0T = carve(B, 9088, NTOK)
        den0 = carve(B, 11136, NT, 16)
        o0 = carve(B, 11392, NT, P)
        o0T = carve(B, 13440, NTOK)
        bqkv = carve(A, 9728, 384)
        s_ones = sem("l0_ones_columns_set")
        s_qkv = sem("l0_qkv_in_psum")
        s_qmax = sem("l0_group_max")
        s_qsub = sem("l0_max_subtracted")
        s_qexp = sem("l0_exp_done")
        s_qrec = sem("l0_softmax_reciprocal")
        s_qk = sem("l0_q_k_normalised")
        s_ctx = sem("l0_context_in_psum")
        s_ctxs = sem("l0_context_masked")
        s_qtp = sem("l0_q_transposed")
        s_q0T = sem("l0_qT_ready")
        s_num = sem("l0_numerator_in_psum")
        s_onum = sem("l0_out_divided")
        s_o0 = sem("l0_out_ready")
        s_otp = sem("l0_out_transposed")
        s_o0T = sem("l0_outT_ready")
        s_qevac = sem("l0_qkv_evacuated")

        h0T = carve(A, 0, 2, 4, CHUNK)
        s_h0 = sem("ffn0_hidden_in_psum")
        s_g0 = sem("ffn0_gelu_done")

        GB = 2
        l1A = carve(B, 10400, HEADS1, P)
        l1B = carve(B, 12448, HEADS1, P)
        gram = carve(B, 0, BATCH, P)
        gbuf = carve(B, 1024, 2, HEADS1, GB * P)
        l1M = carve(B, 9216, BATCH, P)
        s_ab = sem("l1_AB_in_psum")
        s_abs = sem("l1_AB_ready")
        s_g = sem("l1_gram_in_psum")
        s_gs = sem("l1_gram_ready")
        s_gb = sem("l1_gramB_in_psum")
        s_gba = sem("l1_gramB_evacuated_act")
        s_gbv = sem("l1_gramB_evacuated_dve")
        s_m = sem("l1_M_in_psum")
        s_ms = sem("l1_M_ready")

        kA, kB, kC, kE = (carve(A, 13000 + NSTATE * k, NSTATE) for k in range(4))
        kaw = carve(A, 13256, 2, 2, NSTATE)
        dp_row = carve(A, 13512, P)
        ka2 = carve(A, 19400, NSTATE)
        kg2 = carve(A, 19464, NSTATE)
        kWE = carve(A, 19528, NSTATE, 2, 2)
        kexp = carve(A, 11200, NSTATE, P)
        dpr = carve(A, 19784, P)
        four = carve(B, 16384, 2, 2 * SEQ)
        finv = carve(B, 17408, 4, SEQ)
        ktok = carve(B, 18432, 2, P)
        kf = carve(B, 18688, 4, P)
        s_ke = sem("ssm_exp_minus_alog")
        s_ka = sem("ssm_a_W_ready")
        s_katp = sem("ssm_a_W_transposed")
        s_kaw = sem("ssm_a_W_placed")
        s_kg = sem("ssm_step128_ready")
        s_kwe = sem("ssm_weights_ready")
        s_kprod = sem("ssm_products_ready")
        s_kexp = sem("ssm_exp_ready")
        s_kps = sem("ssm_kernel_in_psum")
        s_kt = sem("ssm_kernel_ready")
        s_kfp = sem("ssm_kernel_transformed")
        s_kf = sem("ssm_spectrum_ready")

        RW = 2 * EXP_HID + NFB * P
        ew1 = [carve(A, RW * r, EXP_HID) for r in range(2)]
        ew3 = [carve(A, RW * r + EXP_HID, EXP_HID) for r in range(2)]
        ew2 = [carve(A, RW * r + 2 * EXP_HID, NFB, P) for r in range(2)]
        disp = carve(A, 2816, 2, NT, CAP)
        dispT = carve(A, 5376, 2, NTOK)
        xd = carve(A, 9472, 2, SLOTS)
        eh = carve(A, 10752, 2, NFB, SLOTS)
        esil = carve(A, 15872, 2, HALF_SLOTS)
        eo = carve(A, 16512, 2, BATCH, P)
        (r_pr, r_mask, r_p2, r_oh, r_s, r_pos, r_lg) = (carve(A, 18560 + 128 * k, NT, EXPERTS) for k in range(7))
        (r_mx, r_sum, r_rec, r_t) = (carve(A, 20000 + NT * k, NT) for k in range(4))
        pslot = carve(A, 20100, 2, BATCH)
        s_lg = sem("moe_logits_in_psum")
        s_lsub = sem("moe_max_subtracted")
        s_lexp = sem("moe_exp_ready")
        s_mask = sem("moe_top2_mask_ready")
        s_cnt = sem("moe_counts_in_psum")
        s_pos = sem("moe_positions_ready")
        s_ptp = sem("moe_positions_transposed")
        s_posT = sem("moe_posT_ready")
        s_disp = sem("moe_dispatch_ready")
        s_posb = sem("moe_positions_spread")
        s_dispT = sem("moe_dispatchT_ready")
        s_xdp = sem("moe_tokens_gathered")
        s_xd = sem("moe_xd_ready")
        s_psp = sem("moe_slot_probs_in_psum")
        s_ps = sem("moe_slot_probs_ready")
        s_eh1 = sem("moe_h1_in_psum")
        s_eh3 = sem("moe_h3_in_psum")
        s_sil = sem("moe_silu_ready")
        s_eh = sem("moe_hidden_ready")
        s_eop = sem("moe_expert_out_in_psum")
        s_eo = sem("moe_expert_out_ready")
        s_fin = sem("moe_combined")

        u_tok = carve(B, 0, NT, P)
        yf = carve(B, 2048, 4, BATCH, P)
        prod = carve(B, 6144, 8, 2, 4, P)
        yT = carve(B, 14336, NTOK)
        bin_tok = carve(B, 19200, P)
        s_u = sem("ssm_u_in_psum")
        s_us = sem("ssm_u_ready")
        s_uf = sem("ssm_u_transformed")
        s_prod = sem("ssm_products_of_spectra")
        s_yf = sem("ssm_y_spectrum_ready")
        s_y = sem("ssm_y_in_psum")
        s_yT = sem("ssm_yT_ready")

        xh = carve(A, 0, NT, P)
        xnT = carve(A, 2048, NTOK)
        xqT = carve(A, 4096, NTOK)
        bw = carve(B, 19328, P)
        bwt = carve(B, 19456, P)
        bwq = carve(B, 19584, P)
        mv2 = carve(B, 19712, NT, 2)
        rstd2 = carve(B, 19744, NT)
        s_mv2 = sem("bit_mean_var_ready")
        s_rstd2 = sem("bit_rstd_ready")
        s_xh = sem("bit_x_normalised")
        s_gmx = sem("bit_max_of_partitions")
        s_gt = sem("bit_max_transposed")
        s_gm1 = sem("bit_max_of_all")
        s_gb2 = sem("bit_max_and_sum_spread")
        s_bwq = sem("bit_ternary_weights_ready")
        s_xq = sem("bit_x_quantised")

        xc = carve(B, 0, 3, NTOK)
        cT = carve(B, 6144, NTOK)
        xs = carve(B, 8192, NT, N_HEADS3, HEAD3)
        yg = carve(B, 12288, 2, NTOK)
        ysq = carve(B, 16384, 2, 2, SEQ)
        mring = carve(B, 17408, 4, 384)
        gts = carve(B, 19776, 2, 384)
        (d_v, d_n, d_l, d_dt, d_a, d_acs, d_nacs) = (carve(B, 20560 + 64 * k, NT, N_HEADS3) for k in range(7))
        ssv = carve(B, 21020, NT)
        rms = carve(B, 21040, NT)
        hd = carve(B, 21060, 3, N_HEADS3)
        sz = carve(A, 6144, 2, NTOK)
        acT = carve(A, 10240, NTOK)
        s_hd = sem("ssd_head_constants_loaded")
        s_dtp = sem("ssd_dt_in_psum")
        s_sp1 = sem("ssd_minus_abs_ready")
        s_ea = sem("ssd_exp_alog")
        s_sp2 = sem("ssd_log_ready")
        s_a = sem("ssd_decay_ready")
        s_cum = sem("ssd_cumsum_in_psum")
        s_acs = sem("ssd_cumsum_ready")
        s_actp = sem("ssd_cumsum_transposed")
        s_acT = sem("ssd_acT_ready")
        s_z = sem("ssd_z_in_psum")
        s_sz = sem("ssd_silu_z_ready")
        s_xbc = sem("ssd_xbc_in_psum")
        s_acc = sem("ssd_conv_started")
        s_conv = sem("ssd_conv_done")
        s_xc = sem("ssd_xc_ready")
        s_xsp = sem("ssd_x_transposed")
        s_xs = sem("ssd_xs_ready")
        s_gtp = sem("ssd_scores_in_psum")
        s_gts = sem("ssd_scores_ready")
        s_lp = sem("ssd_decays_in_psum")
        s_le = sem("ssd_decays_ready")
        s_mm = sem("ssd_decayed_scores_ready")
        s_yq = sem("ssd_y_in_psum")
        s_yd = sem("ssd_y_with_D_ready")
        s_yg = sem("ssd_gated_y_ready")
        s_sq = sem("ssd_squares_ready")
        s_ss = sem("ssd_square_sums_in_psum")
        s_ssv = sem("ssd_mean_square_ready")
        s_rms = sem("ssd_rms_ready")
        s_nw = sem("ssd_norm_in_weights")

        xpad = carve(A, 12288, BATCH, SEQ + 1)
        xdif = carve(A, 14400, BATCH, SEQ)
        xr = carve(A, 16448, BATCH, SEQ)
        xk = carve(A, 18496, BATCH, SEQ)
        kact = carve(B, 0, NTOK)
        gate_r = carve(B, 2048, NT, P)
        s_pad = sem("mix_padding_set")
        s_dif = sem("mix_difference_ready")
        s_xr = sem("mix_xr_ready")
        s_xk = sem("mix_xk_ready")
        s_kp = sem("mix_k_in_psum")
        s_kr = sem("mix_relu_ready")
        s_ka2 = sem("mix_k_squared")
        s_rp = sem("mix_r_in_psum")
        s_rs = sem("mix_sigmoid_ready")
        s_ew = [sem(f"moe_weights_loaded_{r}") for r in range(2)]

        block = ctx.enter_context(nc.Block())

        @block.sync
        def _(sp):
            for c in range(NC):
                sp.dma_start(x_tok[:, CT * c:CT * (c + 1), :], x_in[:, CT * c:CT * (c + 1), :]).then_inc(s_x, 16)
                if c == 0:
                    for k, n in enumerate(["Wq", "Wk", "Wv", "Wp"]):
                        sp.dma_start(l0w[:, k, :], I["L0_attn_" + n]).then_inc(s_w0, 16)
                    for k, n in enumerate(["bq", "bk", "bv"]):
                        sp.dma_start(bqkv[:, P * k:P * (k + 1)], I["L0_attn_" + n].partition_broadcast(P)).then_inc(s_b0, 16)
                    sp.dma_start(bias_tok[:, 0, :], I["L0_attn_bp"].partition_broadcast(P)).then_inc(s_b0, 16)
            sp.dma_start(w1s[:], I["L0_ffn_w1"]).then_inc(s_wf, 16)
            sp.dma_start(w2s[:], I["L0_ffn_w2"].rearrange("(j p) e -> p j e", p=P)).then_inc(s_wf, 16)
            sp.dma_start(b1c[:], I["L0_ffn_b1"].rearrange("(j p) -> p j", p=P),
                         allow_slow_non_contiguous=True).then_inc(s_wf, 16)
            sp.dma_start(bias_tok[:, 1, :], I["L0_ffn_b2"].partition_broadcast(P)).then_inc(s_wf, 16)
            for k, n in enumerate(["W_q", "W_k", "W_v"]):
                sp.dma_start(l1w[:, k, :, :], I["L1_attn_" + n].rearrange("(j p) c -> p j c", p=P)).then_inc(s_w1, 16)
            sp.dma_start(l1wo, I["L1_attn_W_o"]).then_inc(s_w1, 16)
            for dst, src in [(gate_nat[0:EXPERTS, :], I["L1_ffn_gate_w"]), (win_nat, I["L2_attn_Win"]),
                             (wout_nat, I["L2_attn_Wout"]),
                             (w3in_nat, I["L3_attn_W_in"][0:640, :].rearrange("(k p) c -> p k c", p=P)),
                             (w3dt_nat[0:N_HEADS3, :], I["L3_attn_W_in"][640:644, :]),
                             (w3out_nat, I["L3_attn_W_out"]), (wrkv_nat[:, 0, :], I["L3_ffn_W_r"]),
                             (wrkv_nat[:, 1, :], I["L3_ffn_W_k"]), (wrkv_nat[:, 2, :], I["L3_ffn_W_v"])]:
                sp.dma_start(dst, src).then_inc(s_wr, 16)
            for dst, src in [(kA, I["L2_attn_A_log"]), (kB, I["L2_attn_B"]), (kC, I["L2_attn_C"]),
                             (cols[:, 0:1], I["L2_attn_dt"].rearrange("(p a) -> p a", a=1)),
                             (dpr[0:1, :], I["L2_attn_Dp"].rearrange("(a c) -> a c", a=1))]:
                sp.dma_start(dst, src).then_inc(s_kw, 16)
            sp.dma_start(bias_tok[:, 2, :], I["L2_attn_bout"].partition_broadcast(P)).then_inc(s_four, 16)
            sp.dma_start(four, fwd_dram.rearrange("(k p) f -> p k f", p=P)).then_inc(s_four, 16)
            sp.dma_start(finv, inv_dram.rearrange("(k p) t -> p k t", p=P)).then_inc(s_four, 16)
            for dst, src in [(bin_tok, I["L2_attn_bin_"].partition_broadcast(P)), (bw, I["L2_ffn_weight"]),
                             (hd[:, 0, :], I["L3_attn_A_log"].partition_broadcast(P)),
                             (hd[:, 1, :], I["L3_attn_dt_bias"].partition_broadcast(P))]:
                sp.dma_start(dst, src).then_inc(s_hd, 16)
            for col, name in [(1, "L2_ffn_ln_gamma"), (2, "L2_ffn_ln_beta"), (22, "L3_ffn_mu_r"), (23, "L3_ffn_mu_k")]:
                sp.dma_start(cols[:, col:col + 1], I[name].rearrange("(p a) -> p a", a=1)).then_inc(s_cols, 16)
            for k in range(3):
                sp.dma_start(cols[:, 3 + k:4 + k], I["L3_attn_conv_b"][P * k:P * (k + 1)].rearrange("(p a) -> p a", a=1)
                             ).then_inc(s_cols, 16)
                sp.dma_start(cols[:, 6 + 4 * k:10 + 4 * k],
                             I["L3_attn_conv_w"][P * k:P * (k + 1)].rearrange("p a j -> p (a j)")).then_inc(s_cols, 16)
            for k in range(2):
                sp.dma_start(cols[:, 20 + k:21 + k], I["L3_attn_norm_w"][P * k:P * (k + 1)].rearrange("(p a) -> p a", a=1)
                             ).then_inc(s_cols, 16)
                for h in range(2):
                    sp.dma_start(cols[HEAD3 * h:HEAD3 * (h + 1), 18 + k:19 + k],
                                 I["L3_attn_D"][2 * k + h:2 * k + h + 1].partition_broadcast(HEAD3)).then_inc(s_cols, 16)
            if levels > 3:
                for e in range(EXPERTS):
                    if e == 0:
                        sp.wait_ge(s_out, 2 * NC)
                        sp.wait_ge(s_ab, 8)
                    if e >= 2:
                        sp.wait_ge(s_eop, 2 * (e - 1))
                    sp.dma_start(ew1[e % 2], I["L1_ffn_w1"][e]).then_inc(s_ew[e % 2], 16)
                    sp.dma_start(ew3[e % 2], I["L1_ffn_w3"][e]).then_inc(s_ew[e % 2], 16)
                    sp.dma_start(ew2[e % 2][0:FB], I["L1_ffn_w2"][e].rearrange("(j p) m -> p j m", p=FB)).then_inc(s_ew[e % 2], 16)
            for c in range(NC):
                sp.wait_ge(s_xtok, NC * (levels - 1) + c + 1)
                sp.dma_start(x_out[:, CT * c:CT * (c + 1), :], x_tok[:, CT * c:CT * (c + 1), :]).then_inc(s_x, 16)
            sp.wait_ge(s_x, 16 * 2 * NC)

        @block.gpsimd
        def _(pool):
            g = nc.gpsimd
            n = [0]

            def link(ins):
                n[0] += 1
                ins.then_inc(s_pool, 1)
                pool.wait_ge(s_pool, n[0])

            link(g.memset(ident[:], 0.0))
            g.affine_select(out=ident[:], in_=ident[:], compare_op=ALU.not_equal, fill=1.0, base=0,
                            pattern=[[-1, P]], channel_multiplier=1).then_inc(s_const, 1)
            g.memset(ones[:], 1.0).then_inc(s_const, 1)
            g.memset(qkv[:, :, 384:400], 1.0).then_inc(s_ones, 1)
            link(g.memset(mask144[:], 1.0))
            m1 = mask144[:, 0:P].rearrange("p (h e) -> p h e", e=HDIM0)
            m2 = mask144[:, P:144]
            link(g.affine_select(out=m1, in_=m1, compare_op=ALU.is_ge, fill=0.0, base=0,
                                 pattern=[[-HDIM0, HEADS0], [0, HDIM0]], channel_multiplier=1))
            link(g.affine_select(out=m1, in_=m1, compare_op=ALU.is_ge, fill=0.0, base=HDIM0 - 1,
                                 pattern=[[HDIM0, HEADS0], [0, HDIM0]], channel_multiplier=-1))
            link(g.affine_select(out=m2, in_=m2, compare_op=ALU.is_ge, fill=0.0, base=0,
                                 pattern=[[-HDIM0, HEADS0]], channel_multiplier=1))
            g.affine_select(out=m2, in_=m2, compare_op=ALU.is_ge, fill=0.0, base=HDIM0 - 1,
                            pattern=[[HDIM0, HEADS0]], channel_multiplier=-1).then_inc(s_const, 1)
            g.memset(mhalf[:], -0.5).then_inc(s_const, 1)
            link(g.memset(tri[:], 1.0))
            g.affine_select(out=tri[:], in_=tri[:], compare_op=ALU.is_ge, fill=0.0, base=0,
                            pattern=[[1, P]], channel_multiplier=-1).then_inc(s_const, 1)

            g.iota(iota_slot[:], pattern=[[1, CAP]], base=1, channel_multiplier=0,
                   allow_small_or_imprecise_dtypes=True).then_inc(s_const, 1)
            g.iota(iota_part[:], pattern=[[1, 1]], base=1, channel_multiplier=1,
                   allow_small_or_imprecise_dtypes=True).then_inc(s_const, 1)
            g.iota(iota_l[:], pattern=[[1, P]], base=0, channel_multiplier=0,
                   allow_small_or_imprecise_dtypes=True).then_inc(s_const, 1)
            g.iota(tie[:], pattern=[[-1, EXPERTS]], base=EXPERTS, channel_multiplier=0,
                   allow_small_or_imprecise_dtypes=True).then_inc(s_const, 1)
            link(g.memset(sel8[:], 1.0))
            g.affine_select(out=sel8[:], in_=sel8[:], compare_op=ALU.is_equal, fill=0.0, base=0,
                            pattern=[[-1, EXPERTS], [0, CAP]], channel_multiplier=1).then_inc(s_const, 1)
            link(g.memset(sel4[:], 1.0))
            g.affine_select(out=sel4[:], in_=sel4[:], compare_op=ALU.is_equal, fill=0.0, base=0,
                            pattern=[[-1, N_HEADS3], [0, P]], channel_multiplier=1).then_inc(s_const, 1)
            link(g.memset(negmask[:], 0.0))
            g.affine_select(out=negmask[:], in_=negmask[:], compare_op=ALU.is_ge, fill=NEG, base=0,
                            pattern=[[1, P]], channel_multiplier=-1).then_inc(s_const, 1)
            link(g.memset(identb[:], 0.0))
            g.affine_select(out=identb[:], in_=identb[:], compare_op=ALU.not_equal, fill=1.0, base=0,
                            pattern=[[-1, P]], channel_multiplier=1).then_inc(s_const, 1)
            g.memset(kWE, 0.0).then_inc(s_const, 1)
            pool.wait_ge(s_const, N_CONST)

            def add_bias(level, c, slot, nth):
                pool.wait_ge(s_tp, NC * level + c + 1)
                xc = x_tok[:, CT * c:CT * (c + 1), :]
                g.tensor_tensor(xc, xc, bias_tok[:, slot, :].unsqueeze(1).broadcast_to([P, CT, P]),
                                ALU.add).then_inc(s_xb, 1)

            def ln_rstd(layer, c, eps=1e-5):
                pool.wait_ge(s_mv, NC * layer + c + 1)
                t = slice(CT * c, CT * (c + 1))
                link(g.tensor_scalar(rstd[:, t], mv[:, t, 1], eps, None, ALU.add))
                g.tensor_tensor(rstd[:, t], rstd[:, t], mhalf[:, t], ALU.pow).then_inc(s_rstd, 1)

            pool.wait_ge(s_b0, 64)
            for s in range(BATCH + 4):
                if s < BATCH:
                    b = s
                    t = slice(2 * b, 2 * b + 2)
                    qk = qkv[:, t, 0:256].rearrange("p t (g e) -> p t g e", e=HDIM0)
                    pool.wait_ge(s_qmax, b + 1)
                    g.tensor_tensor(qk, qk, gmax[:, t, :].unsqueeze(3).broadcast_to([P, 2, 32, HDIM0]),
                                    ALU.subtract).then_inc(s_qsub, 1)
                if 1 <= s <= BATCH:
                    b = s - 1
                    t = slice(2 * b, 2 * b + 2)
                    qk = qkv[:, t, 0:256].rearrange("p t (g e) -> p t g e", e=HDIM0)
                    pool.wait_ge(s_qrec, b + 1)
                    g.tensor_tensor(qk, qk, grec[:, t, :].unsqueeze(3).broadcast_to([P, 2, 32, HDIM0]),
                                    ALU.mult).then_inc(s_qk, 1)
                if s >= 4:
                    b = s - 4
                    t = slice(2 * b, 2 * b + 2)
                    pool.wait_ge(s_onum, b + 1)
                    g.tensor_tensor(o0[:, t, :], o0[:, t, :], qkv[:, t, 0:P], ALU.add).then_inc(s_o0, 1)
            for c in range(NC):
                add_bias(0, c, 0, c)
            for c in range(NC):
                ln_rstd(0, c)
            if levels > 1:
                pool.wait_ge(s_wf, 64)
                for c in range(NC):
                    add_bias(1, c, 1, NC + c)
                pool.wait_ge(s_wtp, len(wgroups))
                pool.wait_ge(s_katp, 1)
                pool.wait_ge(s_kaw, 2)
                for k in range(4):
                    q = slice(16 * k, 16 * k + 16)
                    g.tensor_tensor(kexp[:, q, :], iota_l[:].unsqueeze(1).broadcast_to([P, 16, P]),
                                    ka2[:, q].unsqueeze(2).broadcast_to([P, 16, P]), ALU.mult).then_inc(s_kprod, 1)
                for c in range(NC):
                    ln_rstd(1, c)
            if levels > 2:
                for c in range(NC):
                    ln_rstd(2, c)
            if levels > 3:
                pool.wait_ge(s_pos, 1)
                for e in range(EXPERTS):
                    if e >= 2:
                        pool.wait_ge(s_psp, e - 1)
                    link(g.tensor_tensor(disp[:, e % 2, :, :], iota_slot[:].unsqueeze(1).broadcast_to([P, NT, CAP]),
                                         r_pos[:, :, e].unsqueeze(2).broadcast_to([P, NT, CAP]), ALU.subtract))
                    g.tensor_scalar(disp[:, e % 2, :, :], disp[:, e % 2, :, :], 0.0, None,
                                    ALU.is_equal).then_inc(s_disp, 1)
                for c in range(NC):
                    ln_rstd(3, c)
            if levels > 4:
                pool.wait_ge(s_four, 48)
                for c in range(NC):
                    add_bias(4, c, 2, 2 * NC + c)
                for hb in range(2):
                    bs = slice(4 * hb, 4 * hb + 4)
                    for k, op in enumerate([ALU.subtract, ALU.add]):
                        pool.wait_ge(s_prod, 4 * hb + 2 * k + 2)
                        g.tensor_tensor(yf[:, 2 * k:2 * k + 2, bs, :], prod[:, 4 * hb + 2 * k], prod[:, 4 * hb + 2 * k + 1],
                                        op).then_inc(s_yf, 1)
                for c in range(NC):
                    ln_rstd(4, c)
            if levels > 5:
                for c in range(NC):
                    pool.wait_ge(s_mv2, c + 1)
                    t = slice(CT * c, CT * (c + 1))
                    link(g.tensor_scalar(rstd2[:, t], mv2[:, t, 1], 1e-3, None, ALU.add))
                    g.tensor_tensor(rstd2[:, t], rstd2[:, t], mhalf[:, t], ALU.pow).then_inc(s_rstd2, 1)
                for c in range(NC):
                    ln_rstd(5, c)
            if levels > 6:
                for b in range(BATCH):
                    pool.wait_ge(s_yd, b + 1)
                    t = slice(SEQ * b, SEQ * (b + 1))
                    g.tensor_tensor(yg[:, :, t], yg[:, :, t], sz[:, :, t], ALU.mult).then_inc(s_yg, 1)
                g.memset(xpad[:, :, 0:1], 0.0).then_inc(s_pad, 1)
                pool.wait_ge(s_ssv, 1)
                g.tensor_tensor(rms, ssv, mhalf[:], ALU.pow).then_inc(s_rms, 1)
                for c in range(NC):
                    ln_rstd(6, c)
            if levels > 7:
                for c in range(NC):
                    b = slice(2 * c, 2 * c + 2)
                    pool.wait_ge(s_xT, 7 * NC + c + 1)
                    pool.wait_ge(s_pad, 1)
                    g.tensor_tensor(xdif[:, b, :], xpad[:, b, 1:SEQ + 1], xpad[:, b, 0:SEQ],
                                    ALU.subtract).then_inc(s_dif, 1)
                for c in range(NC):
                    ln_rstd(7, c)

        @block.scalar
        def _(act):
            a = nc.scalar

            def weights_out(k):
                act.wait_ge(s_wtp, k + 1)
                blocks, col, _, _ = wgroups[k]
                w = sum(src.shape[0] for src in blocks)
                a.activation(wT[:, col:col + w], ps[:, 4 + k % 4, 0:w], ACT.Copy).then_inc(s_wev, 1)

            def xT_out(level, c):
                act.wait_ge(s_tp, NC * level + c + 1)
                a.activation(xT[:, CHUNK * c:CHUNK * (c + 1)], ps[:, c, :], ACT.Copy).then_inc(s_xT, 1)

            weights_out(0)
            for c in range(NC):
                xT_out(0, c)
            for s in range(BATCH + 4):
                if s < BATCH:
                    act.wait_ge(s_qsub, s + 1)
                    e = qkv[:, 2 * s:2 * s + 2, 0:256]
                    a.activation(e, e, ACT.Exp).then_inc(s_qexp, 1)
                if 2 <= s < BATCH + 2:
                    b = s - 2
                    act.wait_ge(s_qtp, b + 1)
                    a.activation(q0T[:, 256 * b:256 * (b + 1)], ps[:, 7, 0:256], ACT.Copy).then_inc(s_q0T, 1)
                if s >= 4:
                    b = s - 4
                    act.wait_ge(s_otp, b + 1)
                    a.activation(o0T[:, 256 * b:256 * (b + 1)], ps[:, 2 + b % 2, 0:256], ACT.Copy).then_inc(s_o0T, 1)
            act.wait_ge(s_kw, 16 * 5)
            a.activation(kE, kA, ACT.Exp, scale=-1.0).then_inc(s_ke, 1)
            for k in range(1, len(wgroups)):
                weights_out(k)
            for k in range(4):
                act.wait_ge(s_ab, k + 1)
                a.activation(l1A[:, 4 * k:4 * k + 4, :], ps[:, 4 + k, :].rearrange("p (h c) -> p h c", c=P),
                             ACT.Copy).then_inc(s_abs, 1)
            if levels > 1:
                for c in range(NC):
                    xT_out(1, c)
                    if c >= 2:
                        act.wait_ge(s_out, NC + c - 1)
                    for j in range(4):
                        act.wait_ge(s_h0, 4 * c + j + 1)
                        a.activation(h0T[:, c % 2, j, :], ps[:, 4 + j, :], ACT.Gelu,
                                     bias=b1c[:, j:j + 1]).then_inc(s_g0, 1)
                for k in range(4):
                    act.wait_ge(s_ab, 4 + k + 1)
                    a.activation(l1B[:, 4 * k:4 * k + 4, :], ps[:, 4 + k, :].rearrange("p (h c) -> p h c", c=P),
                                 ACT.Copy).then_inc(s_abs, 1)
                act.wait_ge(s_kaw, 2)
                a.activation(kg2, ka2, ACT.Exp, scale=float(P)).then_inc(s_kg, 1)
                for k in range(4):
                    q = slice(16 * k, 16 * k + 16)
                    act.wait_ge(s_kprod, k + 1)
                    a.activation(kexp[:, q, :], kexp[:, q, :], ACT.Exp).then_inc(s_kexp, 1)
            if levels > 2:
                for c in range(NC):
                    xT_out(2, c)
                for k in range(2):
                    act.wait_ge(s_g, k + 1)
                    a.activation(gram[:, 4 * k:4 * k + 4, :], ps[:, 4 + k, :].rearrange("p (h c) -> p h c", c=P),
                                 ACT.Copy).then_inc(s_gs, 1)
                for g in range(BATCH // GB + 1):
                    if g < BATCH // GB:
                        for b in range(GB):
                            for j in (0, 2):
                                if g >= 2:
                                    act.wait_ge(s_m, g - 1)
                                act.wait_ge(s_gb, (GB * g + b) * 4 + j + 1)
                                a.activation(gbuf[:, g % 2, 4 * j:4 * j + 4, P * b:P * (b + 1)],
                                             ps[:, 4 + j, :].rearrange("p (h c) -> p h c", c=P),
                                             ACT.Copy).then_inc(s_gba, 1)
                    if g >= 1:
                        q = g - 1
                        act.wait_ge(s_m, q + 1)
                        a.activation(l1M[:, GB * q:GB * (q + 1), :],
                                     ps[:, q % 4, 0:GB * P].rearrange("p (b c) -> p b c", c=P),
                                     ACT.Copy, scale=float(HDIM1) ** -0.5).then_inc(s_ms, 1)
            if levels > 3:
                act.wait_ge(s_kfp, 1)
                a.activation(kf, ps[:, 5, :].rearrange("p (m c) -> p m c", c=P), ACT.Copy).then_inc(s_kf, 1)
                for c in range(NC):
                    xT_out(3, c)
                act.wait_ge(s_lsub, 1)
                a.activation(r_pr, r_lg, ACT.Exp).then_inc(s_lexp, 1)
                for k in range(4):
                    act.wait_ge(s_ptp, k + 1)
                    a.activation(posT[:, BANK * k:BANK * (k + 1)], ps[0:EXPERTS, 4 + k, :], ACT.Copy).then_inc(s_posT, 1)

                def gathered(e, hb):
                    act.wait_ge(s_xdp, 2 * e + hb + 1)
                    if e >= 2:
                        act.wait_ge(s_eh3, 8 * (e - 1))
                    a.activation(xd[:, e % 2, HALF_SLOTS * hb:HALF_SLOTS * (hb + 1)], ps[:, 5, 0:HALF_SLOTS],
                                 ACT.Copy).then_inc(s_xd, 1)

                gathered(0, 0)
                gathered(0, 1)
                for e in range(EXPERTS):
                    for u in range(2 * NFB):
                        act.wait_ge(s_eh1, 8 * e + u + 1)
                        if 8 * e + u >= 2:
                            act.wait_ge(s_eh, 8 * e + u - 1)
                        a.activation(esil[0:FB, u % 2, :], ps[0:FB, 6, 0:HALF_SLOTS], ACT.Silu).then_inc(s_sil, 1)
                        if e + 1 < EXPERTS and u in (2, 4):
                            gathered(e + 1, u // 2 - 1)
            if levels > 4:
                for c in range(NC):
                    xT_out(4, c)
                for c in range(NC):
                    act.wait_ge(s_y, c + 1)
                    a.activation(yT[:, CHUNK * c:CHUNK * (c + 1)], ps[:, c, :], ACT.Copy).then_inc(s_yT, 1)
            if levels > 5:
                act.wait_ge(s_cols, 16 * N_COLS)
                for c in range(NC):
                    act.wait_ge(s_tp, NC * 5 + c + 1)
                    a.activation(xnT[:, CHUNK * c:CHUNK * (c + 1)], ps[:, c, :], ACT.Identity,
                                 bias=cols[:, 2:3], scale=cols[:, 1:2]).then_inc(s_xT, 1)
            if levels > 6:
                act.wait_ge(s_hd, 64)
                a.activation(hd[:, 2, :], hd[:, 0, :], ACT.Exp).then_inc(s_ea, 1)
                for c in range(NC):
                    xT_out(6, c)
                act.wait_ge(s_sp1, 1)
                a.activation(d_n, d_n, ACT.Exp).then_inc(s_actc, 1)
                act.wait_ge(s_actc, 1)
                a.activation(d_l, d_n, ACT.Ln, bias=1.0).then_inc(s_sp2, 1)
                for c in range(NC + 1):
                    if c < NC:
                        t = slice(CHUNK * c, CHUNK * (c + 1))
                        for k in range(2):
                            act.wait_ge(s_z, 2 * c + k + 1)
                            a.activation(sz[:, k, t], ps[:, k, :], ACT.Silu).then_inc(s_sz, 1)
                        for k in range(3):
                            act.wait_ge(s_xbc, 3 * c + k + 1)
                            a.activation(xc[:, k, t], ps[:, 2 + k, :], ACT.Identity, bias=cols[:, 3 + k:4 + k],
                                         scale=cols[:, 9 + 4 * k:10 + 4 * k]).then_inc(s_acc, 1)
                    if c >= 1:
                        t = slice(CHUNK * (c - 1), CHUNK * c)
                        for k in range(2):
                            act.wait_ge(s_conv, 3 * (c - 1) + k + 1)
                            a.activation(xc[:, k, t], xc[:, k, t], ACT.Silu).then_inc(s_xc, 1)
                        act.wait_ge(s_conv, 3 * c)
                        a.activation(xc[0:NSTATE, 2, t], xc[0:NSTATE, 2, t], ACT.Silu).then_inc(s_xc, 1)
                        a.activation(cT[0:NSTATE, t], xc[NSTATE:P, 2, t], ACT.Silu).then_inc(s_xc, 1)
                for k in range(4):
                    act.wait_ge(s_actp, k + 1)
                    a.activation(acT[0:N_HEADS3, BANK * k:BANK * (k + 1)], ps[0:N_HEADS3, 4 + k, :],
                                 ACT.Copy).then_inc(s_acT, 1)

                def scores_out(b):
                    act.wait_ge(s_gtp, b + 1)
                    if b >= 2:
                        act.wait_ge(s_mm, 4 * (b - 1))
                    a.activation(gts[:, b % 2, :], ps[:, 6, 0:384], ACT.Copy).then_inc(s_gts, 1)

                def squares(b):
                    act.wait_ge(s_yg, b + 1)
                    if b >= 2:
                        act.wait_ge(s_ss, b - 1)
                    a.activation(ysq[:, b % 2, :, :], yg[:, :, SEQ * b:SEQ * (b + 1)], ACT.Square).then_inc(s_sq, 1)

                act.wait_ge(s_acs, 1)
                for q in range(BATCH * N_HEADS3):
                    b, h = divmod(q, N_HEADS3)
                    if h == 0:
                        scores_out(b)
                    act.wait_ge(s_lp, q + 1)
                    if q >= 4:
                        act.wait_ge(s_yq, q - 3)
                    a.activation(mring[:, q % 4, 0:256], ps[:, 4 + q % 2, 0:256], ACT.Exp,
                                 bias=d_nacs[:, 2 * b, h:h + 1])
                    a.activation(mring[:, q % 4, 256:384], ps[:, 4 + q % 2, 256:384], ACT.Exp,
                                 bias=d_nacs[:, 2 * b + 1, h:h + 1]).then_inc(s_le, 1)
                    if h == 3 and b:
                        squares(b - 1)
                squares(BATCH - 1)
            if levels > 7:
                for c in range(NC):
                    act.wait_ge(s_tp, NC * 7 + c + 1)
                    a.activation(xpad[:, 2 * c:2 * c + 2, 1:SEQ + 1], ps[:, c, :].rearrange("p (b t) -> p b t", b=2),
                                 ACT.Copy).then_inc(s_xT, 1)
                for c in range(NC):
                    act.wait_ge(s_kp, c + 1)
                    a.activation(kact[:, CHUNK * c:CHUNK * (c + 1)], ps[:, 4 + c % 2, :], ACT.Relu).then_inc(s_kr, 1)
                    act.wait_ge(s_rp, c + 1)
                    a.activation(gate_r[:, CT * c:CT * (c + 1), :], ps[:, 6 + c % 2, :].rearrange("p (t c) -> p t c", c=P),
                                 ACT.Sigmoid).then_inc(s_rs, 1)

        @block.vector
        def _(dve):
            v = nc.vector
            n = [0]

            def link(ins):
                n[0] += 1
                ins.then_inc(s_dve, 1)
                dve.wait_ge(s_dve, n[0])

            def ln_stats(layer, c, bias_count=None):
                t = slice(CT * c, CT * (c + 1))
                if bias_count is not None:
                    dve.wait_ge(s_xb, bias_count)
                dve.wait_ge(s_out, NC * layer + c + 1)
                out = ps[:, c, :].rearrange("p (t c) -> p t c", c=P)
                xc_tok = x_tok[:, t, :]
                if layer == 5:
                    link(v.scalar_tensor_tensor(out=xc_tok, in0=out, scalar=cols[:, 38:39], in1=xc_tok,
                                                op0=ALU.mult, op1=ALU.add))
                elif layer == 6:
                    dve.wait_ge(s_rms, 1)
                    for i in range(CT):
                        k = CT * c + i
                        ins = v.scalar_tensor_tensor(out=x_tok[:, k, :], in0=out[:, i, :], scalar=rms[:, k:k + 1],
                                                     in1=x_tok[:, k, :], op0=ALU.mult, op1=ALU.add)
                    link(ins)
                elif layer == 7:
                    dve.wait_ge(s_rs, c + 1)
                    link(v.tensor_tensor(gate_r[:, t, :], out, gate_r[:, t, :], ALU.mult))
                    link(v.tensor_tensor(xc_tok, gate_r[:, t, :], xc_tok, ALU.add))
                else:
                    link(v.tensor_tensor(xc_tok, out, xc_tok, ALU.add))
                for i in range(CT * c, CT * (c + 1)):
                    ins = v.bn_stats(bn[:, i, :], x_tok[:, i, :])
                link(ins)
                for i in range(CT * c, CT * (c + 1)):
                    ins = v.bn_aggr(mv[:, i, :], bn[:, i, :])
                ins.then_inc(s_mv, 1)

            def ln_apply(layer, c):
                dve.wait_ge(s_rstd, NC * layer + c + 1)
                for i in range(CT * c, CT * (c + 1)):
                    ins = v.tensor_scalar(x_tok[:, i, :], x_tok[:, i, :], mv[:, i, 0:1], rstd[:, i:i + 1],
                                          ALU.subtract, ALU.mult)
                ins.then_inc(s_xtok, 1)

            def layer_norm(layer, bias_from=None):
                for c in range(NC + 1):
                    if c < NC:
                        ln_stats(layer, c, None if bias_from is None else bias_from + c + 1)
                    if c >= 1:
                        ln_apply(layer, c - 1)

            def square_k(c):
                t = slice(CHUNK * c, CHUNK * (c + 1))
                dve.wait_ge(s_kr, c + 1)
                v.tensor_tensor(kact[:, t], kact[:, t], kact[:, t], ALU.mult).then_inc(s_ka2, 1)

            dve.wait_ge(s_b0, 64)
            dve.wait_ge(s_const, 3)
            for s in range(BATCH + 4):
                if s < BATCH:
                    b = s
                    t = slice(2 * b, 2 * b + 2)
                    dve.wait_ge(s_qkv, b + 1)
                    ins = v.tensor_tensor(qkv[:, t, 0:384], ps[:, 4:6, 0:384],
                                          bqkv.unsqueeze(1).broadcast_to([P, 2, 384]), ALU.add)
                    ins.then_inc(s_qevac, 1)
                    dve.wait_ge(s_qevac, b + 1)
                    v.tensor_reduce(gmax[:, t, :], qkv[:, t, 0:256].rearrange("p t (g e) -> p t g e", e=HDIM0),
                                    AX.X, ALU.max).then_inc(s_qmax, 1)
                if 1 <= s <= BATCH:
                    b = s - 1
                    t = slice(2 * b, 2 * b + 2)
                    dve.wait_ge(s_qexp, b + 1)
                    link(v.tensor_reduce(gsum[:, t, :], qkv[:, t, 0:256].rearrange("p t (g e) -> p t g e", e=HDIM0),
                                         AX.X, ALU.add))
                    v.reciprocal(grec[:, t, :], gsum[:, t, :]).then_inc(s_qrec, 1)
                if 2 <= s < BATCH + 2:
                    b = s - 2
                    dve.wait_ge(s_ctx, b + 1)
                    v.tensor_tensor(ctxs[:, b, :], ps[:, 6, 0:144], mask144[:], ALU.mult).then_inc(s_ctxs, 1)
                if 3 <= s < BATCH + 3:
                    b = s - 3
                    t = slice(2 * b, 2 * b + 2)
                    dve.wait_ge(s_num, b + 1)
                    nd = ps[:, b % 2, 0:288].rearrange("p (t c) -> p t c", c=144)
                    link(v.reciprocal(den0[:, t, :], nd[:, :, P:144]))
                    v.tensor_tensor(o0[:, t, :].rearrange("p t (h e) -> p t h e", e=HDIM0),
                                    nd[:, :, 0:P].rearrange("p t (h e) -> p t h e", e=HDIM0),
                                    den0[:, t, :].unsqueeze(3).broadcast_to([P, 2, HEADS0, HDIM0]),
                                    ALU.mult).then_inc(s_onum, 1)
            dve.wait_ge(s_kw, 16 * 5)
            dve.wait_ge(s_ke, 1)
            for k in range(2):
                v.tensor_scalar(kaw[:, 0, k, :], kE, cols[:, 0:1], -1.0, ALU.mult, ALU.mult)
                ins = v.scalar_tensor_tensor(out=kaw[:, 1, k, :], in0=kB, scalar=cols[:, 0:1], in1=kC,
                                             op0=ALU.mult, op1=ALU.mult)
            ins.then_inc(s_ka, 1)
            layer_norm(0, 0)
            dve.wait_ge(s_katp, 1)
            dve.wait_ge(s_const, N_CONST)
            for half in range(2):
                r = slice(NSTATE * half, NSTATE * (half + 1))
                v.tensor_copy(ka2[r, :], ps[r, 4, NSTATE * half:NSTATE * (half + 1)])
                v.tensor_copy(kWE[r, :, half, 0], ps[r, 4, P + NSTATE * half:P + NSTATE * (half + 1)]).then_inc(s_kaw, 1)
            if levels > 1:
                layer_norm(1, NC)
                dve.wait_ge(s_kg, 1)
                dve.wait_ge(s_kaw, 2)
                for half in range(2):
                    r = slice(NSTATE * half, NSTATE * (half + 1))
                    v.tensor_tensor(kWE[r, :, half, 1], kWE[r, :, half, 0], kg2[r, :], ALU.mult).then_inc(s_kwe, 1)
            if levels > 2:
                for g in range(BATCH // GB):
                    for b in range(GB):
                        for j in (1, 3):
                            if g >= 2:
                                dve.wait_ge(s_m, g - 1)
                            dve.wait_ge(s_gb, (GB * g + b) * 4 + j + 1)
                            v.tensor_copy(gbuf[:, g % 2, 4 * j:4 * j + 4, P * b:P * (b + 1)],
                                          ps[:, 4 + j, :].rearrange("p (h c) -> p h c", c=P)).then_inc(s_gbv, 1)
                layer_norm(2)
            if levels > 3:
                dve.wait_ge(s_kps, 1)
                link(v.tensor_copy(ktok.rearrange("p i (h q) -> p i h q", h=2),
                                   ps[:, 4, 0:256].rearrange("p (q h i) -> p i h q", h=2, i=2)))
                v.tensor_tensor(ktok[0:1, 0, :], ktok[0:1, 0, :], dpr[0:1, :], ALU.add).then_inc(s_kt, 1)
                wide = lambda x: x.unsqueeze(2).broadcast_to([P, NT, EXPERTS])
                tiew = tie[:].unsqueeze(1).broadcast_to([P, NT, EXPERTS])
                dve.wait_ge(s_lg, 1)
                lg = ps[:, 4, 0:NT * EXPERTS].rearrange("p (t e) -> p t e", e=EXPERTS)
                link(v.tensor_reduce(r_mx, lg, AX.X, ALU.max))
                v.tensor_tensor(r_lg, lg, wide(r_mx), ALU.subtract).then_inc(s_lsub, 1)
                dve.wait_ge(s_lexp, 1)
                link(v.tensor_reduce(r_sum, r_pr, AX.X, ALU.add))
                link(v.reciprocal(r_rec, r_sum))
                link(v.tensor_tensor(r_pr, r_pr, wide(r_rec), ALU.mult))
                link(v.tensor_reduce(r_mx, r_pr, AX.X, ALU.max))
                link(v.tensor_tensor(r_s, r_pr, wide(r_mx), ALU.is_ge))
                link(v.tensor_tensor(r_s, r_s, tiew, ALU.mult))
                link(v.tensor_reduce(r_t, r_s, AX.X, ALU.max))
                link(v.tensor_tensor(r_oh, r_s, wide(r_t), ALU.is_ge))
                link(v.scalar_tensor_tensor(out=r_p2, in0=r_oh, scalar=-2.0, in1=r_pr, op0=ALU.mult, op1=ALU.add))
                link(v.tensor_reduce(r_mx, r_p2, AX.X, ALU.max))
                link(v.tensor_tensor(r_s, r_p2, wide(r_mx), ALU.is_ge))
                link(v.tensor_tensor(r_s, r_s, tiew, ALU.mult))
                link(v.tensor_reduce(r_t, r_s, AX.X, ALU.max))
                link(v.tensor_tensor(r_s, r_s, wide(r_t), ALU.is_ge))
                v.tensor_tensor(r_mask, r_oh, r_s, ALU.add).then_inc(s_mask, 1)
                dve.wait_ge(s_mask, 1)
                dve.wait_ge(s_cnt, 1)
                pair = lambda x: x.rearrange("p (b two) e -> p b two e", two=2)
                v.tensor_tensor(pair(r_pos), ps[:, 5, 0:NT * EXPERTS].rearrange("p (two b e) -> p b two e", two=2, e=EXPERTS),
                                pair(r_mask), ALU.mult).then_inc(s_pos, 1)

                def dispatchT(e, c):
                    dve.wait_ge(s_posb, 4 * e + c + 1)
                    if e >= 2:
                        dve.wait_ge(s_fin, e - 1)
                    v.tensor_scalar(dispT[0:CAP, e % 2, CHUNK * c:CHUNK * (c + 1)], ps[0:CAP, 4, :],
                                    iota_part[0:CAP, :], None, ALU.is_equal).then_inc(s_dispT, 1)

                def slot_probs(e):
                    dve.wait_ge(s_psp, e + 1)
                    v.tensor_copy(pslot[0:CAP, e % 2, :], ps[0:CAP, 4, 0:BATCH]).then_inc(s_ps, 1)

                for c in range(4):
                    dispatchT(0, c)
                slot_probs(0)
                for e in range(EXPERTS):
                    for u in range(2 * NFB):
                        j, hb = divmod(u, 2)
                        dve.wait_ge(s_eh3, 8 * e + u + 1)
                        dve.wait_ge(s_sil, 8 * e + u + 1)
                        if e >= 2:
                            dve.wait_ge(s_eop, 2 * (e - 1))
                        v.tensor_tensor(eh[0:FB, e % 2, j, HALF_SLOTS * hb:HALF_SLOTS * (hb + 1)],
                                        ps[0:FB, 7, 0:HALF_SLOTS], esil[0:FB, u % 2, :], ALU.mult).then_inc(s_eh, 1)
                        if e + 1 < EXPERTS and u % 2 == 1:
                            dispatchT(e + 1, u // 2)
                    if e + 1 < EXPERTS:
                        slot_probs(e + 1)
                    for hb in range(2):
                        dve.wait_ge(s_eop, 2 * e + hb + 1)
                        dve.wait_ge(s_ps, e + 1)
                        v.tensor_tensor(eo[0:CAP, e % 2, 4 * hb:4 * hb + 4, :],
                                        ps[0:CAP, 5, :].rearrange("p (b c) -> p b c", c=P),
                                        pslot[0:CAP, e % 2, 4 * hb:4 * hb + 4].unsqueeze(2).broadcast_to([CAP, 4, P]),
                                        ALU.mult).then_inc(s_eo, 1)
                layer_norm(3)
            if levels > 4:
                dve.wait_ge(s_hd, 64)
                for c in range(NC):
                    dve.wait_ge(s_u, c + 1)
                    v.tensor_tensor(u_tok[:, CT * c:CT * (c + 1), :], ps[:, 4 + c, :].rearrange("p (t c) -> p t c", c=P),
                                    bin_tok.unsqueeze(1).broadcast_to([P, CT, P]), ALU.add).then_inc(s_us, 1)
                dve.wait_ge(s_kf, 1)
                for hb in range(2):
                    dve.wait_ge(s_uf, hb + 1)
                    for k, (um, km) in enumerate([(0, 0), (2, 2), (0, 2), (2, 0)]):
                        v.tensor_tensor(prod[:, 4 * hb + k], ps[:, 4 + um:6 + um, :].rearrange("p m (b c) -> p m b c", c=P),
                                        kf[:, km:km + 2, :].unsqueeze(2).broadcast_to([P, 2, 4, P]),
                                        ALU.mult).then_inc(s_prod, 1)
                layer_norm(4, 2 * NC)
            if levels > 5:
                for c in range(NC + 1):
                    if c < NC:
                        dve.wait_ge(s_xtok, 4 * NC + c + 1)
                        for i in range(CT * c, CT * (c + 1)):
                            ins = v.bn_stats(bn[:, i, :], x_tok[:, i, :])
                        link(ins)
                        for i in range(CT * c, CT * (c + 1)):
                            ins = v.bn_aggr(mv2[:, i, :], bn[:, i, :])
                        ins.then_inc(s_mv2, 1)
                    if c >= 1:
                        dve.wait_ge(s_rstd2, c)
                        dve.wait_ge(s_mv2, c)
                        for i in range(CT * (c - 1), CT * c):
                            ins = v.tensor_scalar(xh[:, i, :], x_tok[:, i, :], mv2[:, i, 0:1], rstd2[:, i:i + 1],
                                                  ALU.subtract, ALU.mult)
                        ins.then_inc(s_xh, 1)
                v.tensor_reduce(cols[:, 24:25], bw, AX.X, ALU.add, apply_absolute_value=True)
                for c in range(NC):
                    dve.wait_ge(s_xT, 5 * NC + c + 1)
                    ins = v.tensor_reduce(cols[:, 25 + c:26 + c], xnT[:, CHUNK * c:CHUNK * (c + 1)], AX.X, ALU.max,
                                          apply_absolute_value=True)
                link(ins)
                v.tensor_reduce(cols[:, 29:30], cols[:, 25:29], AX.X, ALU.max).then_inc(s_gmx, 1)
                dve.wait_ge(s_gt, 1)
                v.tensor_reduce(cols[0:1, 36:37], ps[0:1, 4, 0:P], AX.X, ALU.max).then_inc(s_gm1, 1)
                dve.wait_ge(s_gb2, 1)
                gam, beta, thr, nthr = cols[:, 30:31], cols[:, 34:35], cols[:, 35:36], cols[:, 37:38]
                link(v.tensor_copy(cols[:, 30:32], ps[:, 5, 0:2]))
                v.reciprocal(cols[:, 32:33], gam)
                link(v.tensor_scalar(beta, cols[:, 31:32], 1.0 / (P * P), None, ALU.mult))
                v.tensor_scalar(cols[:, 33:34], cols[:, 32:33], 128.0, None, ALU.mult)
                v.tensor_scalar(cols[:, 38:39], gam, beta, 1.0 / 128.0, ALU.mult, ALU.mult)
                link(v.tensor_scalar(thr, beta, 1e-5, 0.5, ALU.add, ALU.mult))
                link(v.tensor_scalar(nthr, thr, -1.0, None, ALU.mult))
                link(v.tensor_scalar(bwt, bw, nthr, None, ALU.is_lt))
                v.scalar_tensor_tensor(out=bwq, in0=bw, scalar=thr, in1=bwt, op0=ALU.is_gt,
                                       op1=ALU.subtract).then_inc(s_bwq, 1)
                for c in range(NC):
                    t = slice(CHUNK * c, CHUNK * (c + 1))
                    link(v.tensor_scalar(xqT[:, t], xnT[:, t], cols[:, 33:34], QCLIP, ALU.mult, ALU.min))
                    v.tensor_scalar(xqT[:, t], xqT[:, t], -QCLIP, None, ALU.max).then_inc(s_xq, 1)
                layer_norm(5)
            if levels > 6:
                for k in range(2):
                    w = wT[:, W3OUT + P * k:W3OUT + P * (k + 1)]
                    ins = v.tensor_scalar(w, w, cols[:, 20 + k:21 + k], None, ALU.mult)
                ins.then_inc(s_nw, 1)
                head4 = lambda x: x.unsqueeze(1).broadcast_to([P, NT, N_HEADS3])
                dve.wait_ge(s_dtp, 1)
                link(v.tensor_tensor(d_v, ps[:, 7, 0:64].rearrange("p (t h) -> p t h", h=N_HEADS3), head4(hd[:, 1, :]), ALU.add))
                v.scalar_tensor_tensor(out=d_n, in0=d_v, scalar=-1.0, in1=d_v, op0=ALU.mult, op1=ALU.min).then_inc(s_sp1, 1)
                dve.wait_ge(s_ea, 1)
                v.tensor_scalar(hd[:, 2, :], hd[:, 2, :], -1.0, None, ALU.mult)
                dve.wait_ge(s_sp2, 1)
                link(v.scalar_tensor_tensor(out=d_dt, in0=d_v, scalar=0.0, in1=d_l, op0=ALU.max, op1=ALU.add))
                v.tensor_tensor(d_a, d_dt, head4(hd[:, 2, :]), ALU.mult).then_inc(s_a, 1)
                for c in range(NC):
                    for k in range(3):
                        dve.wait_ge(s_acc, 3 * c + k + 1)
                        src = ps[:, 2 + k, :].rearrange("p (b t) -> p b t", b=2)
                        acc = xc[:, k, CHUNK * c:CHUNK * (c + 1)].rearrange("p (b t) -> p b t", b=2)
                        for j in range(1, 4):
                            ins = v.scalar_tensor_tensor(out=acc[:, :, j:SEQ], in0=src[:, :, 0:SEQ - j],
                                                         scalar=cols[:, 9 + 4 * k - j:10 + 4 * k - j],
                                                         in1=acc[:, :, j:SEQ], op0=ALU.mult, op1=ALU.add)
                            if j < 3:
                                link(ins)
                        ins.then_inc(s_conv, 1)
                    if c == 1:
                        dve.wait_ge(s_cum, 1)
                        for out, sign in ((d_acs, 1.0), (d_nacs, -1.0)):
                            ins = v.tensor_scalar(out.rearrange("p (b two) h -> p b two h", two=2),
                                                  ps[:, 6, 0:64].rearrange("p (two b h) -> p b two h", two=2, h=N_HEADS3),
                                                  sign, None, ALU.mult)
                        ins.then_inc(s_acs, 1)

                def xs_out(b):
                    dve.wait_ge(s_xsp, b + 1)
                    t = slice(2 * b, 2 * b + 2)
                    v.tensor_tensor(xs[:, t, :, :], ps[:, 2 + b % 2, :].rearrange("p (t h e) -> p t h e", t=2, h=N_HEADS3),
                                    d_dt[:, t, :].unsqueeze(3).broadcast_to([P, 2, N_HEADS3, HEAD3]),
                                    ALU.mult).then_inc(s_xs, 1)

                def add_d(b):
                    dve.wait_ge(s_yq, 4 * b + 4)
                    for k in range(2):
                        t = slice(SEQ * b, SEQ * (b + 1))
                        ins = v.scalar_tensor_tensor(out=yg[:, k, t], in0=xc[:, k, t], scalar=cols[:, 18 + k:19 + k],
                                                     in1=ps[:, b % 2, SEQ * k:SEQ * (k + 1)], op0=ALU.mult, op1=ALU.add)
                    ins.then_inc(s_yd, 1)

                xs_out(0)
                for q in range(BATCH * N_HEADS3):
                    b, h = divmod(q, N_HEADS3)
                    if h == 2 and b + 1 < BATCH:
                        xs_out(b + 1)
                    dve.wait_ge(s_le, q + 1)
                    dve.wait_ge(s_gts, b + 1)
                    v.tensor_tensor(mring[:, q % 4, :], mring[:, q % 4, :], gts[:, b % 2, :], ALU.mult).then_inc(s_mm, 1)
                    if h == 1 and b:
                        add_d(b - 1)
                add_d(BATCH - 1)
                dve.wait_ge(s_ss, BATCH)
                v.tensor_scalar(ssv, ps[:, 7, 0:NT], 1.0 / D_INNER, 1e-5, ALU.mult, ALU.add).then_inc(s_ssv, 1)
                layer_norm(6)
            if levels > 7:
                for c in range(NC):
                    b = slice(2 * c, 2 * c + 2)
                    dve.wait_ge(s_dif, c + 1)
                    v.scalar_tensor_tensor(out=xk[:, b, :], in0=xdif[:, b, :], scalar=cols[:, 23:24],
                                           in1=xpad[:, b, 0:SEQ], op0=ALU.mult, op1=ALU.add).then_inc(s_xk, 1)
                    v.scalar_tensor_tensor(out=xr[:, b, :], in0=xdif[:, b, :], scalar=cols[:, 22:23],
                                           in1=xpad[:, b, 0:SEQ], op0=ALU.mult, op1=ALU.add).then_inc(s_xr, 1)
                    if c:
                        square_k(c - 1)
                square_k(NC - 1)
                layer_norm(7)

        @block.tensor
        def _(pe):
            te = nc.tensor

            def weights_in(k):
                blocks, _, sm, val = wgroups[k]
                pe.wait_ge(sm, val)
                at = 0
                if k >= 4:
                    pe.wait_ge(s_wev, k - 3)
                for i, src in enumerate(blocks):
                    r = src.shape[0]
                    mm = te.transpose(ps[:, 4 + k % 4, at:at + r], src, ident[0:r, 0:r])
                    at += r
                mm.then_inc(s_wtp, 1)

            def x_transpose(level, c):
                if level == 5:
                    pe.wait_ge(s_xh, c + 1)
                elif level:
                    pe.wait_ge(s_xtok, NC * (level - 1) + c + 1)
                else:
                    pe.wait_ge(s_x, 16 * NC)
                for i in range(CT):
                    src = xh if level == 5 else x_tok
                    mm = te.transpose(ps[:, c, P * i:P * (i + 1)], src[:, CT * c + i, :], ident[:])
                mm.then_inc(s_tp, 1)

            def xTt(t):
                return xT[:, P * t:P * (t + 1)]

            def half_rows(k):
                return slice(HDIM1 * (k // 2), HDIM1 * (k // 2) + HDIM1)

            def square_sums(b):
                pe.wait_ge(s_sq, b + 1)
                for i in range(2):
                    for k in range(2):
                        mm = te.matmul(ps[:, 7, 2 * b + i:2 * b + i + 1], ysq[:, b % 2, k, P * i:P * (i + 1)],
                                       ones[:, 0:1], start=(k == 0), stop=(k == 1))
                mm.then_inc(s_ss, 1)

            pe.wait_ge(s_const, 2)
            weights_in(0)
            for c in range(NC):
                x_transpose(0, c)
            pe.wait_ge(s_ones, 1)
            for s in range(BATCH + 4):
                if s < BATCH:
                    b = s
                    pe.wait_ge(s_xT, b // 2 + 1)
                    if s == 0:
                        pe.wait_ge(s_wev, 1)
                    else:
                        pe.wait_ge(s_qevac, b)
                    for i in range(2):
                        mm = te.matmul(ps[:, 4 + i, 0:384], xTt(2 * b + i), wT[:, WQKV:WQKV + 384],
                                       start=True, stop=True)
                    mm.then_inc(s_qkv, 1)
                if 1 <= s <= BATCH:
                    b = s - 1
                    pe.wait_ge(s_qk, b + 1)
                    if b >= 1:
                        pe.wait_ge(s_ctxs, b)
                    for i in range(2):
                        t = 2 * b + i
                        mm = te.matmul(ps[:, 6, 0:144], qkv[:, t, P:2 * P], qkv[:, t, 256:400],
                                       start=(i == 0), stop=(i == 1))
                    mm.then_inc(s_ctx, 1)
                    if b >= 1:
                        pe.wait_ge(s_q0T, b)
                    for i in range(2):
                        mm = te.transpose(ps[:, 7, P * i:P * (i + 1)], qkv[:, 2 * b + i, 0:P], ident[:])
                    mm.then_inc(s_qtp, 1)
                if 2 <= s < BATCH + 2:
                    b = s - 2
                    pe.wait_ge(s_ctxs, b + 1)
                    pe.wait_ge(s_q0T, b + 1)
                    if b >= 2:
                        pe.wait_ge(s_onum, b - 1)
                    elif b == 0:
                        pe.wait_ge(s_xT, NC)
                    for i in range(2):
                        mm = te.matmul(ps[:, b % 2, 144 * i:144 * (i + 1)], q0T[:, P * (2 * b + i):P * (2 * b + i + 1)],
                                       ctxs[:, b, :], start=True, stop=True)
                    mm.then_inc(s_num, 1)
                if s >= 4:
                    b = s - 4
                    pe.wait_ge(s_o0, b + 1)
                    if b >= 2:
                        pe.wait_ge(s_o0T, b - 1)
                    for i in range(2):
                        mm = te.transpose(ps[:, 2 + b % 2, P * i:P * (i + 1)], o0[:, 2 * b + i, :], ident[:])
                    mm.then_inc(s_otp, 1)
            for c in range(NC):
                pe.wait_ge(s_o0T, BATCH if c >= 2 else 2 * c + 2)
                pe.wait_ge(s_onum, BATCH)
                for i in range(CT):
                    t = CT * c + i
                    mm = te.matmul(ps[:, c, P * i:P * (i + 1)], o0T[:, P * t:P * (t + 1)], wT[:, WP:WP + P],
                                   start=True, stop=True)
                mm.then_inc(s_out, 1)
            pe.wait_ge(s_q0T, BATCH)
            pe.wait_ge(s_ctxs, BATCH)
            pe.wait_ge(s_qevac, BATCH)
            for k in range(1, len(wgroups)):
                weights_in(k)
            for k in range(4):
                pe.wait_ge(s_wev, len(wgroups) - 3 + k)
                r = half_rows(k)
                for i in range(4):
                    pair = 4 * (k % 2) + i
                    mm = te.matmul(ps[:, 4 + k, P * i:P * (i + 1)], l1w[r, 1, pair, :], l1w[r, 0, pair, :],
                                   start=True, stop=True)
                mm.then_inc(s_ab, 1)
            pe.wait_ge(s_abs, 1)
            pe.wait_ge(s_ka, 1)
            te.transpose(ps[:, 4, 0:P], kaw[:, 0, :, :], ident[:])
            te.transpose(ps[:, 4, P:2 * P], kaw[:, 1, :, :], ident[:]).then_inc(s_katp, 1)
            if levels > 1:
                pe.wait_ge(s_wf, 64)

                def hidden0(c):
                    x_transpose(1, c)
                    pe.wait_ge(s_xT, NC + c + 1)
                    for j in range(4):
                        if c:
                            pe.wait_ge(s_g0, 4 * (c - 1) + j + 1)
                        else:
                            pe.wait_ge(s_abs, j + 1)
                            pe.wait_ge(s_kaw, 2)
                        te.matmul(ps[:, 4 + j, :], w1s[:, P * j:P * (j + 1)], xT[:, CHUNK * c:CHUNK * (c + 1)],
                                  start=True, stop=True).then_inc(s_h0, 1)

                def out0(c):
                    pe.wait_ge(s_g0, 4 * c + 4)
                    for i in range(CT):
                        for j in range(4):
                            mm = te.matmul(ps[:, c, P * i:P * (i + 1)], h0T[:, c % 2, j, P * i:P * (i + 1)],
                                           w2s[:, j, :], start=(j == 0), stop=(j == 3))
                    mm.then_inc(s_out, 1)

                for c in range(NC + 1):
                    if c < NC:
                        hidden0(c)
                    if c >= 1:
                        out0(c - 1)
                pe.wait_ge(s_g0, 16)
                for k in range(4):
                    r = half_rows(k)
                    for i in range(4):
                        pair = 4 * (k % 2) + i
                        mm = te.matmul(ps[:, 4 + k, P * i:P * (i + 1)], l1w[r, 2, pair, :],
                                       wT[r, WO1 + P * pair:WO1 + P * (pair + 1)], start=True, stop=True)
                    mm.then_inc(s_ab, 1)
            if levels > 2:
                for c in range(NC):
                    x_transpose(2, c)
                    if c % 2 == 0:
                        pe.wait_ge(s_abs, 8)
                    for b in (2 * c, 2 * c + 1):
                        for i in range(2):
                            mm = te.matmul(ps[:, 4 + b // 4, P * (b % 4):P * (b % 4 + 1)], x_tok[:, 2 * b + i, :],
                                           x_tok[:, 2 * b + i, :], start=(i == 0), stop=(i == 1))
                    if c % 2:
                        mm.then_inc(s_g, 1)
                pe.wait_ge(s_gs, 2)

                def sum_heads(g):
                    pe.wait_ge(s_gba, 2 * GB * (g + 1))
                    pe.wait_ge(s_gbv, 2 * GB * (g + 1))
                    pe.wait_ge(s_xT, 2 * NC + g + 1)
                    for h in range(HEADS1):
                        mm = te.matmul(ps[:, g, 0:GB * P], l1A[:, h, :], gbuf[:, g % 2, h, :],
                                       start=(h == 0), stop=(h == HEADS1 - 1))
                    mm.then_inc(s_m, 1)

                for g in range(BATCH // GB):
                    for b in range(GB * g, GB * (g + 1)):
                        for j in range(4):
                            if b:
                                pe.wait_ge(s_gbv if j % 2 else s_gba, 2 * (b - 1) + j // 2 + 1)
                            te.matmul(ps[:, 4 + j, :], gram[:, b, :],
                                      l1B[:, 4 * j:4 * j + 4, :], start=True, stop=True).then_inc(s_gb, 1)
                    if g:
                        sum_heads(g - 1)
                sum_heads(BATCH // GB - 1)
                for c in range(NC):
                    pe.wait_ge(s_ms, c + 1)
                    for i in range(CT):
                        t = CT * c + i
                        mm = te.matmul(ps[:, c, P * i:P * (i + 1)], xTt(t), l1M[:, t // 2, :], start=True, stop=True)
                    mm.then_inc(s_out, 1)
            if levels > 3:
                pe.wait_ge(s_kwe, 2)
                pe.wait_ge(s_kexp, 4)
                pe.wait_ge(s_gba, BATCH * 2)
                for q in range(NSTATE):
                    mm = te.matmul(ps[:, 4, 4 * q:4 * q + 4], kexp[:, q, :], kWE[:, q, :, :], start=True, stop=True)
                mm.then_inc(s_kps, 1)
                pe.wait_ge(s_kt, 1)
                pe.wait_ge(s_four, 48)
                for m in range(4):
                    for k in range(2):
                        mm = te.matmul(ps[:, 5, P * m:P * (m + 1)], four[:, k, P * m:P * (m + 1)], ktok[:, k, :],
                                       start=(k == 0), stop=(k == 1))
                mm.then_inc(s_kfp, 1)
                for c in range(NC):
                    x_transpose(3, c)
                for t in range(NT):
                    pe.wait_ge(s_xT, 3 * NC + t // CT + 1)
                    mm = te.matmul(ps[:, 4, EXPERTS * t:EXPERTS * (t + 1)], xTt(t), wT[:, GATE:GATE + EXPERTS],
                                   start=True, stop=True)
                mm.then_inc(s_lg, 1)
                pe.wait_ge(s_mask, 1)
                pe.wait_ge(s_kf, 1)
                mpair = r_mask.rearrange("p (b two) e -> p b two e", two=2)
                te.matmul(ps[:, 5, 0:64], tri[:], mpair[:, :, 0, :], start=True, stop=True)
                te.matmul(ps[:, 5, 64:128], tri[:], mpair[:, :, 1, :], start=True, stop=False)
                te.matmul(ps[:, 5, 64:128], ones[:], mpair[:, :, 0, :], start=False, stop=True).then_inc(s_cnt, 1)
                pe.wait_ge(s_pos, 1)
                for t in range(NT):
                    mm = te.transpose(ps[0:EXPERTS, 4 + t // 4, P * (t % 4):P * (t % 4 + 1)], r_pos[:, t, :], ident[:])
                    if t % 4 == 3:
                        mm.then_inc(s_ptp, 1)

                def spread(e, c):
                    pe.wait_ge(s_posT, 4)
                    if e and c == 0:
                        pe.wait_ge(s_ps, e)
                    if c:
                        pe.wait_ge(s_dispT, 4 * e + c)
                    te.matmul(ps[0:CAP, 4, :], sel8[:, e, :], posT[:, CHUNK * c:CHUNK * (c + 1)],
                              start=True, stop=True).then_inc(s_posb, 1)

                def gather(e, hb):
                    pe.wait_ge(s_disp, e + 1)
                    if hb:
                        pe.wait_ge(s_xd, 2 * e + 1)
                    elif e:
                        pe.wait_ge(s_eo, 2 * (e - 1))
                    for i in range(4):
                        for k in range(2):
                            t = 2 * (4 * hb + i) + k
                            mm = te.matmul(ps[:, 5, CAP * i:CAP * (i + 1)], x_tok[:, t, :], disp[:, e % 2, t, :],
                                           start=(k == 0), stop=(k == 1))
                    mm.then_inc(s_xdp, 1)

                def probs(e):
                    pe.wait_ge(s_dispT, 4 * e + 4)
                    for b in range(BATCH):
                        for k in range(2):
                            t = 2 * b + k
                            mm = te.matmul(ps[0:CAP, 4, b:b + 1], disp[:, e % 2, t, :], r_pr[:, t, e:e + 1],
                                           start=(k == 0), stop=(k == 1))
                    mm.then_inc(s_psp, 1)

                def expert_out(e, hb):
                    if hb:
                        pe.wait_ge(s_eo, 2 * e + 1)
                    elif e + 1 < EXPERTS:
                        pe.wait_ge(s_xd, 2 * (e + 1) + 2)
                    pe.wait_ge(s_eh, 8 * e + 8)
                    for i in range(4):
                        b = 4 * hb + i
                        for j in range(NFB):
                            mm = te.matmul(ps[0:CAP, 5, P * i:P * (i + 1)], eh[0:FB, e % 2, j, CAP * b:CAP * (b + 1)],
                                           ew2[e % 2][0:FB, j, :], start=(j == 0), stop=(j == NFB - 1))
                    mm.then_inc(s_eop, 1)

                def combine(e, c):
                    pe.wait_ge(s_eo, 2 * e + c // 2 + 1)
                    pe.wait_ge(s_dispT, 4 * e + c + 1)
                    for i in range(CT):
                        t = CT * c + i
                        mm = te.matmul(ps[:, c, P * i:P * (i + 1)], dispT[0:CAP, e % 2, P * t:P * (t + 1)],
                                       eo[0:CAP, e % 2, t // 2, :], start=(e == 0 and i == 0),
                                       stop=(e == EXPERTS - 1), skip_group_check=True)
                    if e == EXPERTS - 1:
                        mm.then_inc(s_out, 1)
                    elif c == NC - 1:
                        mm.then_inc(s_fin, 1)

                for c in range(4):
                    spread(0, c)
                gather(0, 0)
                gather(0, 1)
                probs(0)
                for e in range(EXPERTS):
                    pe.wait_ge(s_ew[e % 2], 48 * (e // 2 + 1))
                    pe.wait_ge(s_xd, 2 * e + 2)
                    for u in range(2 * NFB):
                        j, hb = divmod(u, 2)
                        n = 8 * e + u
                        rhs = xd[:, e % 2, HALF_SLOTS * hb:HALF_SLOTS * (hb + 1)]
                        if n:
                            pe.wait_ge(s_sil, n)
                        te.matmul(ps[0:FB, 6, 0:HALF_SLOTS], ew1[e % 2][:, FB * j:FB * (j + 1)], rhs,
                                  start=True, stop=True).then_inc(s_eh1, 1)
                        if n:
                            pe.wait_ge(s_eh, n)
                        te.matmul(ps[0:FB, 7, 0:HALF_SLOTS], ew3[e % 2][:, FB * j:FB * (j + 1)], rhs,
                                  start=True, stop=True).then_inc(s_eh3, 1)
                        if e + 1 < EXPERTS:
                            if u % 2 == 0:
                                spread(e + 1, u // 2)
                            if u in (1, 3):
                                gather(e + 1, u // 2)
                    if e + 1 < EXPERTS:
                        probs(e + 1)
                    expert_out(e, 0)
                    expert_out(e, 1)
                    for c in range(NC):
                        combine(e, c)
            if levels > 4:
                for c in range(NC):
                    x_transpose(4, c)
                    pe.wait_ge(s_xT, 4 * NC + c + 1)
                    if c == 0:
                        pe.wait_ge(s_eo, 2 * EXPERTS)
                        pe.wait_ge(s_eh, 8 * EXPERTS)
                    for i in range(CT):
                        mm = te.matmul(ps[:, 4 + c, P * i:P * (i + 1)], xTt(CT * c + i), wT[:, WIN:WIN + P],
                                       start=True, stop=True)
                    mm.then_inc(s_u, 1)
                pe.wait_ge(s_us, NC)
                upair = u_tok.rearrange("p (b two) c -> p b two c", two=2)
                for hb in range(2):
                    if hb:
                        pe.wait_ge(s_prod, 4)
                    for m in range(4):
                        for k in range(2):
                            mm = te.matmul(ps[:, 4 + m, :], four[:, k, P * m:P * (m + 1)],
                                           upair[:, 4 * hb:4 * hb + 4, k, :], start=(k == 0), stop=(k == 1))
                    mm.then_inc(s_uf, 1)
                for c in range(NC):
                    pe.wait_ge(s_yf, 2 * (c // 2) + 2)
                    for i in range(2):
                        for m in range(4):
                            mm = te.matmul(ps[:, c, SEQ * i:SEQ * (i + 1)], yf[:, m, 2 * c + i, :], finv[:, m, :],
                                           start=(m == 0), stop=(m == 3))
                    mm.then_inc(s_y, 1)
                for c in range(NC):
                    pe.wait_ge(s_yT, c + 1)
                    for i in range(CT):
                        t = CT * c + i
                        mm = te.matmul(ps[:, c, P * i:P * (i + 1)], yT[:, P * t:P * (t + 1)], wT[:, WOUT:WOUT + P],
                                       start=True, stop=True)
                    mm.then_inc(s_out, 1)
            if levels > 5:
                for c in range(NC):
                    x_transpose(5, c)
                pe.wait_ge(s_gmx, 1)
                te.transpose(ps[0:1, 4, 0:P], cols[:, 29:30], ident[:]).then_inc(s_gt, 1)
                pe.wait_ge(s_gm1, 1)
                te.matmul(ps[:, 5, 0:1], ones[0:1, :], cols[0:1, 36:37], start=True, stop=True)
                te.matmul(ps[:, 5, 1:2], ones[:], cols[:, 24:25], start=True, stop=True).then_inc(s_gb2, 1)
                pe.wait_ge(s_bwq, 1)
                for c in range(NC):
                    pe.wait_ge(s_xq, c + 1)
                    for i in range(CT):
                        t = CT * c + i
                        mm = te.matmul(ps[:, c, P * i:P * (i + 1)], xqT[:, P * t:P * (t + 1)], bwq, start=True, stop=True)
                    mm.then_inc(s_out, 1)
            if levels > 6:
                for c in range(NC):
                    x_transpose(6, c)
                for t in range(NT):
                    pe.wait_ge(s_xT, 6 * NC + t // CT + 1)
                    mm = te.matmul(ps[:, 7, N_HEADS3 * t:N_HEADS3 * (t + 1)], xTt(t), wT[:, W3IN + 640:W3IN + 644],
                                   start=True, stop=True)
                mm.then_inc(s_dtp, 1)
                for c in range(NC):
                    xcs = xT[:, CHUNK * c:CHUNK * (c + 1)]
                    for k in range(2):
                        if c:
                            pe.wait_ge(s_sz, 2 * (c - 1) + k + 1)
                        te.matmul(ps[:, k, :], wT[:, W3IN + P * k:W3IN + P * (k + 1)], xcs,
                                  start=True, stop=True).then_inc(s_z, 1)
                    for k in range(3):
                        if c:
                            pe.wait_ge(s_conv, 3 * (c - 1) + k + 1)
                        te.matmul(ps[:, 2 + k, :], wT[:, W3IN + P * (2 + k):W3IN + P * (3 + k)], xcs,
                                  start=True, stop=True).then_inc(s_xbc, 1)
                    if c == 1:
                        pe.wait_ge(s_a, 1)
                        apair = d_a.rearrange("p (b two) h -> p b two h", two=2)
                        te.matmul(ps[:, 6, 0:32], tri[:], apair[:, :, 0, :], start=True, stop=True)
                        te.matmul(ps[:, 6, 32:64], tri[:], apair[:, :, 1, :], start=True, stop=False)
                        te.matmul(ps[:, 6, 32:64], ones[:], apair[:, :, 0, :], start=False, stop=True).then_inc(s_cum, 1)
                pe.wait_ge(s_acs, 1)
                pe.wait_ge(s_conv, 12)
                for t in range(NT):
                    mm = te.transpose(ps[0:N_HEADS3, 4 + t // 4, P * (t % 4):P * (t % 4 + 1)], d_acs[:, t, :], ident[:])
                    if t % 4 == 3:
                        mm.then_inc(s_actp, 1)

                def x_tokens(b):
                    pe.wait_ge(s_xc, 4 * (b // 2) + 2)
                    if b >= 2:
                        pe.wait_ge(s_xs, b - 1)
                    for i in range(2):
                        for k in range(2):
                            t = 2 * b + i
                            mm = te.transpose(ps[:, 2 + b % 2, 256 * i + P * k:256 * i + P * (k + 1)],
                                              xc[:, k, P * t:P * (t + 1)], ident[:])
                    mm.then_inc(s_xsp, 1)

                def scores(b):
                    pe.wait_ge(s_xc, 4 * (b // 2) + 4)
                    if b:
                        pe.wait_ge(s_gts, b)
                    else:
                        pe.wait_ge(s_acT, 4)
                    te.matmul(ps[:, 6, 0:256], xc[0:NSTATE, 2, SEQ * b:SEQ * b + P], cT[0:NSTATE, SEQ * b:SEQ * (b + 1)],
                              start=True, stop=True)
                    te.matmul(ps[:, 6, 256:384], xc[0:NSTATE, 2, SEQ * b + P:SEQ * (b + 1)],
                              cT[0:NSTATE, SEQ * b + P:SEQ * (b + 1)], start=True, stop=True).then_inc(s_gtp, 1)

                def decays(q):
                    b, h = divmod(q, N_HEADS3)
                    if h == 0:
                        x_tokens(b)
                        scores(b)
                    if q >= 2:
                        pe.wait_ge(s_le, q - 1)
                    bank = 4 + q % 2
                    te.matmul(ps[:, bank, 0:256], sel4[:, h, :], acT[0:N_HEADS3, SEQ * b:SEQ * (b + 1)],
                              start=True, stop=False, skip_group_check=True)
                    te.matmul(ps[:, bank, 0:P], identb[:], negmask[:], start=False, stop=True, skip_group_check=True)
                    te.matmul(ps[:, bank, 256:384], sel4[:, h, :], acT[0:N_HEADS3, SEQ * b + P:SEQ * (b + 1)],
                              start=False, stop=False, skip_group_check=True)
                    te.matmul(ps[:, bank, 256:384], identb[:], negmask[:], start=False, stop=True,
                              skip_group_check=True).then_inc(s_lp, 1)

                decays(0)
                decays(1)
                for q in range(BATCH * N_HEADS3):
                    b, h = divmod(q, N_HEADS3)
                    if q + 2 < BATCH * N_HEADS3:
                        decays(q + 2)
                    if h == 0:
                        pe.wait_ge(s_xs, b + 1)
                        if b >= 2:
                            pe.wait_ge(s_yd, b - 1)
                    pe.wait_ge(s_mm, q + 1)
                    r = slice(HEAD3 * (h % 2), HEAD3 * (h % 2 + 1))
                    at = SEQ * (h // 2)
                    te.matmul(ps[r, b % 2, at:at + SEQ], xs[:, 2 * b, h, :], mring[:, q % 4, 0:256],
                              start=True, stop=False, skip_group_check=True)
                    te.matmul(ps[r, b % 2, at + P:at + SEQ], xs[:, 2 * b + 1, h, :], mring[:, q % 4, 256:384],
                              start=False, stop=True, skip_group_check=True).then_inc(s_yq, 1)
                    if h == 3 and b:
                        square_sums(b - 1)
                square_sums(BATCH - 1)
                pe.wait_ge(s_nw, 1)
                for c in range(NC):
                    pe.wait_ge(s_yg, BATCH)
                    pe.wait_ge(s_xs, BATCH)
                    for i in range(CT):
                        t = CT * c + i
                        for k in range(2):
                            mm = te.matmul(ps[:, c, P * i:P * (i + 1)], yg[:, k, P * t:P * (t + 1)],
                                           wT[:, W3OUT + P * k:W3OUT + P * (k + 1)], start=(k == 0), stop=(k == 1))
                    mm.then_inc(s_out, 1)
            if levels > 7:
                for c in range(NC):
                    x_transpose(7, c)
                for c in range(NC + 1):
                    if c < NC:
                        b = slice(2 * c, 2 * c + 2)
                        pe.wait_ge(s_xk, c + 1)
                        if c >= 2:
                            pe.wait_ge(s_kr, c - 1)
                        te.matmul(ps[:, 4 + c % 2, :], wT[:, WK:WK + P], xk[:, b, :], start=True, stop=True).then_inc(s_kp, 1)
                        pe.wait_ge(s_xr, c + 1)
                        if c >= 2:
                            pe.wait_ge(s_rs, c - 1)
                        xrf = xr.rearrange("p b t -> p (b t)")
                        for i in range(CT):
                            t = CT * c + i
                            mm = te.matmul(ps[:, 6 + c % 2, P * i:P * (i + 1)], xrf[:, P * t:P * (t + 1)],
                                           wT[:, WR:WR + P], start=True, stop=True)
                        mm.then_inc(s_rp, 1)
                    if c >= 1:
                        pe.wait_ge(s_ka2, c)
                        for i in range(CT):
                            t = CT * (c - 1) + i
                            mm = te.matmul(ps[:, c - 1, P * i:P * (i + 1)], kact[:, P * t:P * (t + 1)],
                                           wT[:, WV:WV + P], start=True, stop=True)
                        mm.then_inc(s_out, 1)


def kernel(**inputs):
    import concourse.bacc as _bacc
    from concourse.bass_utils import run_bass_kernel_spmd as _run

    nc = _bacc.Bacc("TRN2", target_bir_lowering=False, num_devices=1)
    arrays, aps = {}, {}
    for name in inputs:
        a = np.ascontiguousarray(inputs[name])
        arrays["in_" + name] = a
        aps[name] = nc.dram_tensor("in_" + name, a.shape, mybir.dt.from_np(a.dtype), kind="ExternalInput").ap()
    fwd, inv = fourier_constants()
    arrays["fourier_fwd"], arrays["fourier_inv"] = fwd, inv
    fwd_ap = nc.dram_tensor("fourier_fwd", fwd.shape, F32, kind="ExternalInput").ap()
    inv_ap = nc.dram_tensor("fourier_inv", inv.shape, F32, kind="ExternalInput").ap()
    out = nc.dram_tensor("out", (BATCH, SEQ, P), F32, kind="ExternalOutput").ap()
    build(nc, aps, fwd_ap, inv_ap, out)
    r = _run(nc, [arrays], core_ids=[0])
    return r.results[0]["out"]
```

```python
from contextlib import ExitStack

import numpy as np
import concourse.bass as bass
from concourse import mybir

ALU = mybir.AluOpType
ACT = mybir.ActivationFunctionType
AX = mybir.AxisListType
F32 = mybir.dt.float32
BF16 = mybir.dt.bfloat16

P = 128
BATCH = 8
SEQ = 256
NTOK = BATCH * SEQ
NT = NTOK // P
NC = 4
CT = NT // NC
CHUNK = CT * P
BANK = 512

HEADS0, HDIM0 = 16, 8
FFN0 = 512
HEADS1, HDIM1 = 16, 64
EXPERTS, EXP_HID, CAP = 8, 448, 80
FB, NFB = 112, 4
SLOTS = BATCH * CAP
HALF_SLOTS = SLOTS // 2
ST = EXPERTS * CAP // P
NSTATE = 64
D_INNER, N_HEADS3, HEAD3 = 256, 4, 64
QCLIP = float(np.float32(128.0 - 1e-5))
LEVELS = 8


def fourier_constants():
    t = np.arange(SEQ, dtype=np.float64)[:, None]
    theta = (np.pi / 2 + 2 * np.pi * np.arange(SEQ, dtype=np.float64)[None, :]) / SEQ
    fwd = np.concatenate([np.cos(theta * t), np.sin(theta * t)], axis=1)
    inv = fwd.T / SEQ
    return fwd.astype(np.float32), np.ascontiguousarray(inv).astype(np.float32)


def build(nc, I, fwd_dram, inv_dram, out, levels=LEVELS):
    with ExitStack() as ctx:
        def sb(name, shape, dt=F32):
            return ctx.enter_context(nc.sbuf_tensor(name, shape, dt))

        def sem(name):
            return ctx.enter_context(nc.semaphore(name))

        ps = ctx.enter_context(nc.psum_tensor("ps", [P, 8, BANK], F32))
        x_tok = sb("x_tok", [P, NT, P])
        xT = sb("xT", [P, NTOK])
        wT = sb("wT", [P, 3084])
        ident = sb("ident", [P, P])
        ones = sb("ones", [P, P])
        tri = sb("tri", [P, P])
        causal = sb("causal", [P, 3, P])
        below = sb("below", [P, P])
        mask144 = sb("mask144", [P, 144])
        bias_tok = sb("bias_tok", [P, 3, P])
        bn = sb("bn", [P, NT, 6])
        mv = sb("mv", [P, NT, 2])
        rstd = sb("rstd", [P, NT])
        mhalf = sb("mhalf", [P, NT])
        b1c = sb("b1c", [P, 4])
        iota_slot = sb("iota_slot", [P, CAP])
        iota_l = sb("iota_l", [P, P])
        tie = sb("tie", [P, EXPERTS])
        cols = sb("cols", [P, 40])
        A = sb("arena_a", [P, 20900])
        B = sb("arena_b", [P, 21700])

        def carve(arena, at, *dims):
            n = int(np.prod(dims))
            v = arena[:, at:at + n]
            if len(dims) == 1:
                return v
            names = ["a", "b", "c", "d"][:len(dims)]
            return v.rearrange(f"p ({' '.join(names)}) -> p {' '.join(names)}",
                               **{k: d for k, d in zip(names[1:], dims[1:])})

        WQKV, WP, WO1, GATE, WIN, WOUT, W3IN, W3OUT, WR, WK, WV = (
            0, 384, 512, 1536, 1544, 1672, 1800, 2444, 2700, 2828, 2956)

        s_x = sem("x_loaded")
        s_w0 = sem("weights_l0_loaded")
        s_b0 = sem("biases_l0_loaded")
        s_wf = sem("weights_ffn0_loaded")
        s_w1 = sem("weights_l1_loaded")
        s_wr = sem("weights_rest_loaded")
        s_kw = sem("ssm_parameters_loaded")
        s_four = sem("fourier_loaded")
        s_cols = sem("columns_loaded")
        s_const = sem("constants_ready")
        N_CONST = 12
        N_COLS = 12
        s_pool = sem("pool_chain")
        s_dve = sem("dve_chain")
        s_actc = sem("act_chain")
        s_out = sem("layer_out_ready")
        s_xb = sem("bias_added_to_x")
        s_res = sem("residual_in_x_tok")
        s_mv = sem("mean_var_ready")
        s_rstd = sem("rstd_ready")
        s_xtok = sem("x_tok_normalised")
        s_tp = sem("x_transposed_in_psum")
        s_xT = sem("xT_ready")
        s_wtp = sem("weights_transposed")
        s_wev = sem("weights_T_ready")

        w1s = carve(A, 10112, FFN0)
        w2s = carve(A, 10624, 4, P)
        l0w = carve(A, 9216, 4, P)
        l1w = carve(A, 4096, 3, 8, P)
        l1wo = carve(A, 4096 + 3072, 8 * P)

        gate_nat = carve(A, 11200, P)
        win_nat = carve(A, 11328, P)
        wout_nat = carve(A, 11456, P)
        w3in_nat = carve(A, 11584, 5, P)
        w3dt_nat = carve(A, 12224, P)
        w3out_nat = carve(A, 12352, 2 * P)
        wrkv_nat = carve(A, 12608, 3, P)
        N_WR = 9

        wgroups = [
            ([l0w[:, 0, :], l0w[:, 1, :], l0w[:, 2, :], l0w[:, 3, :]], WQKV, s_w0, 64),
            ([l1wo[:, P * k:P * (k + 1)] for k in range(4)], WO1, s_w1, 64),
            ([l1wo[:, P * k:P * (k + 1)] for k in range(4, 8)], WO1 + 512, s_w1, 64),
            ([gate_nat[0:EXPERTS, :], win_nat, wout_nat], GATE, s_wr, 16 * N_WR),
            ([w3in_nat[:, k, :] for k in range(4)], W3IN, s_wr, 16 * N_WR),
            ([w3in_nat[:, 4, :], w3dt_nat[0:N_HEADS3, :]], W3IN + 512, s_wr, 16 * N_WR),
            ([w3out_nat[:, 0:P], w3out_nat[:, P:2 * P], wrkv_nat[:, 0, :], wrkv_nat[:, 1, :]], W3OUT, s_wr, 16 * N_WR),
            ([wrkv_nat[:, 2, :]], WV, s_wr, 16 * N_WR),
        ]

        x_in = I["L0_attn_x"].rearrange("b (t p) c -> p (b t) c", p=P)
        x_out = out.rearrange("b (t p) c -> p (b t) c", p=P)

        qkv = carve(B, 0, NT, 400)
        gmax = carve(B, 6400, NT, 32)
        gsum = carve(B, 6912, NT, 32)
        grec = carve(B, 7424, NT, 32)
        ctxs = carve(B, 7936, BATCH, 144)
        q0T = carve(B, 9088, NTOK)
        den0 = carve(B, 11136, NT, 16)
        o0 = carve(B, 11392, NT, P)
        o0T = carve(B, 13440, NTOK)
        bqkv = carve(A, 9728, 384)
        s_ones = sem("l0_ones_columns_set")
        s_qkv = sem("l0_qkv_in_psum")
        s_qmax = sem("l0_group_max")
        s_qsub = sem("l0_max_subtracted")
        s_qexp = sem("l0_exp_done")
        s_qrec = sem("l0_softmax_reciprocal")
        s_qk = sem("l0_q_k_normalised")
        s_ctx = sem("l0_context_in_psum")
        s_ctxs = sem("l0_context_masked")
        s_qtp = sem("l0_q_transposed")
        s_q0T = sem("l0_qT_ready")
        s_num = sem("l0_numerator_in_psum")
        s_onum = sem("l0_out_divided")
        s_o0 = sem("l0_out_ready")
        s_otp = sem("l0_out_transposed")
        s_o0T = sem("l0_outT_ready")
        s_qevac = sem("l0_qkv_evacuated")

        h0T = carve(A, 0, 2, 4, CHUNK)
        s_h0 = sem("ffn0_hidden_in_psum")
        s_g0 = sem("ffn0_gelu_done")

        GB = 2
        l1A = carve(B, 10400, HEADS1, P)
        l1B = carve(B, 12448, HEADS1, P)
        gram = carve(B, 0, BATCH, P)
        gbuf = carve(B, 1024, 2, HEADS1, GB * P)
        l1M = carve(B, 9216, BATCH, P)
        s_ab = sem("l1_AB_in_psum")
        s_abs = sem("l1_AB_ready")
        s_g = sem("l1_gram_in_psum")
        s_gs = sem("l1_gram_ready")
        s_gb = sem("l1_gramB_in_psum")
        s_gba = sem("l1_gramB_evacuated_act")
        s_gbv = sem("l1_gramB_evacuated_dve")
        s_m = sem("l1_M_in_psum")
        s_ms = sem("l1_M_ready")

        kA, kB, kC, kE = (carve(A, 13000 + NSTATE * k, NSTATE) for k in range(4))
        kaw = carve(A, 13256, 2, 2, NSTATE)
        dp_row = carve(A, 13512, P)
        ka2 = carve(A, 19400, NSTATE)
        kg2 = carve(A, 19464, NSTATE)
        kWE = carve(A, 19528, NSTATE, 2, 2)
        kexp = carve(A, 11200, NSTATE, P)
        dpr = carve(A, 19784, P)
        four = carve(B, 16384, 2, 2 * SEQ)
        finv = carve(B, 17408, 4, SEQ)
        ktok = carve(B, 18432, 2, P)
        kf = carve(B, 18688, 4, P)
        s_ke = sem("ssm_exp_minus_alog")
        s_ka = sem("ssm_a_W_ready")
        s_katp = sem("ssm_a_W_transposed")
        s_kaw = sem("ssm_a_W_placed")
        s_kg = sem("ssm_step128_ready")
        s_kwe = sem("ssm_weights_ready")
        s_kprod = sem("ssm_products_ready")
        s_kexp = sem("ssm_exp_ready")
        s_kps = sem("ssm_kernel_in_psum")
        s_kt = sem("ssm_kernel_ready")
        s_kfp = sem("ssm_kernel_transformed")
        s_kf = sem("ssm_spectrum_ready")

        RW = 2 * EXP_HID + NFB * P
        ew1 = [carve(A, RW * r, EXP_HID) for r in range(2)]
        ew3 = [carve(A, RW * r + EXP_HID, EXP_HID) for r in range(2)]
        ew2 = [carve(A, RW * r + 2 * EXP_HID, NFB, P) for r in range(2)]
        disp = carve(A, 2816, 4, EXPERTS, CAP)
        comb = carve(A, 5376, 4, EXPERTS * CAP)
        eh = carve(A, 7936, 2, NFB, SLOTS)
        eoT = carve(A, 13440, BATCH, EXPERTS, CAP)
        xd = carve(B, 0, EXPERTS, BATCH, CAP)
        combT = carve(B, 5120, NT, ST * P)
        eo = carve(B, 0, BATCH, ST, P)
        esil = carve(B, 15360, 2, HALF_SLOTS)
        (r_pr, r_mask, r_p2, r_oh, r_s, r_pos, r_lg) = (carve(A, 18560 + 128 * k, NT, EXPERTS) for k in range(7))
        (r_mx, r_sum, r_rec, r_t) = (carve(A, 20000 + NT * k, NT) for k in range(4))
        s_lg = sem("moe_logits_in_psum")
        s_lsub = sem("moe_max_subtracted")
        s_lexp = sem("moe_exp_ready")
        s_mask = sem("moe_top2_mask_ready")
        s_cnt = sem("moe_counts_in_psum")
        s_pos = sem("moe_positions_ready")
        s_disp = sem("moe_dispatch_ready")
        s_comb = sem("moe_combine_weights_ready")
        s_ctp = sem("moe_combine_weights_transposed")
        s_cT = sem("moe_combT_ready")
        s_xdp = sem("moe_tokens_gathered")
        s_xda = sem("moe_xd_ready_experts_0_to_3")
        s_xdv = sem("moe_xd_ready_experts_4_to_7")
        s_eh1 = sem("moe_h1_in_psum")
        s_eh3 = sem("moe_h3_in_psum")
        s_sil = sem("moe_silu_ready")
        s_eh = sem("moe_hidden_ready")
        s_eop = sem("moe_expert_out_in_psum")
        s_eoT = sem("moe_expert_outT_ready")
        s_eot = sem("moe_expert_out_transposed")
        s_eo = sem("moe_expert_out_ready")

        u_tok = carve(B, 0, NT, P)
        yf = carve(B, 2048, 4, BATCH, P)
        prod = carve(B, 6144, 8, 2, 4, P)
        yT = carve(B, 14336, NTOK)
        bin_tok = carve(B, 19200, P)
        s_u = sem("ssm_u_in_psum")
        s_us = sem("ssm_u_ready")
        s_uf = sem("ssm_u_transformed")
        s_prod = sem("ssm_products_of_spectra")
        s_yf = sem("ssm_y_spectrum_ready")
        s_y = sem("ssm_y_in_psum")
        s_yT = sem("ssm_yT_ready")

        xh = carve(A, 0, NT, P)
        xnT = carve(A, 2048, NTOK)
        xqT = carve(A, 4096, NTOK)
        bw = carve(B, 19328, P)
        bwt = carve(B, 19456, P)
        bwq = carve(B, 19584, P)
        mv2 = carve(B, 19712, NT, 2)
        rstd2 = carve(B, 19744, NT)
        s_mv2 = sem("bit_mean_var_ready")
        s_rstd2 = sem("bit_rstd_ready")
        s_xh = sem("bit_x_normalised")
        s_gmx = sem("bit_max_of_partitions")
        s_gt = sem("bit_max_transposed")
        s_gm1 = sem("bit_max_of_all")
        s_gb2 = sem("bit_max_and_sum_spread")
        s_bwq = sem("bit_ternary_weights_ready")
        s_xq = sem("bit_x_quantised")

        xc = carve(B, 0, 3, NTOK)
        cT = carve(B, 6144, NTOK)
        xs = carve(B, 8192, NT, N_HEADS3, HEAD3)
        ygT = carve(B, 12288, 2, NTOK)
        ygt = carve(B, 16384, 2, 2, D_INNER)
        mring = carve(B, 17408, 4, 3, P)
        gts = carve(B, 19776, 2, 3, P)
        (d_v, d_n, d_l, d_dt, d_a) = (carve(B, 20560 + 64 * k, NT, N_HEADS3) for k in range(5))
        ssv = carve(B, 21020, NT)
        rms = carve(B, 21040, NT)
        hd = carve(B, 21060, 3, N_HEADS3)
        dsk = carve(B, 21072, N_HEADS3)
        sqj = carve(B, 21080, 2, D_INNER)
        sz = carve(A, 6144, NT, D_INNER)
        xdd = carve(A, 10240, 2, 2, N_HEADS3, HEAD3)
        lmat = carve(A, 14400, 2, 2, N_HEADS3, P)
        s_hd = sem("ssd_head_constants_loaded")
        s_dtp = sem("ssd_dt_in_psum")
        s_sp1 = sem("ssd_minus_abs_ready")
        s_ea = sem("ssd_exp_alog")
        s_sp2 = sem("ssd_log_ready")
        s_a = sem("ssd_decay_ready")
        s_z = sem("ssd_z_in_psum")
        s_sz = sem("ssd_silu_z_ready")
        s_xbc = sem("ssd_xbc_in_psum")
        s_acc = sem("ssd_conv_started")
        s_conv = sem("ssd_conv_done")
        s_xc = sem("ssd_xc_ready")
        s_xsp = sem("ssd_x_transposed")
        s_xs = sem("ssd_xs_ready")
        s_gtp = sem("ssd_scores_in_psum")
        s_gts = sem("ssd_scores_ready")
        s_lp = sem("ssd_decays_in_psum")
        s_le = sem("ssd_decays_ready")
        s_mm = sem("ssd_decayed_scores_ready")
        s_yq = sem("ssd_y_in_psum")
        s_yd = sem("ssd_y_with_D_ready")
        s_yg = sem("ssd_gated_y_ready")
        s_sq = sem("ssd_squares_ready")
        s_ssv = sem("ssd_mean_square_ready")
        s_rms = sem("ssd_rms_ready")
        s_lm = sem("ssd_decay_matrices_ready")
        s_yt = sem("ssd_y_transposed")
        s_ygT = sem("ssd_yT_ready")
        s_nw = sem("ssd_norm_in_weights")

        xpad = carve(A, 12288, BATCH, SEQ + 1)
        xdif = carve(A, 14400, BATCH, SEQ)
        xr = carve(A, 16448, BATCH, SEQ)
        xk = carve(A, 18496, BATCH, SEQ)
        kact = carve(B, 0, NTOK)
        gate_r = carve(B, 2048, NT, P)
        s_pad = sem("mix_padding_set")
        s_dif = sem("mix_difference_ready")
        s_xr = sem("mix_xr_ready")
        s_xk = sem("mix_xk_ready")
        s_kp = sem("mix_k_in_psum")
        s_kr = sem("mix_relu_ready")
        s_ka2 = sem("mix_k_squared")
        s_rp = sem("mix_r_in_psum")
        s_rs = sem("mix_sigmoid_ready")
        s_ew = [sem(f"moe_weights_loaded_{r}") for r in range(2)]

        block = ctx.enter_context(nc.Block())

        @block.sync
        def _(sp):
            for c in range(NC):
                sp.dma_start(x_tok[:, CT * c:CT * (c + 1), :], x_in[:, CT * c:CT * (c + 1), :]).then_inc(s_x, 16)
                if c == 0:
                    for k, n in enumerate(["Wq", "Wk", "Wv", "Wp"]):
                        sp.dma_start(l0w[:, k, :], I["L0_attn_" + n]).then_inc(s_w0, 16)
                    for k, n in enumerate(["bq", "bk", "bv"]):
                        sp.dma_start(bqkv[:, P * k:P * (k + 1)], I["L0_attn_" + n].partition_broadcast(P)).then_inc(s_b0, 16)
                    sp.dma_start(bias_tok[:, 0, :], I["L0_attn_bp"].partition_broadcast(P)).then_inc(s_b0, 16)
            sp.dma_start(w1s[:], I["L0_ffn_w1"]).then_inc(s_wf, 16)
            sp.dma_start(w2s[:], I["L0_ffn_w2"].rearrange("(j p) e -> p j e", p=P)).then_inc(s_wf, 16)
            sp.dma_start(b1c[:], I["L0_ffn_b1"].rearrange("(j p) -> p j", p=P),
                         allow_slow_non_contiguous=True).then_inc(s_wf, 16)
            sp.dma_start(bias_tok[:, 1, :], I["L0_ffn_b2"].partition_broadcast(P)).then_inc(s_wf, 16)
            for k, n in enumerate(["W_q", "W_k", "W_v"]):
                sp.dma_start(l1w[:, k, :, :], I["L1_attn_" + n].rearrange("(j p) c -> p j c", p=P)).then_inc(s_w1, 16)
            sp.dma_start(l1wo, I["L1_attn_W_o"]).then_inc(s_w1, 16)
            for dst, src in [(gate_nat[0:EXPERTS, :], I["L1_ffn_gate_w"]), (win_nat, I["L2_attn_Win"]),
                             (wout_nat, I["L2_attn_Wout"]),
                             (w3in_nat, I["L3_attn_W_in"][0:640, :].rearrange("(k p) c -> p k c", p=P)),
                             (w3dt_nat[0:N_HEADS3, :], I["L3_attn_W_in"][640:644, :]),
                             (w3out_nat, I["L3_attn_W_out"]), (wrkv_nat[:, 0, :], I["L3_ffn_W_r"]),
                             (wrkv_nat[:, 1, :], I["L3_ffn_W_k"]), (wrkv_nat[:, 2, :], I["L3_ffn_W_v"])]:
                sp.dma_start(dst, src).then_inc(s_wr, 16)
            for dst, src in [(kA, I["L2_attn_A_log"]), (kB, I["L2_attn_B"]), (kC, I["L2_attn_C"]),
                             (cols[:, 0:1], I["L2_attn_dt"].rearrange("(p a) -> p a", a=1)),
                             (dpr[0:1, :], I["L2_attn_Dp"].rearrange("(a c) -> a c", a=1))]:
                sp.dma_start(dst, src).then_inc(s_kw, 16)
            sp.dma_start(bias_tok[:, 2, :], I["L2_attn_bout"].partition_broadcast(P)).then_inc(s_four, 16)
            sp.dma_start(four, fwd_dram.rearrange("(k p) f -> p k f", p=P)).then_inc(s_four, 16)
            sp.dma_start(finv, inv_dram.rearrange("(k p) t -> p k t", p=P)).then_inc(s_four, 16)
            for dst, src in [(bin_tok, I["L2_attn_bin_"].partition_broadcast(P)), (bw, I["L2_ffn_weight"]),
                             (hd[:, 0, :], I["L3_attn_A_log"].partition_broadcast(P)),
                             (hd[:, 1, :], I["L3_attn_dt_bias"].partition_broadcast(P)),
                             (dsk, I["L3_attn_D"].partition_broadcast(P))]:
                sp.dma_start(dst, src).then_inc(s_hd, 16)
            for col, name in [(1, "L2_ffn_ln_gamma"), (2, "L2_ffn_ln_beta"), (22, "L3_ffn_mu_r"), (23, "L3_ffn_mu_k")]:
                sp.dma_start(cols[:, col:col + 1], I[name].rearrange("(p a) -> p a", a=1)).then_inc(s_cols, 16)
            for k in range(3):
                sp.dma_start(cols[:, 3 + k:4 + k], I["L3_attn_conv_b"][P * k:P * (k + 1)].rearrange("(p a) -> p a", a=1)
                             ).then_inc(s_cols, 16)
                sp.dma_start(cols[:, 6 + 4 * k:10 + 4 * k],
                             I["L3_attn_conv_w"][P * k:P * (k + 1)].rearrange("p a j -> p (a j)")).then_inc(s_cols, 16)
            for k in range(2):
                sp.dma_start(cols[:, 20 + k:21 + k], I["L3_attn_norm_w"][P * k:P * (k + 1)].rearrange("(p a) -> p a", a=1)
                             ).then_inc(s_cols, 16)
            if levels > 3:
                for e in range(EXPERTS):
                    if e == 0:
                        sp.wait_ge(s_out, 2 * NC)
                        sp.wait_ge(s_ab, 8)
                    if e >= 2:
                        sp.wait_ge(s_eop, 2 * (e - 1))
                    sp.dma_start(ew1[e % 2], I["L1_ffn_w1"][e]).then_inc(s_ew[e % 2], 16)
                    sp.dma_start(ew3[e % 2], I["L1_ffn_w3"][e]).then_inc(s_ew[e % 2], 16)
                    sp.dma_start(ew2[e % 2][0:FB], I["L1_ffn_w2"][e].rearrange("(j p) m -> p j m", p=FB)).then_inc(s_ew[e % 2], 16)
            for c in range(NC):
                sp.wait_ge(s_xtok, NC * (levels - 1) + c + 1)
                sp.dma_start(x_out[:, CT * c:CT * (c + 1), :], x_tok[:, CT * c:CT * (c + 1), :]).then_inc(s_x, 16)
            sp.wait_ge(s_x, 16 * 2 * NC)

        @block.gpsimd
        def _(pool):
            g = nc.gpsimd
            n = [0]

            def link(ins):
                n[0] += 1
                ins.then_inc(s_pool, 1)
                pool.wait_ge(s_pool, n[0])

            link(g.memset(ident[:], 0.0))
            g.affine_select(out=ident[:], in_=ident[:], compare_op=ALU.not_equal, fill=1.0, base=0,
                            pattern=[[-1, P]], channel_multiplier=1).then_inc(s_const, 1)
            g.memset(ones[:], 1.0).then_inc(s_const, 1)
            g.memset(qkv[:, :, 384:400], 1.0).then_inc(s_ones, 1)
            link(g.memset(mask144[:], 1.0))
            m1 = mask144[:, 0:P].rearrange("p (h e) -> p h e", e=HDIM0)
            m2 = mask144[:, P:144]
            link(g.affine_select(out=m1, in_=m1, compare_op=ALU.is_ge, fill=0.0, base=0,
                                 pattern=[[-HDIM0, HEADS0], [0, HDIM0]], channel_multiplier=1))
            link(g.affine_select(out=m1, in_=m1, compare_op=ALU.is_ge, fill=0.0, base=HDIM0 - 1,
                                 pattern=[[HDIM0, HEADS0], [0, HDIM0]], channel_multiplier=-1))
            link(g.affine_select(out=m2, in_=m2, compare_op=ALU.is_ge, fill=0.0, base=0,
                                 pattern=[[-HDIM0, HEADS0]], channel_multiplier=1))
            g.affine_select(out=m2, in_=m2, compare_op=ALU.is_ge, fill=0.0, base=HDIM0 - 1,
                            pattern=[[HDIM0, HEADS0]], channel_multiplier=-1).then_inc(s_const, 1)
            g.memset(mhalf[:], -0.5).then_inc(s_const, 1)
            link(g.memset(tri[:], 1.0))
            g.affine_select(out=tri[:], in_=tri[:], compare_op=ALU.is_ge, fill=0.0, base=0,
                            pattern=[[1, P]], channel_multiplier=-1).then_inc(s_const, 1)

            g.iota(iota_slot[:], pattern=[[1, CAP]], base=1, channel_multiplier=0,
                   allow_small_or_imprecise_dtypes=True).then_inc(s_const, 1)
            g.iota(iota_l[:], pattern=[[1, P]], base=0, channel_multiplier=0,
                   allow_small_or_imprecise_dtypes=True).then_inc(s_const, 1)
            g.iota(tie[:], pattern=[[-1, EXPERTS]], base=EXPERTS, channel_multiplier=0,
                   allow_small_or_imprecise_dtypes=True).then_inc(s_const, 1)
            link(g.memset(below[:], 1.0))
            g.affine_select(out=below[:], in_=below[:], compare_op=ALU.is_gt, fill=0.0, base=0,
                            pattern=[[-1, P]], channel_multiplier=1).then_inc(s_const, 1)
            link(g.memset(causal[:], 1.0))
            for k in (0, 2):
                g.affine_select(out=causal[:, k, :], in_=causal[:, k, :], compare_op=ALU.is_ge, fill=0.0, base=0,
                                pattern=[[1, P]], channel_multiplier=-1).then_inc(s_const, 1)
            g.memset(kWE, 0.0).then_inc(s_const, 1)
            pool.wait_ge(s_const, N_CONST)

            def add_bias(level, c, slot, nth):
                pool.wait_ge(s_tp, NC * level + c + 1)
                xc = x_tok[:, CT * c:CT * (c + 1), :]
                g.tensor_tensor(xc, xc, bias_tok[:, slot, :].unsqueeze(1).broadcast_to([P, CT, P]),
                                ALU.add).then_inc(s_xb, 1)

            def ln_rstd(layer, c, eps=1e-5):
                pool.wait_ge(s_mv, NC * layer + c + 1)
                t = slice(CT * c, CT * (c + 1))
                link(g.tensor_scalar(rstd[:, t], mv[:, t, 1], eps, None, ALU.add))
                g.tensor_tensor(rstd[:, t], rstd[:, t], mhalf[:, t], ALU.pow).then_inc(s_rstd, 1)

            def mean_square_pow(c):
                t = slice(CT * c, CT * (c + 1))
                pool.wait_ge(s_ssv, c + 1)
                g.tensor_tensor(rms[:, t], ssv[:, t], mhalf[:, t], ALU.pow).then_inc(s_rms, 1)

            pool.wait_ge(s_b0, 64)
            for s in range(BATCH + 4):
                if s < BATCH:
                    b = s
                    t = slice(2 * b, 2 * b + 2)
                    qk = qkv[:, t, 0:256].rearrange("p t (g e) -> p t g e", e=HDIM0)
                    pool.wait_ge(s_qmax, b + 1)
                    g.tensor_tensor(qk, qk, gmax[:, t, :].unsqueeze(3).broadcast_to([P, 2, 32, HDIM0]),
                                    ALU.subtract).then_inc(s_qsub, 1)
                if 1 <= s <= BATCH:
                    b = s - 1
                    t = slice(2 * b, 2 * b + 2)
                    qk = qkv[:, t, 0:256].rearrange("p t (g e) -> p t g e", e=HDIM0)
                    pool.wait_ge(s_qrec, b + 1)
                    g.tensor_tensor(qk, qk, grec[:, t, :].unsqueeze(3).broadcast_to([P, 2, 32, HDIM0]),
                                    ALU.mult).then_inc(s_qk, 1)
                if s >= 4:
                    b = s - 4
                    t = slice(2 * b, 2 * b + 2)
                    pool.wait_ge(s_onum, b + 1)
                    g.tensor_tensor(o0[:, t, :], o0[:, t, :], qkv[:, t, 0:P], ALU.add).then_inc(s_o0, 1)
            for c in range(NC):
                add_bias(0, c, 0, c)
            for c in range(NC):
                ln_rstd(0, c)
            if levels > 1:
                pool.wait_ge(s_wf, 64)
                for c in range(NC):
                    add_bias(1, c, 1, NC + c)
                pool.wait_ge(s_wtp, len(wgroups))
                pool.wait_ge(s_katp, 1)
                pool.wait_ge(s_kaw, 2)
                for k in range(4):
                    q = slice(16 * k, 16 * k + 16)
                    g.tensor_tensor(kexp[:, q, :], iota_l[:].unsqueeze(1).broadcast_to([P, 16, P]),
                                    ka2[:, q].unsqueeze(2).broadcast_to([P, 16, P]), ALU.mult).then_inc(s_kprod, 1)
                for c in range(NC):
                    ln_rstd(1, c)
            if levels > 2:
                for c in range(NC):
                    ln_rstd(2, c)
            if levels > 3:
                for t in range(NT):
                    pool.wait_ge(s_disp, t + 1)
                    if t >= 4:
                        pool.wait_ge(s_ctp, t - 3)
                    g.tensor_tensor(comb[:, t % 4].rearrange("p (e s) -> p e s", s=CAP), disp[:, t % 4],
                                    r_pr[:, t, :].unsqueeze(2).broadcast_to([P, EXPERTS, CAP]),
                                    ALU.mult).then_inc(s_comb, 1)
                for c in range(NC):
                    ln_rstd(3, c)
            if levels > 4:
                pool.wait_ge(s_four, 48)
                for c in range(NC):
                    add_bias(4, c, 2, 2 * NC + c)
                for hb in range(2):
                    bs = slice(4 * hb, 4 * hb + 4)
                    for k, op in enumerate([ALU.subtract, ALU.add]):
                        pool.wait_ge(s_prod, 4 * hb + 2 * k + 2)
                        g.tensor_tensor(yf[:, 2 * k:2 * k + 2, bs, :], prod[:, 4 * hb + 2 * k], prod[:, 4 * hb + 2 * k + 1],
                                        op).then_inc(s_yf, 1)
                for c in range(NC):
                    ln_rstd(4, c)
            if levels > 5:
                for c in range(NC):
                    pool.wait_ge(s_mv2, c + 1)
                    t = slice(CT * c, CT * (c + 1))
                    link(g.tensor_scalar(rstd2[:, t], mv2[:, t, 1], 1e-3, None, ALU.add))
                    g.tensor_tensor(rstd2[:, t], rstd2[:, t], mhalf[:, t], ALU.pow).then_inc(s_rstd2, 1)
                for c in range(NC):
                    ln_rstd(5, c)
            if levels > 6:
                def decay_matrices(b):
                    if b >= 2:
                        pool.wait_ge(s_lp, 4 * (b - 1))
                    g.tensor_tensor(lmat[:, b % 2], below[:].unsqueeze(1).unsqueeze(1).broadcast_to([P, 2, N_HEADS3, P]),
                                    d_a[:, 2 * b:2 * b + 2, :].unsqueeze(3).broadcast_to([P, 2, N_HEADS3, P]),
                                    ALU.mult).then_inc(s_lm, 1)

                pool.wait_ge(s_a, 1)
                decay_matrices(0)
                decay_matrices(1)
                g.memset(xpad[:, :, 0:1], 0.0).then_inc(s_pad, 1)
                for b in range(BATCH):
                    pool.wait_ge(s_yd, b + 1)
                    pool.wait_ge(s_sz, 2 * NC)
                    g.tensor_tensor(ygt[:, b % 2], ygt[:, b % 2], sz[:, 2 * b:2 * b + 2, :], ALU.mult).then_inc(s_yg, 1)
                    if b + 2 < BATCH:
                        decay_matrices(b + 2)
                    if b in (2, 4, 6):
                        mean_square_pow(b // 2 - 1)
                    if b in (3, 5):
                        ln_rstd(6, (b - 3) // 2)
                ln_rstd(6, 2)
                mean_square_pow(3)
                ln_rstd(6, 3)
            if levels > 7:
                for c in range(NC):
                    b = slice(2 * c, 2 * c + 2)
                    pool.wait_ge(s_xT, 7 * NC + c + 1)
                    pool.wait_ge(s_pad, 1)
                    g.tensor_tensor(xdif[:, b, :], xpad[:, b, 1:SEQ + 1], xpad[:, b, 0:SEQ],
                                    ALU.subtract).then_inc(s_dif, 1)
                for c in range(NC):
                    ln_rstd(7, c)

        @block.scalar
        def _(act):
            a = nc.scalar

            def weights_out(k):
                act.wait_ge(s_wtp, k + 1)
                blocks, col, _, _ = wgroups[k]
                w = sum(src.shape[0] for src in blocks)
                a.activation(wT[:, col:col + w], ps[:, 4 + k % 4, 0:w], ACT.Copy).then_inc(s_wev, 1)

            def pair_of_banks(bank):
                return ps[:, bank:bank + 2, :].rearrange("p k c -> p (k c)")[:, 0:ST * P]

            def xT_out(level, c):
                act.wait_ge(s_tp, NC * level + c + 1)
                a.activation(xT[:, CHUNK * c:CHUNK * (c + 1)], ps[:, c, :], ACT.Copy).then_inc(s_xT, 1)

            weights_out(0)
            for c in range(NC):
                xT_out(0, c)
            for s in range(BATCH + 4):
                if s < BATCH:
                    act.wait_ge(s_qsub, s + 1)
                    e = qkv[:, 2 * s:2 * s + 2, 0:256]
                    a.activation(e, e, ACT.Exp).then_inc(s_qexp, 1)
                if 2 <= s < BATCH + 2:
                    b = s - 2
                    act.wait_ge(s_qtp, b + 1)
                    a.activation(q0T[:, 256 * b:256 * (b + 1)], ps[:, 7, 0:256], ACT.Copy).then_inc(s_q0T, 1)
                if s >= 4:
                    b = s - 4
                    act.wait_ge(s_otp, b + 1)
                    a.activation(o0T[:, 256 * b:256 * (b + 1)], ps[:, 2 + b % 2, 0:256], ACT.Copy).then_inc(s_o0T, 1)
            act.wait_ge(s_kw, 16 * 5)
            a.activation(kE, kA, ACT.Exp, scale=-1.0).then_inc(s_ke, 1)
            for k in range(1, len(wgroups)):
                weights_out(k)
            for k in range(4):
                act.wait_ge(s_ab, k + 1)
                a.activation(l1A[:, 4 * k:4 * k + 4, :], ps[:, 4 + k, :].rearrange("p (h c) -> p h c", c=P),
                             ACT.Copy).then_inc(s_abs, 1)
            if levels > 1:
                for c in range(NC):
                    xT_out(1, c)
                    if c >= 2:
                        act.wait_ge(s_out, NC + c - 1)
                    for j in range(4):
                        act.wait_ge(s_h0, 4 * c + j + 1)
                        a.activation(h0T[:, c % 2, j, :], ps[:, 4 + j, :], ACT.Gelu,
                                     bias=b1c[:, j:j + 1]).then_inc(s_g0, 1)
                for k in range(4):
                    act.wait_ge(s_ab, 4 + k + 1)
                    a.activation(l1B[:, 4 * k:4 * k + 4, :], ps[:, 4 + k, :].rearrange("p (h c) -> p h c", c=P),
                                 ACT.Copy).then_inc(s_abs, 1)
                act.wait_ge(s_kaw, 2)
                a.activation(kg2, ka2, ACT.Exp, scale=float(P)).then_inc(s_kg, 1)
                for k in range(4):
                    q = slice(16 * k, 16 * k + 16)
                    act.wait_ge(s_kprod, k + 1)
                    a.activation(kexp[:, q, :], kexp[:, q, :], ACT.Exp).then_inc(s_kexp, 1)
            if levels > 2:
                for c in range(NC):
                    xT_out(2, c)
                for k in range(2):
                    act.wait_ge(s_g, k + 1)
                    a.activation(gram[:, 4 * k:4 * k + 4, :], ps[:, 4 + k, :].rearrange("p (h c) -> p h c", c=P),
                                 ACT.Copy).then_inc(s_gs, 1)
                for g in range(BATCH // GB + 1):
                    if g < BATCH // GB:
                        for b in range(GB):
                            for j in (0, 2):
                                if g >= 2:
                                    act.wait_ge(s_m, g - 1)
                                act.wait_ge(s_gb, (GB * g + b) * 4 + j + 1)
                                a.activation(gbuf[:, g % 2, 4 * j:4 * j + 4, P * b:P * (b + 1)],
                                             ps[:, 4 + j, :].rearrange("p (h c) -> p h c", c=P),
                                             ACT.Copy).then_inc(s_gba, 1)
                    if g >= 1:
                        q = g - 1
                        act.wait_ge(s_m, q + 1)
                        a.activation(l1M[:, GB * q:GB * (q + 1), :],
                                     ps[:, q % 4, 0:GB * P].rearrange("p (b c) -> p b c", c=P),
                                     ACT.Copy, scale=float(HDIM1) ** -0.5).then_inc(s_ms, 1)
            if levels > 3:
                act.wait_ge(s_kfp, 1)
                a.activation(kf, ps[:, 5, :].rearrange("p (m c) -> p m c", c=P), ACT.Copy).then_inc(s_kf, 1)
                for c in range(NC):
                    xT_out(3, c)
                act.wait_ge(s_lsub, 1)
                a.activation(r_pr, r_lg, ACT.Exp).then_inc(s_lexp, 1)
                def combT_out(t):
                    act.wait_ge(s_ctp, t + 1)
                    a.activation(combT[:, t, :], pair_of_banks(2 * (t % 2)), ACT.Copy).then_inc(s_cT, 1)

                for b in range(BATCH):
                    act.wait_ge(s_xdp, 2 * b + 1)
                    a.activation(xd[:, 0:4, b, :], ps[:, 4 + 2 * (b % 2), 0:HALF_SLOTS].rearrange("p (e s) -> p e s", s=CAP),
                                 ACT.Copy).then_inc(s_xda, 1)
                    if b:
                        combT_out(2 * b - 2)
                        combT_out(2 * b - 1)

                def outT(e):
                    for hb in range(2):
                        act.wait_ge(s_eop, 2 * e + hb + 1)
                        a.activation(eoT[:, 4 * hb:4 * hb + 4, e, :],
                                     ps[:, 2 * (e % 2) + hb, 0:HALF_SLOTS].rearrange("p (b s) -> p b s", s=CAP),
                                     ACT.Copy).then_inc(s_eoT, 1)

                for n in range(EXPERTS * 2 * NFB):
                    e, u = divmod(n, 2 * NFB)
                    act.wait_ge(s_eh1, n + 1)
                    if n >= 2:
                        act.wait_ge(s_eh, n - 1)
                    a.activation(esil[0:FB, n % 2, :], ps[0:FB, 4 + n % 2, 0:HALF_SLOTS], ACT.Silu).then_inc(s_sil, 1)
                    if e == 0 and u == 1:
                        combT_out(NT - 2)
                        combT_out(NT - 1)
                    if e and u == 2:
                        outT(e - 1)
                outT(EXPERTS - 1)
                for b in range(BATCH):
                    act.wait_ge(s_eot, b + 1)
                    a.activation(eo[:, b].rearrange("p k c -> p (k c)"), pair_of_banks(4 + 2 * (b % 2)),
                                 ACT.Copy).then_inc(s_eo, 1)
            if levels > 4:
                for c in range(NC):
                    xT_out(4, c)
                for c in range(NC):
                    act.wait_ge(s_y, c + 1)
                    a.activation(yT[:, CHUNK * c:CHUNK * (c + 1)], ps[:, c, :], ACT.Copy).then_inc(s_yT, 1)
            if levels > 5:
                act.wait_ge(s_cols, 16 * N_COLS)
                for c in range(NC):
                    act.wait_ge(s_tp, NC * 5 + c + 1)
                    a.activation(xnT[:, CHUNK * c:CHUNK * (c + 1)], ps[:, c, :], ACT.Identity,
                                 bias=cols[:, 2:3], scale=cols[:, 1:2]).then_inc(s_xT, 1)
            if levels > 6:
                act.wait_ge(s_hd, 80)
                a.activation(hd[:, 2, :], hd[:, 0, :], ACT.Exp).then_inc(s_ea, 1)
                for c in range(NC):
                    xT_out(6, c)
                act.wait_ge(s_sp1, 1)
                a.activation(d_n, d_n, ACT.Exp).then_inc(s_actc, 1)
                act.wait_ge(s_actc, 1)
                a.activation(d_l, d_n, ACT.Ln, bias=1.0).then_inc(s_sp2, 1)
                for c in range(NC + 1):
                    if c < NC:
                        t = slice(CHUNK * c, CHUNK * (c + 1))
                        for k in range(2):
                            act.wait_ge(s_z, 2 * c + k + 1)
                            i = CT * c + 2 * k
                            a.activation(sz[:, i:i + 2, :], ps[:, k, :].rearrange("p (t c) -> p t c", t=2),
                                         ACT.Silu).then_inc(s_sz, 1)
                        for k in range(3):
                            act.wait_ge(s_xbc, 3 * c + k + 1)
                            a.activation(xc[:, k, t], ps[:, 2 + k, :], ACT.Identity, bias=cols[:, 3 + k:4 + k],
                                         scale=cols[:, 9 + 4 * k:10 + 4 * k]).then_inc(s_acc, 1)
                    if c >= 1:
                        t = slice(CHUNK * (c - 1), CHUNK * c)
                        for k in range(2):
                            act.wait_ge(s_conv, 3 * (c - 1) + k + 1)
                            a.activation(xc[:, k, t], xc[:, k, t], ACT.Silu).then_inc(s_xc, 1)
                        act.wait_ge(s_conv, 3 * c)
                        a.activation(xc[0:NSTATE, 2, t], xc[0:NSTATE, 2, t], ACT.Silu).then_inc(s_xc, 1)
                        a.activation(cT[0:NSTATE, t], xc[NSTATE:P, 2, t], ACT.Silu).then_inc(s_xc, 1)
                def squares(b):
                    act.wait_ge(s_yg, b + 1)
                    if b:
                        act.wait_ge(s_sq, b)
                    for i in range(2):
                        t = 2 * b + i
                        ins = a.activation(sqj[:, i], ygt[:, b % 2, i, :], ACT.Square, accum_out=ssv[:, t:t + 1])
                    ins.then_inc(s_sq, 1)

                def yT_out(b):
                    act.wait_ge(s_yt, b + 1)
                    a.activation(ygT[:, :, SEQ * b:SEQ * (b + 1)], ps[:, 3, :].rearrange("p (k t) -> p k t", k=2),
                                 ACT.Copy).then_inc(s_ygT, 1)

                for q in range(BATCH * N_HEADS3):
                    b, h = divmod(q, N_HEADS3)
                    act.wait_ge(s_lp, q + 1)
                    if q >= 4:
                        act.wait_ge(s_yq, q - 3)
                    a.activation(mring[:, q % 4], ps[:, 4 + q % 2, 0:384].rearrange("p (k t) -> p k t", k=3),
                                 ACT.Exp).then_inc(s_le, 1)
                    if h == 2 and b:
                        squares(b - 1)
                    if h == 0 and b >= 2:
                        yT_out(b - 2)
                yT_out(BATCH - 2)
                squares(BATCH - 1)
                yT_out(BATCH - 1)
            if levels > 7:
                for c in range(NC):
                    act.wait_ge(s_tp, NC * 7 + c + 1)
                    a.activation(xpad[:, 2 * c:2 * c + 2, 1:SEQ + 1], ps[:, c, :].rearrange("p (b t) -> p b t", b=2),
                                 ACT.Copy).then_inc(s_xT, 1)
                for c in range(NC):
                    act.wait_ge(s_kp, c + 1)
                    a.activation(kact[:, CHUNK * c:CHUNK * (c + 1)], ps[:, 4 + c % 2, :], ACT.Relu).then_inc(s_kr, 1)
                    act.wait_ge(s_rp, c + 1)
                    a.activation(gate_r[:, CT * c:CT * (c + 1), :], ps[:, 6 + c % 2, :].rearrange("p (t c) -> p t c", c=P),
                                 ACT.Sigmoid).then_inc(s_rs, 1)

        @block.vector
        def _(dve):
            v = nc.vector
            n = [0]

            def link(ins):
                n[0] += 1
                ins.then_inc(s_dve, 1)
                dve.wait_ge(s_dve, n[0])

            def ln_stats(layer, c, bias_count=None):
                t = slice(CT * c, CT * (c + 1))
                if bias_count is not None:
                    dve.wait_ge(s_xb, bias_count)
                dve.wait_ge(s_out, NC * layer + c + 1)
                out = ps[:, c, :].rearrange("p (t c) -> p t c", c=P)
                xc_tok = x_tok[:, t, :]
                if layer == 5:
                    link(v.scalar_tensor_tensor(out=xc_tok, in0=out, scalar=cols[:, 38:39], in1=xc_tok,
                                                op0=ALU.mult, op1=ALU.add))
                elif layer == 6:
                    dve.wait_ge(s_rms, c + 1)
                    for i in range(CT):
                        k = CT * c + i
                        ins = v.scalar_tensor_tensor(out=x_tok[:, k, :], in0=out[:, i, :], scalar=rms[:, k:k + 1],
                                                     in1=x_tok[:, k, :], op0=ALU.mult, op1=ALU.add)
                    link(ins)
                elif layer == 7:
                    dve.wait_ge(s_rs, c + 1)
                    link(v.tensor_tensor(gate_r[:, t, :], out, gate_r[:, t, :], ALU.mult))
                    link(v.tensor_tensor(xc_tok, gate_r[:, t, :], xc_tok, ALU.add))
                else:
                    link(v.tensor_tensor(xc_tok, out, xc_tok, ALU.add))
                for i in range(CT * c, CT * (c + 1)):
                    ins = v.bn_stats(bn[:, i, :], x_tok[:, i, :])
                link(ins)
                for i in range(CT * c, CT * (c + 1)):
                    ins = v.bn_aggr(mv[:, i, :], bn[:, i, :])
                ins.then_inc(s_mv, 1)

            def ln_apply(layer, c):
                dve.wait_ge(s_rstd, NC * layer + c + 1)
                for i in range(CT * c, CT * (c + 1)):
                    ins = v.tensor_scalar(x_tok[:, i, :], x_tok[:, i, :], mv[:, i, 0:1], rstd[:, i:i + 1],
                                          ALU.subtract, ALU.mult)
                ins.then_inc(s_xtok, 1)

            def layer_norm(layer, bias_from=None):
                for c in range(NC + 1):
                    if c < NC:
                        ln_stats(layer, c, None if bias_from is None else bias_from + c + 1)
                    if c >= 1:
                        ln_apply(layer, c - 1)

            def square_k(c):
                t = slice(CHUNK * c, CHUNK * (c + 1))
                dve.wait_ge(s_kr, c + 1)
                v.tensor_tensor(kact[:, t], kact[:, t], kact[:, t], ALU.mult).then_inc(s_ka2, 1)

            dve.wait_ge(s_b0, 64)
            dve.wait_ge(s_const, 3)
            for s in range(BATCH + 4):
                if s < BATCH:
                    b = s
                    t = slice(2 * b, 2 * b + 2)
                    dve.wait_ge(s_qkv, b + 1)
                    ins = v.tensor_tensor(qkv[:, t, 0:384], ps[:, 4:6, 0:384],
                                          bqkv.unsqueeze(1).broadcast_to([P, 2, 384]), ALU.add)
                    ins.then_inc(s_qevac, 1)
                    dve.wait_ge(s_qevac, b + 1)
                    v.tensor_reduce(gmax[:, t, :], qkv[:, t, 0:256].rearrange("p t (g e) -> p t g e", e=HDIM0),
                                    AX.X, ALU.max).then_inc(s_qmax, 1)
                if 1 <= s <= BATCH:
                    b = s - 1
                    t = slice(2 * b, 2 * b + 2)
                    dve.wait_ge(s_qexp, b + 1)
                    link(v.tensor_reduce(gsum[:, t, :], qkv[:, t, 0:256].rearrange("p t (g e) -> p t g e", e=HDIM0),
                                         AX.X, ALU.add))
                    v.reciprocal(grec[:, t, :], gsum[:, t, :]).then_inc(s_qrec, 1)
                if 2 <= s < BATCH + 2:
                    b = s - 2
                    dve.wait_ge(s_ctx, b + 1)
                    v.tensor_tensor(ctxs[:, b, :], ps[:, 6, 0:144], mask144[:], ALU.mult).then_inc(s_ctxs, 1)
                if 3 <= s < BATCH + 3:
                    b = s - 3
                    t = slice(2 * b, 2 * b + 2)
                    dve.wait_ge(s_num, b + 1)
                    nd = ps[:, b % 2, 0:288].rearrange("p (t c) -> p t c", c=144)
                    link(v.reciprocal(den0[:, t, :], nd[:, :, P:144]))
                    v.tensor_tensor(o0[:, t, :].rearrange("p t (h e) -> p t h e", e=HDIM0),
                                    nd[:, :, 0:P].rearrange("p t (h e) -> p t h e", e=HDIM0),
                                    den0[:, t, :].unsqueeze(3).broadcast_to([P, 2, HEADS0, HDIM0]),
                                    ALU.mult).then_inc(s_onum, 1)
            dve.wait_ge(s_kw, 16 * 5)
            dve.wait_ge(s_ke, 1)
            for k in range(2):
                v.tensor_scalar(kaw[:, 0, k, :], kE, cols[:, 0:1], -1.0, ALU.mult, ALU.mult)
                ins = v.scalar_tensor_tensor(out=kaw[:, 1, k, :], in0=kB, scalar=cols[:, 0:1], in1=kC,
                                             op0=ALU.mult, op1=ALU.mult)
            ins.then_inc(s_ka, 1)
            layer_norm(0, 0)
            dve.wait_ge(s_katp, 1)
            dve.wait_ge(s_const, N_CONST)
            for half in range(2):
                r = slice(NSTATE * half, NSTATE * (half + 1))
                v.tensor_copy(ka2[r, :], ps[r, 4, NSTATE * half:NSTATE * (half + 1)])
                v.tensor_copy(kWE[r, :, half, 0], ps[r, 4, P + NSTATE * half:P + NSTATE * (half + 1)]).then_inc(s_kaw, 1)
            if levels > 1:
                layer_norm(1, NC)
                dve.wait_ge(s_kg, 1)
                dve.wait_ge(s_kaw, 2)
                for half in range(2):
                    r = slice(NSTATE * half, NSTATE * (half + 1))
                    v.tensor_tensor(kWE[r, :, half, 1], kWE[r, :, half, 0], kg2[r, :], ALU.mult).then_inc(s_kwe, 1)
            if levels > 2:
                for g in range(BATCH // GB):
                    for b in range(GB):
                        for j in (1, 3):
                            if g >= 2:
                                dve.wait_ge(s_m, g - 1)
                            dve.wait_ge(s_gb, (GB * g + b) * 4 + j + 1)
                            v.tensor_copy(gbuf[:, g % 2, 4 * j:4 * j + 4, P * b:P * (b + 1)],
                                          ps[:, 4 + j, :].rearrange("p (h c) -> p h c", c=P)).then_inc(s_gbv, 1)
                layer_norm(2)
            if levels > 3:
                dve.wait_ge(s_kps, 1)
                link(v.tensor_copy(ktok.rearrange("p i (h q) -> p i h q", h=2),
                                   ps[:, 4, 0:256].rearrange("p (q h i) -> p i h q", h=2, i=2)))
                v.tensor_tensor(ktok[0:1, 0, :], ktok[0:1, 0, :], dpr[0:1, :], ALU.add).then_inc(s_kt, 1)
                wide = lambda x: x.unsqueeze(2).broadcast_to([P, NT, EXPERTS])
                tiew = tie[:].unsqueeze(1).broadcast_to([P, NT, EXPERTS])
                dve.wait_ge(s_lg, 1)
                lg = ps[:, 4, 0:NT * EXPERTS].rearrange("p (t e) -> p t e", e=EXPERTS)
                link(v.tensor_reduce(r_mx, lg, AX.X, ALU.max))
                v.tensor_tensor(r_lg, lg, wide(r_mx), ALU.subtract).then_inc(s_lsub, 1)
                dve.wait_ge(s_lexp, 1)
                link(v.tensor_reduce(r_sum, r_pr, AX.X, ALU.add))
                link(v.reciprocal(r_rec, r_sum))
                link(v.tensor_tensor(r_pr, r_pr, wide(r_rec), ALU.mult))
                link(v.tensor_reduce(r_mx, r_pr, AX.X, ALU.max))
                link(v.tensor_tensor(r_s, r_pr, wide(r_mx), ALU.is_ge))
                link(v.tensor_tensor(r_s, r_s, tiew, ALU.mult))
                link(v.tensor_reduce(r_t, r_s, AX.X, ALU.max))
                link(v.tensor_tensor(r_oh, r_s, wide(r_t), ALU.is_ge))
                link(v.scalar_tensor_tensor(out=r_p2, in0=r_oh, scalar=-2.0, in1=r_pr, op0=ALU.mult, op1=ALU.add))
                link(v.tensor_reduce(r_mx, r_p2, AX.X, ALU.max))
                link(v.tensor_tensor(r_s, r_p2, wide(r_mx), ALU.is_ge))
                link(v.tensor_tensor(r_s, r_s, tiew, ALU.mult))
                link(v.tensor_reduce(r_t, r_s, AX.X, ALU.max))
                link(v.tensor_tensor(r_s, r_s, wide(r_t), ALU.is_ge))
                v.tensor_tensor(r_mask, r_oh, r_s, ALU.add).then_inc(s_mask, 1)
                dve.wait_ge(s_mask, 1)
                dve.wait_ge(s_cnt, 1)
                pair = lambda x: x.rearrange("p (b two) e -> p b two e", two=2)
                v.tensor_tensor(pair(r_pos), ps[:, 5, 0:NT * EXPERTS].rearrange("p (two b e) -> p b two e", two=2, e=EXPERTS),
                                pair(r_mask), ALU.mult).then_inc(s_pos, 1)

                def dispatch(t):
                    if t >= 4:
                        dve.wait_ge(s_xdp, t - 2 if t % 2 == 0 else t - 3)
                        dve.wait_ge(s_comb, t - 3)
                    v.tensor_tensor(disp[:, t % 4], iota_slot[:].unsqueeze(1).broadcast_to([P, EXPERTS, CAP]),
                                    r_pos[:, t, :].unsqueeze(2).broadcast_to([P, EXPERTS, CAP]),
                                    ALU.is_equal).then_inc(s_disp, 1)

                dve.wait_ge(s_pos, 1)
                for t in range(4):
                    dispatch(t)
                for b in range(BATCH):
                    dve.wait_ge(s_xdp, 2 * b + 2)
                    v.tensor_copy(xd[:, 4:8, b, :], ps[:, 5 + 2 * (b % 2), 0:HALF_SLOTS].rearrange("p (e s) -> p e s", s=CAP)
                                  ).then_inc(s_xdv, 1)
                    if b + 2 < BATCH:
                        dispatch(2 * b + 4)
                        dispatch(2 * b + 5)
                for m in range(EXPERTS * 2 * NFB):
                    e, u = divmod(m, 2 * NFB)
                    j, hb = divmod(u, 2)
                    dve.wait_ge(s_eh3, m + 1)
                    dve.wait_ge(s_sil, m + 1)
                    if e >= 2:
                        dve.wait_ge(s_eop, 2 * (e - 1))
                    v.tensor_tensor(eh[0:FB, e % 2, j, HALF_SLOTS * hb:HALF_SLOTS * (hb + 1)],
                                    ps[0:FB, 6 + m % 2, 0:HALF_SLOTS], esil[0:FB, m % 2, :], ALU.mult).then_inc(s_eh, 1)
                layer_norm(3)
            if levels > 4:
                dve.wait_ge(s_hd, 80)
                for c in range(NC):
                    dve.wait_ge(s_u, c + 1)
                    v.tensor_tensor(u_tok[:, CT * c:CT * (c + 1), :], ps[:, 4 + c, :].rearrange("p (t c) -> p t c", c=P),
                                    bin_tok.unsqueeze(1).broadcast_to([P, CT, P]), ALU.add).then_inc(s_us, 1)
                dve.wait_ge(s_kf, 1)
                for hb in range(2):
                    dve.wait_ge(s_uf, hb + 1)
                    for k, (um, km) in enumerate([(0, 0), (2, 2), (0, 2), (2, 0)]):
                        v.tensor_tensor(prod[:, 4 * hb + k], ps[:, 4 + um:6 + um, :].rearrange("p m (b c) -> p m b c", c=P),
                                        kf[:, km:km + 2, :].unsqueeze(2).broadcast_to([P, 2, 4, P]),
                                        ALU.mult).then_inc(s_prod, 1)
                layer_norm(4, 2 * NC)
            if levels > 5:
                for c in range(NC + 1):
                    if c < NC:
                        dve.wait_ge(s_xtok, 4 * NC + c + 1)
                        for i in range(CT * c, CT * (c + 1)):
                            ins = v.bn_stats(bn[:, i, :], x_tok[:, i, :])
                        link(ins)
                        for i in range(CT * c, CT * (c + 1)):
                            ins = v.bn_aggr(mv2[:, i, :], bn[:, i, :])
                        ins.then_inc(s_mv2, 1)
                    if c >= 1:
                        dve.wait_ge(s_rstd2, c)
                        dve.wait_ge(s_mv2, c)
                        for i in range(CT * (c - 1), CT * c):
                            ins = v.tensor_scalar(xh[:, i, :], x_tok[:, i, :], mv2[:, i, 0:1], rstd2[:, i:i + 1],
                                                  ALU.subtract, ALU.mult)
                        ins.then_inc(s_xh, 1)
                v.tensor_reduce(cols[:, 24:25], bw, AX.X, ALU.add, apply_absolute_value=True)
                for c in range(NC):
                    dve.wait_ge(s_xT, 5 * NC + c + 1)
                    ins = v.tensor_reduce(cols[:, 25 + c:26 + c], xnT[:, CHUNK * c:CHUNK * (c + 1)], AX.X, ALU.max,
                                          apply_absolute_value=True)
                link(ins)
                v.tensor_reduce(cols[:, 29:30], cols[:, 25:29], AX.X, ALU.max).then_inc(s_gmx, 1)
                dve.wait_ge(s_gt, 1)
                v.tensor_reduce(cols[0:1, 36:37], ps[0:1, 4, 0:P], AX.X, ALU.max).then_inc(s_gm1, 1)
                dve.wait_ge(s_gb2, 1)
                gam, beta, thr, nthr = cols[:, 30:31], cols[:, 34:35], cols[:, 35:36], cols[:, 37:38]
                link(v.tensor_copy(cols[:, 30:32], ps[:, 5, 0:2]))
                v.reciprocal(cols[:, 32:33], gam)
                link(v.tensor_scalar(beta, cols[:, 31:32], 1.0 / (P * P), None, ALU.mult))
                v.tensor_scalar(cols[:, 33:34], cols[:, 32:33], 128.0, None, ALU.mult)
                v.tensor_scalar(cols[:, 38:39], gam, beta, 1.0 / 128.0, ALU.mult, ALU.mult)
                link(v.tensor_scalar(thr, beta, 1e-5, 0.5, ALU.add, ALU.mult))
                link(v.tensor_scalar(nthr, thr, -1.0, None, ALU.mult))
                link(v.tensor_scalar(bwt, bw, nthr, None, ALU.is_lt))
                v.scalar_tensor_tensor(out=bwq, in0=bw, scalar=thr, in1=bwt, op0=ALU.is_gt,
                                       op1=ALU.subtract).then_inc(s_bwq, 1)
                for c in range(NC):
                    t = slice(CHUNK * c, CHUNK * (c + 1))
                    link(v.tensor_scalar(xqT[:, t], xnT[:, t], cols[:, 33:34], QCLIP, ALU.mult, ALU.min))
                    v.tensor_scalar(xqT[:, t], xqT[:, t], -QCLIP, None, ALU.max).then_inc(s_xq, 1)
                layer_norm(5)
            if levels > 6:
                for k in range(2):
                    w = wT[:, W3OUT + P * k:W3OUT + P * (k + 1)]
                    ins = v.tensor_scalar(w, w, cols[:, 20 + k:21 + k], None, ALU.mult)
                ins.then_inc(s_nw, 1)
                head4 = lambda x: x.unsqueeze(1).broadcast_to([P, NT, N_HEADS3])
                dve.wait_ge(s_dtp, 1)
                link(v.tensor_tensor(d_v, ps[:, 7, 0:64].rearrange("p (t h) -> p t h", h=N_HEADS3), head4(hd[:, 1, :]), ALU.add))
                v.scalar_tensor_tensor(out=d_n, in0=d_v, scalar=-1.0, in1=d_v, op0=ALU.mult, op1=ALU.min).then_inc(s_sp1, 1)
                dve.wait_ge(s_ea, 1)
                v.tensor_scalar(hd[:, 2, :], hd[:, 2, :], -1.0, None, ALU.mult)
                dve.wait_ge(s_sp2, 1)
                link(v.scalar_tensor_tensor(out=d_dt, in0=d_v, scalar=0.0, in1=d_l, op0=ALU.max, op1=ALU.add))
                v.tensor_tensor(d_a, d_dt, head4(hd[:, 2, :]), ALU.mult).then_inc(s_a, 1)
                for c in range(NC):
                    for k in range(3):
                        dve.wait_ge(s_acc, 3 * c + k + 1)
                        src = ps[:, 2 + k, :].rearrange("p (b t) -> p b t", b=2)
                        acc = xc[:, k, CHUNK * c:CHUNK * (c + 1)].rearrange("p (b t) -> p b t", b=2)
                        for j in range(1, 4):
                            ins = v.scalar_tensor_tensor(out=acc[:, :, j:SEQ], in0=src[:, :, 0:SEQ - j],
                                                         scalar=cols[:, 9 + 4 * k - j:10 + 4 * k - j],
                                                         in1=acc[:, :, j:SEQ], op0=ALU.mult, op1=ALU.add)
                            if j < 3:
                                link(ins)
                        ins.then_inc(s_conv, 1)

                def xs_out(b):
                    dve.wait_ge(s_xsp, b + 1)
                    t = slice(2 * b, 2 * b + 2)
                    src = ps[:, 2, :].rearrange("p (t h e) -> p t h e", t=2, h=N_HEADS3)
                    v.tensor_tensor(xs[:, t, :, :], src, d_dt[:, t, :].unsqueeze(3).broadcast_to([P, 2, N_HEADS3, HEAD3]),
                                    ALU.mult)
                    v.tensor_tensor(xdd[:, b % 2], src,
                                    dsk.unsqueeze(1).unsqueeze(3).broadcast_to([P, 2, N_HEADS3, HEAD3]),
                                    ALU.mult).then_inc(s_xs, 1)

                def scores_out(b):
                    dve.wait_ge(s_gtp, b + 1)
                    v.tensor_tensor(gts[:, b % 2], ps[:, 6, 0:384].rearrange("p (k t) -> p k t", k=3), causal[:],
                                    ALU.mult).then_inc(s_gts, 1)

                def add_d(b):
                    dve.wait_ge(s_yq, 4 * b + 4)
                    if b >= 2:
                        dve.wait_ge(s_yt, b - 1)
                        dve.wait_ge(s_sq, b - 1)
                    v.tensor_tensor(ygt[:, b % 2], ps[:, 7, :].rearrange("p (t c) -> p t c", t=2),
                                    xdd[:, b % 2].rearrange("p t h e -> p t (h e)"), ALU.add).then_inc(s_yd, 1)

                def mean_square(c):
                    dve.wait_ge(s_sq, 2 * c + 2)
                    t = slice(CT * c, CT * (c + 1))
                    v.tensor_scalar(ssv[:, t], ssv[:, t], 1.0 / D_INNER, 1e-5, ALU.mult, ALU.add).then_inc(s_ssv, 1)

                xs_out(0)
                scores_out(0)
                for q in range(BATCH * N_HEADS3):
                    b, h = divmod(q, N_HEADS3)
                    if h == 2 and b + 1 < BATCH:
                        xs_out(b + 1)
                        scores_out(b + 1)
                    dve.wait_ge(s_le, q + 1)
                    dve.wait_ge(s_gts, b + 1)
                    v.tensor_tensor(mring[:, q % 4], mring[:, q % 4], gts[:, b % 2], ALU.mult).then_inc(s_mm, 1)
                    if h == 0 and b:
                        add_d(b - 1)
                    if h == 0 and b in (3, 5, 7):
                        mean_square((b - 3) // 2)
                    if h == 0 and b in (4, 6):
                        ln_stats(6, b // 2 - 2)
                    if h == 1 and b in (5, 7):
                        ln_apply(6, (b - 5) // 2)
                add_d(BATCH - 1)
                ln_stats(6, 2)
                mean_square(3)
                ln_apply(6, 2)
                ln_stats(6, 3)
                ln_apply(6, 3)
            if levels > 7:
                for c in range(NC):
                    b = slice(2 * c, 2 * c + 2)
                    dve.wait_ge(s_dif, c + 1)
                    v.scalar_tensor_tensor(out=xk[:, b, :], in0=xdif[:, b, :], scalar=cols[:, 23:24],
                                           in1=xpad[:, b, 0:SEQ], op0=ALU.mult, op1=ALU.add).then_inc(s_xk, 1)
                    v.scalar_tensor_tensor(out=xr[:, b, :], in0=xdif[:, b, :], scalar=cols[:, 22:23],
                                           in1=xpad[:, b, 0:SEQ], op0=ALU.mult, op1=ALU.add).then_inc(s_xr, 1)
                    if c:
                        square_k(c - 1)
                square_k(NC - 1)
                layer_norm(7)

        @block.tensor
        def _(pe):
            te = nc.tensor

            def weights_in(k):
                blocks, _, sm, val = wgroups[k]
                pe.wait_ge(sm, val)
                at = 0
                if k >= 4:
                    pe.wait_ge(s_wev, k - 3)
                for i, src in enumerate(blocks):
                    r = src.shape[0]
                    mm = te.transpose(ps[:, 4 + k % 4, at:at + r], src, ident[0:r, 0:r])
                    at += r
                mm.then_inc(s_wtp, 1)

            def x_transpose(level, c):
                if level == 5:
                    pe.wait_ge(s_xh, c + 1)
                elif level:
                    pe.wait_ge(s_xtok, NC * (level - 1) + c + 1)
                else:
                    pe.wait_ge(s_x, 16 * NC)
                for i in range(CT):
                    src = xh if level == 5 else x_tok
                    mm = te.transpose(ps[:, c, P * i:P * (i + 1)], src[:, CT * c + i, :], ident[:])
                mm.then_inc(s_tp, 1)

            def xTt(t):
                return xT[:, P * t:P * (t + 1)]

            def half_rows(k):
                return slice(HDIM1 * (k // 2), HDIM1 * (k // 2) + HDIM1)

            pe.wait_ge(s_const, 2)
            weights_in(0)
            for c in range(NC):
                x_transpose(0, c)
            pe.wait_ge(s_ones, 1)
            for s in range(BATCH + 4):
                if s < BATCH:
                    b = s
                    pe.wait_ge(s_xT, b // 2 + 1)
                    if s == 0:
                        pe.wait_ge(s_wev, 1)
                    else:
                        pe.wait_ge(s_qevac, b)
                    for i in range(2):
                        mm = te.matmul(ps[:, 4 + i, 0:384], xTt(2 * b + i), wT[:, WQKV:WQKV + 384],
                                       start=True, stop=True)
                    mm.then_inc(s_qkv, 1)
                if 1 <= s <= BATCH:
                    b = s - 1
                    pe.wait_ge(s_qk, b + 1)
                    if b >= 1:
                        pe.wait_ge(s_ctxs, b)
                    for i in range(2):
                        t = 2 * b + i
                        mm = te.matmul(ps[:, 6, 0:144], qkv[:, t, P:2 * P], qkv[:, t, 256:400],
                                       start=(i == 0), stop=(i == 1))
                    mm.then_inc(s_ctx, 1)
                    if b >= 1:
                        pe.wait_ge(s_q0T, b)
                    for i in range(2):
                        mm = te.transpose(ps[:, 7, P * i:P * (i + 1)], qkv[:, 2 * b + i, 0:P], ident[:])
                    mm.then_inc(s_qtp, 1)
                if 2 <= s < BATCH + 2:
                    b = s - 2
                    pe.wait_ge(s_ctxs, b + 1)
                    pe.wait_ge(s_q0T, b + 1)
                    if b >= 2:
                        pe.wait_ge(s_onum, b - 1)
                    elif b == 0:
                        pe.wait_ge(s_xT, NC)
                    for i in range(2):
                        mm = te.matmul(ps[:, b % 2, 144 * i:144 * (i + 1)], q0T[:, P * (2 * b + i):P * (2 * b + i + 1)],
                                       ctxs[:, b, :], start=True, stop=True)
                    mm.then_inc(s_num, 1)
                if s >= 4:
                    b = s - 4
                    pe.wait_ge(s_o0, b + 1)
                    if b >= 2:
                        pe.wait_ge(s_o0T, b - 1)
                    for i in range(2):
                        mm = te.transpose(ps[:, 2 + b % 2, P * i:P * (i + 1)], o0[:, 2 * b + i, :], ident[:])
                    mm.then_inc(s_otp, 1)
            for c in range(NC):
                pe.wait_ge(s_o0T, BATCH if c >= 2 else 2 * c + 2)
                pe.wait_ge(s_onum, BATCH)
                for i in range(CT):
                    t = CT * c + i
                    mm = te.matmul(ps[:, c, P * i:P * (i + 1)], o0T[:, P * t:P * (t + 1)], wT[:, WP:WP + P],
                                   start=True, stop=True)
                mm.then_inc(s_out, 1)
            pe.wait_ge(s_q0T, BATCH)
            pe.wait_ge(s_ctxs, BATCH)
            pe.wait_ge(s_qevac, BATCH)
            for k in range(1, len(wgroups)):
                weights_in(k)
            for k in range(4):
                pe.wait_ge(s_wev, len(wgroups) - 3 + k)
                r = half_rows(k)
                for i in range(4):
                    pair = 4 * (k % 2) + i
                    mm = te.matmul(ps[:, 4 + k, P * i:P * (i + 1)], l1w[r, 1, pair, :], l1w[r, 0, pair, :],
                                   start=True, stop=True)
                mm.then_inc(s_ab, 1)
            pe.wait_ge(s_abs, 1)
            pe.wait_ge(s_ka, 1)
            te.transpose(ps[:, 4, 0:P], kaw[:, 0, :, :], ident[:])
            te.transpose(ps[:, 4, P:2 * P], kaw[:, 1, :, :], ident[:]).then_inc(s_katp, 1)
            if levels > 1:
                pe.wait_ge(s_wf, 64)

                def hidden0(c):
                    x_transpose(1, c)
                    pe.wait_ge(s_xT, NC + c + 1)
                    for j in range(4):
                        if c:
                            pe.wait_ge(s_g0, 4 * (c - 1) + j + 1)
                        else:
                            pe.wait_ge(s_abs, j + 1)
                            pe.wait_ge(s_kaw, 2)
                        te.matmul(ps[:, 4 + j, :], w1s[:, P * j:P * (j + 1)], xT[:, CHUNK * c:CHUNK * (c + 1)],
                                  start=True, stop=True).then_inc(s_h0, 1)

                def out0(c):
                    pe.wait_ge(s_g0, 4 * c + 4)
                    for i in range(CT):
                        for j in range(4):
                            mm = te.matmul(ps[:, c, P * i:P * (i + 1)], h0T[:, c % 2, j, P * i:P * (i + 1)],
                                           w2s[:, j, :], start=(j == 0), stop=(j == 3))
                    mm.then_inc(s_out, 1)

                for c in range(NC + 1):
                    if c < NC:
                        hidden0(c)
                    if c >= 1:
                        out0(c - 1)
                pe.wait_ge(s_g0, 16)
                for k in range(4):
                    r = half_rows(k)
                    for i in range(4):
                        pair = 4 * (k % 2) + i
                        mm = te.matmul(ps[:, 4 + k, P * i:P * (i + 1)], l1w[r, 2, pair, :],
                                       wT[r, WO1 + P * pair:WO1 + P * (pair + 1)], start=True, stop=True)
                    mm.then_inc(s_ab, 1)
            if levels > 2:
                for c in range(NC):
                    x_transpose(2, c)
                    if c % 2 == 0:
                        pe.wait_ge(s_abs, 8)
                    for b in (2 * c, 2 * c + 1):
                        for i in range(2):
                            mm = te.matmul(ps[:, 4 + b // 4, P * (b % 4):P * (b % 4 + 1)], x_tok[:, 2 * b + i, :],
                                           x_tok[:, 2 * b + i, :], start=(i == 0), stop=(i == 1))
                    if c % 2:
                        mm.then_inc(s_g, 1)
                pe.wait_ge(s_gs, 2)

                def sum_heads(g):
                    pe.wait_ge(s_gba, 2 * GB * (g + 1))
                    pe.wait_ge(s_gbv, 2 * GB * (g + 1))
                    pe.wait_ge(s_xT, 2 * NC + g + 1)
                    for h in range(HEADS1):
                        mm = te.matmul(ps[:, g, 0:GB * P], l1A[:, h, :], gbuf[:, g % 2, h, :],
                                       start=(h == 0), stop=(h == HEADS1 - 1))
                    mm.then_inc(s_m, 1)

                for g in range(BATCH // GB):
                    for b in range(GB * g, GB * (g + 1)):
                        for j in range(4):
                            if b:
                                pe.wait_ge(s_gbv if j % 2 else s_gba, 2 * (b - 1) + j // 2 + 1)
                            te.matmul(ps[:, 4 + j, :], gram[:, b, :],
                                      l1B[:, 4 * j:4 * j + 4, :], start=True, stop=True).then_inc(s_gb, 1)
                    if g:
                        sum_heads(g - 1)
                sum_heads(BATCH // GB - 1)
                for c in range(NC):
                    pe.wait_ge(s_ms, c + 1)
                    for i in range(CT):
                        t = CT * c + i
                        mm = te.matmul(ps[:, c, P * i:P * (i + 1)], xTt(t), l1M[:, t // 2, :], start=True, stop=True)
                    mm.then_inc(s_out, 1)
            if levels > 3:
                pe.wait_ge(s_kwe, 2)
                pe.wait_ge(s_kexp, 4)
                pe.wait_ge(s_gba, BATCH * 2)
                for q in range(NSTATE):
                    mm = te.matmul(ps[:, 4, 4 * q:4 * q + 4], kexp[:, q, :], kWE[:, q, :, :], start=True, stop=True)
                mm.then_inc(s_kps, 1)
                pe.wait_ge(s_kt, 1)
                pe.wait_ge(s_four, 48)
                for m in range(4):
                    for k in range(2):
                        mm = te.matmul(ps[:, 5, P * m:P * (m + 1)], four[:, k, P * m:P * (m + 1)], ktok[:, k, :],
                                       start=(k == 0), stop=(k == 1))
                mm.then_inc(s_kfp, 1)
                for c in range(NC):
                    x_transpose(3, c)
                for t in range(NT):
                    pe.wait_ge(s_xT, 3 * NC + t // CT + 1)
                    mm = te.matmul(ps[:, 4, EXPERTS * t:EXPERTS * (t + 1)], xTt(t), wT[:, GATE:GATE + EXPERTS],
                                   start=True, stop=True)
                mm.then_inc(s_lg, 1)
                pe.wait_ge(s_mask, 1)
                pe.wait_ge(s_kf, 1)
                mpair = r_mask.rearrange("p (b two) e -> p b two e", two=2)
                te.matmul(ps[:, 5, 0:64], tri[:], mpair[:, :, 0, :], start=True, stop=True)
                te.matmul(ps[:, 5, 64:128], tri[:], mpair[:, :, 1, :], start=True, stop=False)
                te.matmul(ps[:, 5, 64:128], ones[:], mpair[:, :, 0, :], start=False, stop=True).then_inc(s_cnt, 1)
                pe.wait_ge(s_pos, 1)

                def gather(b):
                    pe.wait_ge(s_disp, 2 * b + 2)
                    if b >= 2:
                        pe.wait_ge(s_xda, b - 1)
                        pe.wait_ge(s_xdv, b - 1)
                    for h in range(2):
                        for k in range(2):
                            t = 2 * b + k
                            mm = te.matmul(ps[:, 4 + 2 * (b % 2) + h, 0:HALF_SLOTS], x_tok[:, t, :],
                                           disp[:, t % 4, 4 * h:4 * h + 4, :], start=(k == 0), stop=(k == 1))
                        mm.then_inc(s_xdp, 1)

                def comb_transpose(b):
                    for t in (2 * b, 2 * b + 1):
                        pe.wait_ge(s_comb, t + 1)
                        if t >= 2:
                            pe.wait_ge(s_cT, t - 1)
                        for k in range(ST):
                            mm = te.transpose(ps[:, 2 * (t % 2) + k // 4, P * (k % 4):P * (k % 4 + 1)],
                                              comb[:, t % 4, P * k:P * (k + 1)], ident[:])
                        mm.then_inc(s_ctp, 1)

                def expert_out(e):
                    pe.wait_ge(s_eh, 8 * e + 8)
                    if e >= 2:
                        pe.wait_ge(s_eoT, 2 * (e - 1))
                    elif e == 0:
                        pe.wait_ge(s_cT, NT)
                    for hb in range(2):
                        for j in range(NFB):
                            mm = te.matmul(ps[:, 2 * (e % 2) + hb, 0:HALF_SLOTS], ew2[e % 2][0:FB, j, :],
                                           eh[0:FB, e % 2, j, HALF_SLOTS * hb:HALF_SLOTS * (hb + 1)],
                                           start=(j == 0), stop=(j == NFB - 1))
                        mm.then_inc(s_eop, 1)

                for b in range(BATCH):
                    gather(b)
                    if b:
                        comb_transpose(b - 1)
                for n in range(EXPERTS * 2 * NFB):
                    e, u = divmod(n, 2 * NFB)
                    j, hb = divmod(u, 2)
                    if u == 0:
                        pe.wait_ge(s_ew[e % 2], 48 * (e // 2 + 1))
                    rhs = xd[:, e, 4 * hb:4 * hb + 4, :]
                    if n >= 2:
                        pe.wait_ge(s_sil, n - 1)
                    else:
                        pe.wait_ge(s_xda, BATCH)
                        pe.wait_ge(s_xdv, BATCH)
                    te.matmul(ps[0:FB, 4 + n % 2, 0:HALF_SLOTS], ew1[e % 2][:, FB * j:FB * (j + 1)], rhs,
                              start=True, stop=True).then_inc(s_eh1, 1)
                    if n >= 2:
                        pe.wait_ge(s_eh, n - 1)
                    te.matmul(ps[0:FB, 6 + n % 2, 0:HALF_SLOTS], ew3[e % 2][:, FB * j:FB * (j + 1)], rhs,
                              start=True, stop=True).then_inc(s_eh3, 1)
                    if n == 0:
                        comb_transpose(BATCH - 1)
                    if e and u == 1:
                        expert_out(e - 1)
                expert_out(EXPERTS - 1)

                def out_transpose(b):
                    pe.wait_ge(s_eoT, 2 * EXPERTS)
                    if b >= 2:
                        pe.wait_ge(s_eo, b - 1)
                    slots = eoT[:, b].rearrange("p e s -> p (e s)")
                    for k in range(ST):
                        mm = te.transpose(ps[:, 4 + 2 * (b % 2) + k // 4, P * (k % 4):P * (k % 4 + 1)],
                                          slots[:, P * k:P * (k + 1)], ident[:])
                    mm.then_inc(s_eot, 1)

                out_transpose(0)
                for b in range(BATCH):
                    if b + 1 < BATCH:
                        out_transpose(b + 1)
                    pe.wait_ge(s_eo, b + 1)
                    for t in (2 * b, 2 * b + 1):
                        for k in range(ST):
                            mm = te.matmul(ps[:, t // CT, P * (t % CT):P * (t % CT + 1)], combT[:, t, P * k:P * (k + 1)],
                                           eo[:, b, k, :], start=(k == 0), stop=(k == ST - 1))
                    if b % 2:
                        mm.then_inc(s_out, 1)
            if levels > 4:
                for c in range(NC):
                    x_transpose(4, c)
                    pe.wait_ge(s_xT, 4 * NC + c + 1)
                    if c == 0:
                        pe.wait_ge(s_eo, BATCH)
                    for i in range(CT):
                        mm = te.matmul(ps[:, 4 + c, P * i:P * (i + 1)], xTt(CT * c + i), wT[:, WIN:WIN + P],
                                       start=True, stop=True)
                    mm.then_inc(s_u, 1)
                pe.wait_ge(s_us, NC)
                upair = u_tok.rearrange("p (b two) c -> p b two c", two=2)
                for hb in range(2):
                    if hb:
                        pe.wait_ge(s_prod, 4)
                    for m in range(4):
                        for k in range(2):
                            mm = te.matmul(ps[:, 4 + m, :], four[:, k, P * m:P * (m + 1)],
                                           upair[:, 4 * hb:4 * hb + 4, k, :], start=(k == 0), stop=(k == 1))
                    mm.then_inc(s_uf, 1)
                for c in range(NC):
                    pe.wait_ge(s_yf, 2 * (c // 2) + 2)
                    for i in range(2):
                        for m in range(4):
                            mm = te.matmul(ps[:, c, SEQ * i:SEQ * (i + 1)], yf[:, m, 2 * c + i, :], finv[:, m, :],
                                           start=(m == 0), stop=(m == 3))
                    mm.then_inc(s_y, 1)
                for c in range(NC):
                    pe.wait_ge(s_yT, c + 1)
                    for i in range(CT):
                        t = CT * c + i
                        mm = te.matmul(ps[:, c, P * i:P * (i + 1)], yT[:, P * t:P * (t + 1)], wT[:, WOUT:WOUT + P],
                                       start=True, stop=True)
                    mm.then_inc(s_out, 1)
            if levels > 5:
                for c in range(NC):
                    x_transpose(5, c)
                pe.wait_ge(s_gmx, 1)
                te.transpose(ps[0:1, 4, 0:P], cols[:, 29:30], ident[:]).then_inc(s_gt, 1)
                pe.wait_ge(s_gm1, 1)
                te.matmul(ps[:, 5, 0:1], ones[0:1, :], cols[0:1, 36:37], start=True, stop=True)
                te.matmul(ps[:, 5, 1:2], ones[:], cols[:, 24:25], start=True, stop=True).then_inc(s_gb2, 1)
                pe.wait_ge(s_bwq, 1)
                for c in range(NC):
                    pe.wait_ge(s_xq, c + 1)
                    for i in range(CT):
                        t = CT * c + i
                        mm = te.matmul(ps[:, c, P * i:P * (i + 1)], xqT[:, P * t:P * (t + 1)], bwq, start=True, stop=True)
                    mm.then_inc(s_out, 1)
            if levels > 6:
                for c in range(NC):
                    x_transpose(6, c)
                for t in range(NT):
                    pe.wait_ge(s_xT, 6 * NC + t // CT + 1)
                    mm = te.matmul(ps[:, 7, N_HEADS3 * t:N_HEADS3 * (t + 1)], xTt(t), wT[:, W3IN + 640:W3IN + 644],
                                   start=True, stop=True)
                mm.then_inc(s_dtp, 1)
                for c in range(NC):
                    xcs = xT[:, CHUNK * c:CHUNK * (c + 1)]
                    for k in range(2):
                        if c:
                            pe.wait_ge(s_sz, 2 * (c - 1) + k + 1)
                        for i in range(2):
                            mm = te.matmul(ps[:, k, D_INNER * i:D_INNER * (i + 1)], xTt(CT * c + 2 * k + i),
                                           wT[:, W3IN:W3IN + D_INNER], start=True, stop=True)
                        mm.then_inc(s_z, 1)
                    for k in range(3):
                        if c:
                            pe.wait_ge(s_conv, 3 * (c - 1) + k + 1)
                        te.matmul(ps[:, 2 + k, :], wT[:, W3IN + P * (2 + k):W3IN + P * (3 + k)], xcs,
                                  start=True, stop=True).then_inc(s_xbc, 1)

                def x_tokens(b):
                    pe.wait_ge(s_xc, 4 * (b // 2) + 2)
                    if b:
                        pe.wait_ge(s_xs, b)
                    else:
                        pe.wait_ge(s_conv, 12)
                    for i in range(2):
                        for k in range(2):
                            t = 2 * b + i
                            mm = te.transpose(ps[:, 2, 256 * i + P * k:256 * i + P * (k + 1)],
                                              xc[:, k, P * t:P * (t + 1)], ident[:])
                    mm.then_inc(s_xsp, 1)

                def scores(b):
                    pe.wait_ge(s_xc, 4 * (b // 2) + 4)
                    if b:
                        pe.wait_ge(s_gts, b)
                    te.matmul(ps[:, 6, 0:256], xc[0:NSTATE, 2, SEQ * b:SEQ * b + P], cT[0:NSTATE, SEQ * b:SEQ * (b + 1)],
                              start=True, stop=True)
                    te.matmul(ps[:, 6, 256:384], xc[0:NSTATE, 2, SEQ * b + P:SEQ * (b + 1)],
                              cT[0:NSTATE, SEQ * b + P:SEQ * (b + 1)], start=True, stop=True).then_inc(s_gtp, 1)

                def decays(q):
                    b, h = divmod(q, N_HEADS3)
                    if h == 0:
                        x_tokens(b)
                        scores(b)
                        pe.wait_ge(s_lm, b + 1)
                    if q >= 2:
                        pe.wait_ge(s_le, q - 1)
                    bank = 4 + q % 2
                    te.matmul(ps[:, bank, 0:256], lmat[:, b % 2, 0, h, :], causal[:, 0:2, :],
                              start=True, stop=False, skip_group_check=True)
                    te.matmul(ps[:, bank, 128:256], d_a[:, 2 * b + 1, h:h + 1].broadcast_to([P, P]), tri[:],
                              start=False, stop=True, skip_group_check=True)
                    te.matmul(ps[:, bank, 256:384], lmat[:, b % 2, 1, h, :], tri[:],
                              start=False, stop=True, skip_group_check=True).then_inc(s_lp, 1)

                def y_transpose(b):
                    pe.wait_ge(s_yg, b + 1)
                    if b:
                        pe.wait_ge(s_ygT, b)
                    for k in range(2):
                        for i in range(2):
                            mm = te.transpose(ps[:, 3, SEQ * k + P * i:SEQ * k + P * (i + 1)],
                                              ygt[:, b % 2, i, P * k:P * (k + 1)], ident[:])
                    mm.then_inc(s_yt, 1)

                def out3(c):
                    pe.wait_ge(s_ygT, 2 * c + 2)
                    if c == 2:
                        pe.wait_ge(s_xs, BATCH)
                    for i in range(CT):
                        t = CT * c + i
                        for k in range(2):
                            mm = te.matmul(ps[:, c, P * i:P * (i + 1)], ygT[:, k, P * t:P * (t + 1)],
                                           wT[:, W3OUT + P * k:W3OUT + P * (k + 1)], start=(k == 0), stop=(k == 1))
                    mm.then_inc(s_out, 1)

                decays(0)
                decays(1)
                pe.wait_ge(s_nw, 1)
                for q in range(BATCH * N_HEADS3):
                    b, h = divmod(q, N_HEADS3)
                    if q + 2 < BATCH * N_HEADS3:
                        decays(q + 2)
                    if h == 0:
                        pe.wait_ge(s_xs, b + 1)
                        if b:
                            pe.wait_ge(s_yd, b)
                    pe.wait_ge(s_mm, q + 1)
                    m = mring[:, q % 4]
                    at = HEAD3 * h
                    te.matmul(ps[:, 7, at:at + HEAD3], m[:, 0, :], xs[:, 2 * b, h, :],
                              start=(h == 0), stop=True, skip_group_check=True)
                    te.matmul(ps[:, 7, 256 + at:256 + at + HEAD3], m[:, 1, :], xs[:, 2 * b, h, :],
                              start=False, stop=False, skip_group_check=True)
                    te.matmul(ps[:, 7, 256 + at:256 + at + HEAD3], m[:, 2, :], xs[:, 2 * b + 1, h, :],
                              start=False, stop=True, skip_group_check=True).then_inc(s_yq, 1)
                    if h == 3 and b:
                        y_transpose(b - 1)
                    if h == 1 and b in (3, 5, 7):
                        out3((b - 3) // 2)
                y_transpose(BATCH - 1)
                out3(3)
            if levels > 7:
                for c in range(NC):
                    x_transpose(7, c)
                for c in range(NC + 1):
                    if c < NC:
                        b = slice(2 * c, 2 * c + 2)
                        pe.wait_ge(s_xk, c + 1)
                        if c >= 2:
                            pe.wait_ge(s_kr, c - 1)
                        te.matmul(ps[:, 4 + c % 2, :], wT[:, WK:WK + P], xk[:, b, :], start=True, stop=True).then_inc(s_kp, 1)
                        pe.wait_ge(s_xr, c + 1)
                        if c >= 2:
                            pe.wait_ge(s_rs, c - 1)
                        xrf = xr.rearrange("p b t -> p (b t)")
                        for i in range(CT):
                            t = CT * c + i
                            mm = te.matmul(ps[:, 6 + c % 2, P * i:P * (i + 1)], xrf[:, P * t:P * (t + 1)],
                                           wT[:, WR:WR + P], start=True, stop=True)
                        mm.then_inc(s_rp, 1)
                    if c >= 1:
                        pe.wait_ge(s_ka2, c)
                        for i in range(CT):
                            t = CT * (c - 1) + i
                            mm = te.matmul(ps[:, c - 1, P * i:P * (i + 1)], kact[:, P * t:P * (t + 1)],
                                           wT[:, WV:WV + P], start=True, stop=True)
                        mm.then_inc(s_out, 1)


def kernel(**inputs):
    import concourse.bacc as _bacc
    from concourse.bass_utils import run_bass_kernel_spmd as _run

    nc = _bacc.Bacc("TRN2", target_bir_lowering=False, num_devices=1)
    arrays, aps = {}, {}
    for name in inputs:
        a = np.ascontiguousarray(inputs[name])
        arrays["in_" + name] = a
        aps[name] = nc.dram_tensor("in_" + name, a.shape, mybir.dt.from_np(a.dtype), kind="ExternalInput").ap()
    fwd, inv = fourier_constants()
    arrays["fourier_fwd"], arrays["fourier_inv"] = fwd, inv
    fwd_ap = nc.dram_tensor("fourier_fwd", fwd.shape, F32, kind="ExternalInput").ap()
    inv_ap = nc.dram_tensor("fourier_inv", inv.shape, F32, kind="ExternalInput").ap()
    out = nc.dram_tensor("out", (BATCH, SEQ, P), F32, kind="ExternalOutput").ap()
    build(nc, aps, fwd_ap, inv_ap, out)
    r = _run(nc, [arrays], core_ids=[0])
    return r.results[0]["out"]
```

```python
from contextlib import ExitStack

import numpy as np
import concourse.bass as bass
from concourse import mybir

ALU = mybir.AluOpType
ACT = mybir.ActivationFunctionType
AX = mybir.AxisListType
F32 = mybir.dt.float32

P = 128
BATCH = 8
SEQ = 256
NTOK = BATCH * SEQ
NT = NTOK // P
NC = 4
CT = NT // NC
CHUNK = CT * P
BANK = 512

HEADS0, HDIM0 = 16, 8
FFN0 = 512
HEADS1, HDIM1 = 16, 64
EXPERTS, EXP_HID, CAP = 8, 448, 80
NFB = 4
FULL = (NFB - 1) * P
TAIL = EXP_HID - FULL
SLOTS = BATCH * CAP
HALF_SLOTS = SLOTS // 2
ST = EXPERTS * CAP // P
NSTATE = 64
D_INNER, N_HEADS3, HEAD3 = 256, 4, 64
QCLIP = float(np.float32(128.0 - 1e-5))
LEVELS = 8


def fourier_constants():
    t = np.arange(SEQ, dtype=np.float64)[:, None]
    theta = (np.pi / 2 + 2 * np.pi * np.arange(SEQ, dtype=np.float64)[None, :]) / SEQ
    fwd = np.concatenate([np.cos(theta * t), np.sin(theta * t)], axis=1)
    inv = fwd.T / SEQ
    return fwd.astype(np.float32), np.ascontiguousarray(inv).astype(np.float32)


def build(nc, I, fwd_dram, inv_dram, out):
    with ExitStack() as ctx:
        def sb(name, shape, dt=F32):
            return ctx.enter_context(nc.sbuf_tensor(name, shape, dt))

        def sem(name):
            return ctx.enter_context(nc.semaphore(name))

        ps = ctx.enter_context(nc.psum_tensor("ps", [P, 8, BANK], F32))
        x_tok = sb("x_tok", [P, NT, P])
        xT = sb("xT", [P, NTOK])
        wT = sb("wT", [P, 3084])
        ident = sb("ident", [P, P])
        ones = sb("ones", [P, P])
        tri = sb("tri", [P, P])
        below = sb("below", [P, P])
        mask144 = sb("mask144", [P, 144])
        bias_tok = sb("bias_tok", [P, 3, P])
        bn = sb("bn", [P, NT, 6])
        mv = sb("mv", [P, NT, 2])
        rstd = sb("rstd", [P, NT])
        nmr = sb("nmr", [P, NT])
        mhalf = sb("mhalf", [P, NT])
        b1c = sb("b1c", [P, 4])
        iota_slot = sb("iota_slot", [P, CAP])
        iota_l = sb("iota_l", [P, P])
        tie = sb("tie", [P, EXPERTS])
        cols = sb("cols", [P, 40])
        A = sb("arena_a", [P, 20900])
        B = sb("arena_b", [P, 21700])

        def carve(arena, at, *dims):
            n = int(np.prod(dims))
            v = arena[:, at:at + n]
            if len(dims) == 1:
                return v
            names = ["a", "b", "c", "d"][:len(dims)]
            return v.rearrange(f"p ({' '.join(names)}) -> p {' '.join(names)}",
                               **{k: d for k, d in zip(names[1:], dims[1:])})

        WQKV, WP, WO1, GATE, WIN, WOUT, W3IN, W3OUT, WR, WK, WV = (
            0, 384, 512, 1536, 1544, 1672, 1800, 2444, 2700, 2828, 2956)

        s_x = [sem(f"x_loaded_{c}") for c in range(NC)]
        s_stored = sem("result_stored")
        s_w0 = sem("weights_l0_loaded")
        s_b0 = sem("biases_l0_loaded")
        s_wf = sem("weights_ffn0_loaded")
        s_w1 = sem("weights_l1_loaded")
        s_wr = sem("weights_rest_loaded")
        s_kw = sem("ssm_parameters_loaded")
        s_four = sem("fourier_loaded")
        s_cols = sem("columns_loaded")
        s_const = sem("constants_ready")
        N_CONST = 9
        N_COLS = 12
        s_pool = sem("pool_chain")
        s_dve = sem("dve_chain")
        s_actc = sem("act_chain")
        s_out = sem("layer_out_ready")
        s_xb = sem("bias_added_to_x")
        s_mv = sem("mean_var_ready")
        s_rstd = sem("rstd_ready")
        s_xtok = sem("x_tok_normalised")
        s_tp = sem("x_transposed_in_psum")
        s_xT = sem("xT_ready")
        s_wtp = sem("weights_transposed")
        s_wev = sem("weights_T_ready")

        w1s = carve(A, 10112, FFN0)
        w2s = carve(A, 10624, 4, P)
        l0w = carve(A, 9216, 4, P)
        l1w = carve(A, 4096, 3, 8, P)
        l1wo = carve(A, 4096 + 3072, 8 * P)

        gate_nat = carve(A, 11200, P)
        win_nat = carve(A, 11328, P)
        wout_nat = carve(A, 11456, P)
        w3in_nat = carve(A, 11584, 5, P)
        w3dt_nat = carve(A, 12224, P)
        w3out_nat = carve(A, 12352, 2 * P)
        wrkv_nat = carve(A, 12608, 3, P)
        N_WR = 9

        wgroups = [
            ([l0w[:, 0, :], l0w[:, 1, :], l0w[:, 2, :], l0w[:, 3, :]], WQKV, s_w0, 64),
            ([l1wo[:, P * k:P * (k + 1)] for k in range(4)], WO1, s_w1, 64),
            ([l1wo[:, P * k:P * (k + 1)] for k in range(4, 8)], WO1 + 512, s_w1, 64),
            ([gate_nat[0:EXPERTS, :], win_nat, wout_nat], GATE, s_wr, 16 * N_WR),
            ([w3in_nat[:, k, :] for k in range(4)], W3IN, s_wr, 16 * N_WR),
            ([w3in_nat[:, 4, :], w3dt_nat[0:N_HEADS3, :]], W3IN + 512, s_wr, 16 * N_WR),
            ([w3out_nat[:, 0:P], w3out_nat[:, P:2 * P], wrkv_nat[:, 0, :], wrkv_nat[:, 1, :]], W3OUT, s_wr, 16 * N_WR),
            ([wrkv_nat[:, 2, :]], WV, s_wr, 16 * N_WR),
        ]

        def weights_bank(k):
            return 4 if k == 0 else 4 + (k - 1) % 2

        x_in = I["L0_attn_x"].rearrange("b (t p) c -> p (b t) c", p=P)
        x_out = out.rearrange("b (t p) c -> p (b t) c", p=P)

        qkv = carve(B, 0, NT, 400)
        gmax = carve(B, 6400, NT, 32)
        gsum = carve(B, 6912, NT, 32)
        grec = carve(B, 7424, NT, 32)
        ctxs = carve(B, 7936, BATCH, 144)
        q0T = carve(B, 9088, NTOK)
        den0 = carve(B, 11136, NT, 16)
        o0 = carve(B, 11392, NT, P)
        o0T = carve(B, 13440, NTOK)
        bqkv = carve(A, 9728, 384)
        s_ones = sem("l0_ones_columns_set")
        s_qkv = sem("l0_qkv_in_psum")
        s_qmax = sem("l0_group_max")
        s_qsub = sem("l0_max_subtracted")
        s_qexp = sem("l0_exp_done")
        s_qsum = sem("l0_group_sum")
        s_qrec = sem("l0_softmax_reciprocal")
        s_den = sem("l0_denominator_reciprocal")
        s_qk = sem("l0_q_k_normalised")
        s_ctx = sem("l0_context_in_psum")
        s_ctxs = sem("l0_context_masked")
        s_qtp = sem("l0_q_transposed")
        s_q0T = sem("l0_qT_ready")
        s_num = sem("l0_numerator_in_psum")
        s_onum = sem("l0_out_divided")
        s_o0 = sem("l0_out_ready")
        s_otp = sem("l0_out_transposed")
        s_o0T = sem("l0_outT_ready")
        s_qevac = sem("l0_qkv_evacuated")

        h0T = carve(A, 0, 2, 4, CHUNK)
        s_h0 = sem("ffn0_hidden_in_psum")
        s_g0 = sem("ffn0_gelu_done")

        GB = 2
        l1A = carve(B, 10400, HEADS1, P)
        l1B = carve(B, 12448, HEADS1, P)
        gram = carve(B, 0, BATCH, P)
        gbuf = carve(B, 1024, 2, HEADS1, GB * P)
        l1M = carve(B, 9216, BATCH, P)
        s_ab = sem("l1_AB_in_psum")
        s_abs = sem("l1_AB_ready")
        s_g = sem("l1_gram_in_psum")
        s_gs = sem("l1_gram_ready")
        s_gb = sem("l1_gramB_in_psum")
        s_gba = sem("l1_gramB_evacuated_act")
        s_gbv = sem("l1_gramB_evacuated_dve")
        s_m = sem("l1_M_in_psum")
        s_ms = sem("l1_M_ready")

        kA, kB, kC, kE = (carve(A, 13000 + NSTATE * k, NSTATE) for k in range(4))
        kexp = carve(A, 11200, NSTATE, P)
        ka = carve(A, 19400, NSTATE)
        kg = carve(A, 19464, NSTATE)
        kW = carve(A, 19528, 2, NSTATE)
        kT = carve(A, 19656, 2, P)
        four = carve(B, 16384, 2, 2 * SEQ)
        finv = carve(B, 17408, 4, SEQ)
        ktok = carve(B, 18432, 2, P)
        kf = carve(B, 18688, 4, P)
        s_ke = sem("ssm_exp_minus_alog")
        s_ka = sem("ssm_a_W_ready")
        s_kg = sem("ssm_step128_ready")
        s_kacc = sem("ssm_kernel_terms_added")
        s_kprod = sem("ssm_products_ready")
        s_kexp = sem("ssm_exp_ready")
        s_kps = sem("ssm_kernel_in_psum")
        s_kt = sem("ssm_kernel_ready")
        s_kfp = sem("ssm_kernel_transformed")
        s_kf = sem("ssm_spectrum_ready")

        RW = 2 * EXP_HID + NFB * P
        ew13 = [carve(A, RW * r, 2 * EXP_HID) for r in range(2)]
        ew2 = [carve(A, RW * r + 2 * EXP_HID, NFB, P) for r in range(2)]
        disp = carve(A, 2816, 4, EXPERTS, CAP)
        comb = carve(A, 5376, 4, EXPERTS * CAP)
        eh = carve(A, 7936, 2, NFB, SLOTS)
        eoT = carve(A, 13440, BATCH, EXPERTS, CAP)
        xd = carve(B, 0, EXPERTS, BATCH, CAP)
        combT = carve(B, 5120, NT, ST * P)
        eo = carve(B, 0, BATCH, ST, P)
        esil = carve(B, 15360, 2, HALF_SLOTS)
        (r_mask, r_p2, r_oh, r_s, r_lg, r_pr, r_pos) = (carve(A, 10304 + 128 * k, NT, EXPERTS) for k in range(7))
        (r_mx, r_sum, r_rec, r_t) = (carve(A, 20000 + NT * k, NT) for k in range(4))
        s_lg = sem("moe_logits_in_psum")
        s_lsub = sem("moe_max_subtracted")
        s_lexp = sem("moe_exp_ready")
        s_mask = sem("moe_top2_mask_ready")
        s_cnt = sem("moe_counts_in_psum")
        s_pos = sem("moe_positions_ready")
        s_disp = sem("moe_dispatch_ready")
        s_comb = sem("moe_combine_weights_ready")
        s_ctp = sem("moe_combine_weights_transposed")
        s_cT = sem("moe_combT_ready")
        s_xdp = sem("moe_tokens_gathered")
        s_xda = sem("moe_xd_ready_experts_0_to_3")
        s_xdv = sem("moe_xd_ready_experts_4_to_7")
        s_eh1 = sem("moe_h1_in_psum")
        s_eh3 = sem("moe_h3_in_psum")
        s_sil = sem("moe_silu_ready")
        s_eh = sem("moe_hidden_ready")
        s_zero = sem("moe_half_blocks_padded")
        s_eop = sem("moe_expert_out_in_psum")
        s_eoT = sem("moe_expert_outT_ready")
        s_eot = sem("moe_expert_out_transposed")
        s_eo = sem("moe_expert_out_ready")

        u_tok = carve(B, 0, NT, P)
        yf = carve(B, 2048, 4, BATCH, P)
        prod = carve(B, 6144, 8, 2, 4, P)
        yT = carve(B, 14336, NTOK)
        bin_tok = carve(B, 19200, P)
        s_u = sem("ssm_u_in_psum")
        s_us = sem("ssm_u_ready")
        s_uf = sem("ssm_u_transformed")
        s_prod = sem("ssm_products_of_spectra")
        s_yf = sem("ssm_y_spectrum_ready")
        s_y = sem("ssm_y_in_psum")
        s_yT = sem("ssm_yT_ready")

        xh = carve(A, 0, NT, P)
        xnT = carve(A, 2048, NTOK)
        xqT = carve(A, 4096, NTOK)
        bw = carve(B, 19328, P)
        bwt = carve(B, 19456, P)
        bwq = carve(B, 19584, P)
        mv2 = carve(B, 19712, NT, 2)
        rstd2 = carve(B, 19744, NT)
        nmr2 = carve(B, 19760, NT)
        s_mv2 = sem("bit_mean_var_ready")
        s_rstd2 = sem("bit_rstd_ready")
        s_xh = sem("bit_x_normalised")
        s_gmx = sem("bit_max_of_partitions")
        s_gt = sem("bit_max_transposed")
        s_gm1 = sem("bit_max_of_all")
        s_bsum = sem("bit_weight_sums_ready")
        s_bws = sem("bit_weight_sum_spread")
        s_gb2 = sem("bit_max_spread")
        s_bwq = sem("bit_ternary_weights_ready")
        s_xq = sem("bit_x_quantised")

        xc = carve(B, 0, 3, NTOK)
        cT = carve(B, 6144, NTOK)
        xs = carve(B, 8192, NT, N_HEADS3, HEAD3)
        ygT = carve(B, 12288, 2, NTOK)
        ygt = carve(B, 16384, 2, 2, D_INNER)
        mring = carve(B, 17408, 3, 2, 2, P)
        gts = carve(B, 19776, 2, 2, P)
        (d_v, d_n, d_l, d_dt, d_a) = (carve(B, 20560 + 64 * k, NT, N_HEADS3) for k in range(5))
        ssv = carve(B, 21020, NT)
        rms = carve(B, 21040, NT)
        hd = carve(B, 21060, 3, N_HEADS3)
        dsk = carve(B, 21072, N_HEADS3)
        sqj = carve(B, 21080, 2, D_INNER)
        sz = carve(A, 6144, NT, D_INNER)
        xdd = carve(A, 10240, 2, 2, N_HEADS3, HEAD3)
        lmat = carve(A, 14400, 2, 2, N_HEADS3, P)
        xraw = carve(A, 0, 3, NTOK)
        state = carve(A, 16448, 2, D_INNER)
        b_tok = carve(A, 16960, 2, NSTATE)
        xend = carve(A, 17088, 2, N_HEADS3, HEAD3)
        yst = carve(A, 17600, 2, N_HEADS3, HEAD3)
        dexp = carve(A, 18112, 2, BATCH, N_HEADS3)
        s_hd = sem("ssd_head_constants_loaded")
        s_cum = sem("ssd_tile_decays_in_psum")
        s_dexp = sem("ssd_tile_decays_ready")
        s_xe = sem("ssd_xend_ready")
        s_stp = sem("ssd_state_in_psum")
        s_st = sem("ssd_state_ready")
        s_yip = sem("ssd_y_of_state_in_psum")
        s_yi = sem("ssd_y_of_state_ready")
        s_yd2 = sem("ssd_y_of_state_with_D")
        s_dtp = sem("ssd_dt_in_psum")
        s_sp1 = sem("ssd_minus_abs_ready")
        s_ea = sem("ssd_exp_alog")
        s_sp2 = sem("ssd_log_ready")
        s_a = sem("ssd_decay_ready")
        s_z = sem("ssd_z_in_psum")
        s_sz = sem("ssd_silu_z_ready")
        s_xbc = sem("ssd_xbc_in_psum")
        s_raw = sem("ssd_xbc_ready")
        s_conv = sem("ssd_conv_done")
        s_xc = sem("ssd_xc_ready")
        s_xsp = sem("ssd_x_transposed")
        s_xs = sem("ssd_xs_ready")
        s_gtp = sem("ssd_scores_in_psum")
        s_gts = sem("ssd_scores_ready")
        s_lp = sem("ssd_decays_in_psum")
        s_le = sem("ssd_decays_ready")
        s_mm = sem("ssd_decayed_scores_ready")
        s_yq = sem("ssd_y_in_psum")
        s_yd = sem("ssd_y_with_D_ready")
        s_yg = sem("ssd_gated_y_ready")
        s_sq = sem("ssd_squares_ready")
        s_ssv = sem("ssd_mean_square_ready")
        s_rms = sem("ssd_rms_ready")
        s_lm = sem("ssd_decay_matrices_ready")
        s_yt = sem("ssd_y_transposed")
        s_ygT = sem("ssd_yT_ready")
        s_nw = sem("ssd_norm_in_weights")

        xpad = carve(A, 12288, BATCH, SEQ + 1)
        xdif = carve(A, 14400, BATCH, SEQ)
        xr = carve(A, 16448, BATCH, SEQ)
        xk = carve(A, 18496, BATCH, SEQ)
        kact = carve(B, 0, NTOK)
        gate_r = carve(B, 2048, NT, P)
        s_pad = sem("mix_padding_set")
        s_dif = sem("mix_difference_ready")
        s_xr = sem("mix_xr_ready")
        s_xk = sem("mix_xk_ready")
        s_kp = sem("mix_k_in_psum")
        s_kr = sem("mix_relu_ready")
        s_ka2 = sem("mix_k_squared")
        s_rp = sem("mix_r_in_psum")
        s_rs = sem("mix_sigmoid_ready")
        s_ew = [sem(f"moe_weights_loaded_{r}") for r in range(2)]

        BURST = (2, 4, 5, 7)

        def normalised(layer, c):
            return 2 * (NC * layer + c + 1)

        def out3_bank(c):
            return 0 if c < 2 else c

        def expert_block(u):
            return (u // 2 - 1) % NFB

        def xbc_bank(n):
            return (4, 5, 6, 2, 3)[n % 5]

        def z_bank(n):
            return (0, 1, 7, 6, 2, 3, 4, 5)[n]

        def ssd_bank(b):
            return 1 if b % 2 else 7

        block = ctx.enter_context(nc.Block())

        @block.sync
        def _(sp):
            for c in range(NC):
                sp.dma_start(x_tok[:, CT * c:CT * (c + 1), :], x_in[:, CT * c:CT * (c + 1), :]).then_inc(s_x[c], 16)
                if c == 0:
                    for k, n in enumerate(["Wq", "Wk", "Wv", "Wp"]):
                        sp.dma_start(l0w[:, k, :], I["L0_attn_" + n]).then_inc(s_w0, 16)
                    for k, n in enumerate(["bq", "bk", "bv"]):
                        sp.dma_start(bqkv[:, P * k:P * (k + 1)], I["L0_attn_" + n].partition_broadcast(P)).then_inc(s_b0, 16)
                    sp.dma_start(bias_tok[:, 0, :], I["L0_attn_bp"].partition_broadcast(P)).then_inc(s_b0, 16)
            sp.dma_start(w1s[:], I["L0_ffn_w1"]).then_inc(s_wf, 16)
            sp.dma_start(w2s[:], I["L0_ffn_w2"].rearrange("(j p) e -> p j e", p=P)).then_inc(s_wf, 16)
            sp.dma_start(b1c[:], I["L0_ffn_b1"].rearrange("(j p) -> p j", p=P),
                         allow_slow_non_contiguous=True).then_inc(s_wf, 16)
            sp.dma_start(bias_tok[:, 1, :], I["L0_ffn_b2"].partition_broadcast(P)).then_inc(s_wf, 16)
            for k, n in enumerate(["W_q", "W_k", "W_v"]):
                sp.dma_start(l1w[:, k, :, :], I["L1_attn_" + n].rearrange("(j p) c -> p j c", p=P)).then_inc(s_w1, 16)
            sp.dma_start(l1wo, I["L1_attn_W_o"]).then_inc(s_w1, 16)
            for dst, src in [(gate_nat[0:EXPERTS, :], I["L1_ffn_gate_w"]), (win_nat, I["L2_attn_Win"]),
                             (wout_nat, I["L2_attn_Wout"]),
                             (w3in_nat, I["L3_attn_W_in"][0:640, :].rearrange("(k p) c -> p k c", p=P)),
                             (w3dt_nat[0:N_HEADS3, :], I["L3_attn_W_in"][640:644, :]),
                             (w3out_nat, I["L3_attn_W_out"]), (wrkv_nat[:, 0, :], I["L3_ffn_W_r"]),
                             (wrkv_nat[:, 1, :], I["L3_ffn_W_k"]), (wrkv_nat[:, 2, :], I["L3_ffn_W_v"])]:
                sp.dma_start(dst, src).then_inc(s_wr, 16)
            for dst, src in [(kA, I["L2_attn_A_log"]), (kB, I["L2_attn_B"]), (kC, I["L2_attn_C"]),
                             (cols[:, 0:1], I["L2_attn_dt"].rearrange("(p a) -> p a", a=1)),
                             (cols[:, 18:19], I["L2_attn_Dp"].rearrange("(p a) -> p a", a=1))]:
                sp.dma_start(dst, src).then_inc(s_kw, 16)
            sp.dma_start(bias_tok[:, 2, :], I["L2_attn_bout"].partition_broadcast(P)).then_inc(s_four, 16)
            sp.dma_start(four, fwd_dram.rearrange("(k p) f -> p k f", p=P)).then_inc(s_four, 16)
            sp.dma_start(finv, inv_dram.rearrange("(k p) t -> p k t", p=P)).then_inc(s_four, 16)
            for dst, src in [(bin_tok, I["L2_attn_bin_"].partition_broadcast(P)), (bw, I["L2_ffn_weight"]),
                             (hd[:, 0, :], I["L3_attn_A_log"].partition_broadcast(P)),
                             (hd[:, 1, :], I["L3_attn_dt_bias"].partition_broadcast(P)),
                             (dsk, I["L3_attn_D"].partition_broadcast(P))]:
                sp.dma_start(dst, src).then_inc(s_hd, 16)
            for col, name in [(1, "L2_ffn_ln_gamma"), (2, "L2_ffn_ln_beta"), (22, "L3_ffn_mu_r"), (23, "L3_ffn_mu_k")]:
                sp.dma_start(cols[:, col:col + 1], I[name].rearrange("(p a) -> p a", a=1)).then_inc(s_cols, 16)
            for k in range(3):
                sp.dma_start(cols[:, 3 + k:4 + k], I["L3_attn_conv_b"][P * k:P * (k + 1)].rearrange("(p a) -> p a", a=1)
                             ).then_inc(s_cols, 16)
                sp.dma_start(cols[:, 6 + 4 * k:10 + 4 * k],
                             I["L3_attn_conv_w"][P * k:P * (k + 1)].rearrange("p a j -> p (a j)")).then_inc(s_cols, 16)
            for k in range(2):
                sp.dma_start(cols[:, 20 + k:21 + k], I["L3_attn_norm_w"][P * k:P * (k + 1)].rearrange("(p a) -> p a", a=1)
                             ).then_inc(s_cols, 16)
            for e in range(EXPERTS):
                if e == 0:
                    sp.wait_ge(s_out, 2 * NC)
                    sp.wait_ge(s_ab, 8)
                if e >= 2:
                    sp.wait_ge(s_eop, 2 * (e - 1))
                w2 = I["L1_ffn_w2"][e]
                for dst, src in [(ew13[e % 2][:, 0:EXP_HID], I["L1_ffn_w1"][e]),
                                 (ew13[e % 2][:, EXP_HID:EXP_HID + TAIL], I["L1_ffn_w3"][e][:, FULL:EXP_HID]),
                                 (ew13[e % 2][:, EXP_HID + TAIL:2 * EXP_HID], I["L1_ffn_w3"][e][:, 0:FULL]),
                                 (ew2[e % 2][:, 0:NFB - 1], w2[0:FULL, :].rearrange("(j p) m -> p j m", p=P)),
                                 (ew2[e % 2][P - TAIL:P, NFB - 1, :], w2[FULL:EXP_HID, :])]:
                    sp.dma_start(dst, src).then_inc(s_ew[e % 2], 16)
            for c in range(NC):
                sp.wait_ge(s_xtok, normalised(LEVELS - 1, c))
                sp.dma_start(x_out[:, CT * c:CT * (c + 1), :], x_tok[:, CT * c:CT * (c + 1), :]).then_inc(s_stored, 16)
            sp.wait_ge(s_stored, 16 * NC)

        @block.gpsimd
        def _(pool):
            g = nc.gpsimd
            n = [0]

            def link(ins):
                n[0] += 1
                ins.then_inc(s_pool, 1)
                pool.wait_ge(s_pool, n[0])

            link(g.memset(ident[:], 0.0))
            g.affine_select(out=ident[:], in_=ident[:], compare_op=ALU.not_equal, fill=1.0, base=0,
                            pattern=[[-1, P]], channel_multiplier=1).then_inc(s_const, 1)
            g.memset(ones[:], 1.0).then_inc(s_const, 1)
            g.memset(qkv[:, :, 384:400], 1.0).then_inc(s_ones, 1)
            link(g.memset(mask144[:], 1.0))
            m1 = mask144[:, 0:P].rearrange("p (h e) -> p h e", e=HDIM0)
            m2 = mask144[:, P:144]
            link(g.affine_select(out=m1, in_=m1, compare_op=ALU.is_ge, fill=0.0, base=0,
                                 pattern=[[-HDIM0, HEADS0], [0, HDIM0]], channel_multiplier=1))
            link(g.affine_select(out=m1, in_=m1, compare_op=ALU.is_ge, fill=0.0, base=HDIM0 - 1,
                                 pattern=[[HDIM0, HEADS0], [0, HDIM0]], channel_multiplier=-1))
            link(g.affine_select(out=m2, in_=m2, compare_op=ALU.is_ge, fill=0.0, base=0,
                                 pattern=[[-HDIM0, HEADS0]], channel_multiplier=1))
            g.affine_select(out=m2, in_=m2, compare_op=ALU.is_ge, fill=0.0, base=HDIM0 - 1,
                            pattern=[[HDIM0, HEADS0]], channel_multiplier=-1).then_inc(s_const, 1)
            g.memset(mhalf[:], -0.5).then_inc(s_const, 1)
            link(g.memset(tri[:], 1.0))
            g.affine_select(out=tri[:], in_=tri[:], compare_op=ALU.is_ge, fill=0.0, base=0,
                            pattern=[[1, P]], channel_multiplier=-1).then_inc(s_const, 1)

            g.iota(iota_slot[:], pattern=[[1, CAP]], base=1, channel_multiplier=0,
                   allow_small_or_imprecise_dtypes=True).then_inc(s_const, 1)
            g.iota(iota_l[:], pattern=[[1, P]], base=0, channel_multiplier=0,
                   allow_small_or_imprecise_dtypes=True).then_inc(s_const, 1)
            g.iota(tie[:], pattern=[[-1, EXPERTS]], base=EXPERTS, channel_multiplier=0,
                   allow_small_or_imprecise_dtypes=True).then_inc(s_const, 1)
            link(g.memset(below[:], 1.0))
            g.affine_select(out=below[:], in_=below[:], compare_op=ALU.is_gt, fill=0.0, base=0,
                            pattern=[[-1, P]], channel_multiplier=1).then_inc(s_const, 1)
            pool.wait_ge(s_const, N_CONST)

            def add_bias(level, c, slot):
                pool.wait_ge(s_tp, NC * level + c + 1)
                xc = x_tok[:, CT * c:CT * (c + 1), :]
                g.tensor_tensor(xc, xc, bias_tok[:, slot, :].unsqueeze(1).broadcast_to([P, CT, P]),
                                ALU.add).then_inc(s_xb, 1)

            def normaliser(stats, scale, offset, c, eps):
                t = slice(CT * c, CT * (c + 1))
                g.tensor_scalar(offset[:, t], stats[:, t, 0], -1.0, None, ALU.mult)
                link(g.tensor_scalar(scale[:, t], stats[:, t, 1], eps, None, ALU.add))
                link(g.tensor_tensor(scale[:, t], scale[:, t], mhalf[:, t], ALU.pow))
                return g.tensor_tensor(offset[:, t], offset[:, t], scale[:, t], ALU.mult)

            def ln_rstd(layer, c):
                pool.wait_ge(s_mv, NC * layer + c + 1)
                if layer:
                    pool.wait_ge(s_xtok, normalised(layer - 1, c))
                normaliser(mv, rstd, nmr, c, 1e-5).then_inc(s_rstd, 1)

            def mean_square_pow(c):
                t = slice(CT * c, CT * (c + 1))
                pool.wait_ge(s_ssv, c + 1)
                g.tensor_tensor(rms[:, t], ssv[:, t], mhalf[:, t], ALU.pow).then_inc(s_rms, 1)

            pool.wait_ge(s_b0, 64)
            for s in range(BATCH + 8):
                if s < BATCH:
                    b = s
                    t = slice(2 * b, 2 * b + 2)
                    qk = qkv[:, t, 0:256].rearrange("p t (g e) -> p t g e", e=HDIM0)
                    pool.wait_ge(s_qmax, b + 1)
                    g.tensor_tensor(qk, qk, gmax[:, t, :].unsqueeze(3).broadcast_to([P, 2, 32, HDIM0]),
                                    ALU.subtract).then_inc(s_qsub, 1)
                if 1 <= s <= BATCH:
                    b = s - 1
                    t = slice(2 * b, 2 * b + 2)
                    qk = qkv[:, t, 0:256].rearrange("p t (g e) -> p t g e", e=HDIM0)
                    pool.wait_ge(s_qrec, b + 1)
                    g.tensor_tensor(qk, qk, grec[:, t, :].unsqueeze(3).broadcast_to([P, 2, 32, HDIM0]),
                                    ALU.mult).then_inc(s_qk, 1)
                if 4 <= s < BATCH + 4:
                    b = s - 4
                    t = slice(2 * b, 2 * b + 2)
                    pool.wait_ge(s_onum, b + 1)
                    g.tensor_tensor(o0[:, t, :], o0[:, t, :], qkv[:, t, 0:P], ALU.add).then_inc(s_o0, 1)
                if 2 <= s < 2 + NC:
                    add_bias(0, s - 2, 0)
                if s in (8, 11, 12, 14):
                    ln_rstd(0, (s - 8) // 2)
            pool.wait_ge(s_wf, 64)
            pool.wait_ge(s_wtp, len(wgroups))
            pool.wait_ge(s_ka, 1)
            for c in range(NC):
                add_bias(1, c, 1)
                if c >= 2:
                    ln_rstd(1, c - 2)
                q = slice(16 * c, 16 * c + 16)
                g.tensor_tensor(kexp[:, q, :], iota_l[:].unsqueeze(1).broadcast_to([P, 16, P]),
                                ka[:, q].unsqueeze(2).broadcast_to([P, 16, P]), ALU.mult).then_inc(s_kprod, 1)
            ln_rstd(1, 2)
            ln_rstd(1, 3)
            for c in range(NC):
                ln_rstd(2, c)
            for r in range(2):
                g.memset(ew2[r][0:P - TAIL, NFB - 1, :], 0.0).then_inc(s_zero, 1)
            for t in range(NT):
                if t == 4:
                    pool.wait_ge(s_kps, 1)
                    for r in range(2):
                        g.memset(eh[0:P - TAIL, r, NFB - 1, :], 0.0).then_inc(s_zero, 1)
                pool.wait_ge(s_disp, t + 1)
                if t >= 4:
                    pool.wait_ge(s_ctp, t - 3)
                g.tensor_tensor(comb[:, t % 4].rearrange("p (e s) -> p e s", s=CAP), disp[:, t % 4],
                                r_pr[:, t, :].unsqueeze(2).broadcast_to([P, EXPERTS, CAP]),
                                ALU.mult).then_inc(s_comb, 1)
            for c in range(NC):
                ln_rstd(3, c)
            pool.wait_ge(s_four, 48)
            for c in range(NC):
                add_bias(4, c, 2)
            for hb in range(2):
                bs = slice(4 * hb, 4 * hb + 4)
                for k, op in enumerate([ALU.subtract, ALU.add]):
                    pool.wait_ge(s_prod, 4 * hb + k + 3)
                    g.tensor_tensor(yf[:, 2 * k:2 * k + 2, bs, :], prod[:, 4 * hb + k], prod[:, 4 * hb + k + 2],
                                    op).then_inc(s_yf, 1)
            for half in range(2):
                for c in (2 * half, 2 * half + 1):
                    ln_rstd(4, c)
                for c in (2 * half, 2 * half + 1):
                    pool.wait_ge(s_mv2, c + 1)
                    normaliser(mv2, rstd2, nmr2, c, 1e-3).then_inc(s_rstd2, 1)
            for c in range(NC):
                ln_rstd(5, c)
            def decay_matrices(b):
                if b >= 2:
                    pool.wait_ge(s_lp, 2 * (b - 1))
                g.tensor_tensor(lmat[:, b % 2], below[:].unsqueeze(1).unsqueeze(1).broadcast_to([P, 2, N_HEADS3, P]),
                                d_a[:, 2 * b:2 * b + 2, :].unsqueeze(3).broadcast_to([P, 2, N_HEADS3, P]),
                                ALU.mult).then_inc(s_lm, 1)

            pool.wait_ge(s_a, 1)
            decay_matrices(0)
            decay_matrices(1)
            g.memset(xpad[:, :, 0:1], 0.0).then_inc(s_pad, 1)

            def decayed_x(b):
                pool.wait_ge(s_xs, b + 1)
                if b >= 2:
                    pool.wait_ge(s_stp, b - 1)
                g.tensor_tensor(xend[:, b % 2], xs[:, 2 * b, :, :],
                                dexp[:, 0, b, :].unsqueeze(2).broadcast_to([P, N_HEADS3, HEAD3]),
                                ALU.mult).then_inc(s_xe, 1)

            pool.wait_ge(s_dexp, 1)
            decayed_x(0)
            for b in range(BATCH):
                if b + 2 < BATCH:
                    decay_matrices(b + 2)
                pool.wait_ge(s_yi, b + 1)
                pool.wait_ge(s_xs, b + 1)
                second = xdd[:, b % 2, 1]
                g.tensor_tensor(second, second, yst[:, b % 2], ALU.add).then_inc(s_yd2, 1)
                if b == 7:
                    ln_rstd(6, 1)
                if b + 1 < BATCH:
                    decayed_x(b + 1)
                pool.wait_ge(s_yd, b + 1)
                pool.wait_ge(s_sz, 2 * NC)
                g.tensor_tensor(ygt[:, b % 2], ygt[:, b % 2], sz[:, 2 * b:2 * b + 2, :], ALU.mult).then_inc(s_yg, 1)
                if b in (2, 4, 6):
                    mean_square_pow(b // 2 - 1)
                if b == 5:
                    ln_rstd(6, 0)

            def difference(c):
                b = slice(2 * c, 2 * c + 2)
                pool.wait_ge(s_xT, 7 * NC + c + 1)
                pool.wait_ge(s_pad, 1)
                g.tensor_tensor(xdif[:, b, :], xpad[:, b, 1:SEQ + 1], xpad[:, b, 0:SEQ],
                                ALU.subtract).then_inc(s_dif, 1)

            difference(0)
            ln_rstd(6, 2)
            mean_square_pow(3)
            difference(1)
            ln_rstd(6, 3)
            difference(2)
            difference(3)
            for c in range(NC):
                ln_rstd(7, c)

        @block.scalar
        def _(act):
            a = nc.scalar

            def weights_out(k):
                act.wait_ge(s_wtp, k + 1)
                blocks, col, _, _ = wgroups[k]
                w = sum(src.shape[0] for src in blocks)
                a.activation(wT[:, col:col + w], ps[:, weights_bank(k), 0:w], ACT.Copy).then_inc(s_wev, 1)

            def pair_of_banks(bank):
                return ps[:, bank:bank + 2, :].rearrange("p k c -> p (k c)")[:, 0:ST * P]

            def xT_out(level, c):
                act.wait_ge(s_tp, NC * level + c + 1)
                a.activation(xT[:, CHUNK * c:CHUNK * (c + 1)], ps[:, c, :], ACT.Copy).then_inc(s_xT, 1)

            def normalise(dst, scale, offset, c, signal):
                last = c == NC - 1
                for i in range(CT * c, CT * (c + 1) - (2 if last else 0)):
                    ins = a.activation(dst[:, i, :], x_tok[:, i, :], ACT.Identity, bias=offset[:, i:i + 1],
                                       scale=scale[:, i:i + 1])
                ins.then_inc(signal, 1 if last else 2)

            def ln_apply(layer, c):
                act.wait_ge(s_rstd, NC * layer + c + 1)
                normalise(x_tok, rstd, nmr, c, s_xtok)

            weights_out(0)
            xT_out(0, 0)
            for s in range(BATCH + 5):
                if s + 1 < NC:
                    xT_out(0, s + 1)
                if s < BATCH:
                    act.wait_ge(s_qsub, s + 1)
                    e = qkv[:, 2 * s:2 * s + 2, 0:256]
                    a.activation(e, e, ACT.Exp).then_inc(s_qexp, 1)
                if 2 <= s < BATCH + 2:
                    b = s - 2
                    act.wait_ge(s_qtp, b + 1)
                    a.activation(q0T[:, 256 * b:256 * (b + 1)], ps[:, 7, 0:256], ACT.Copy).then_inc(s_q0T, 1)
                if 5 <= s < BATCH + 5:
                    b = s - 5
                    act.wait_ge(s_otp, b + 1)
                    a.activation(o0T[:, 256 * b:256 * (b + 1)], ps[:, 2, 0:256], ACT.Copy).then_inc(s_o0T, 1)
                if s == BATCH:
                    act.wait_ge(s_kw, 16 * 5)
                    a.activation(kE, kA, ACT.Exp, scale=-1.0).then_inc(s_ke, 1)
                if s >= BATCH:
                    for k in (2 * (s - BATCH) + 1, 2 * (s - BATCH) + 2):
                        if k < len(wgroups):
                            weights_out(k)
            xT_out(1, 0)
            for k in range(4):
                act.wait_ge(s_ab, k + 1)
                a.activation(l1A[:, 4 * k:4 * k + 4, :], ps[:, 4 + k, :].rearrange("p (h c) -> p h c", c=P),
                             ACT.Copy).then_inc(s_abs, 1)
            for c in range(NC):
                if c:
                    xT_out(1, c)
                if c >= 2:
                    act.wait_ge(s_out, NC + c - 1)
                for j in range(4):
                    act.wait_ge(s_h0, 4 * c + j + 1)
                    a.activation(h0T[:, c % 2, j, :], ps[:, 4 + j, :], ACT.Gelu,
                                 bias=b1c[:, j:j + 1]).then_inc(s_g0, 1)
            for k in range(4):
                act.wait_ge(s_ab, 4 + k + 1)
                a.activation(l1B[:, 4 * k:4 * k + 4, :], ps[:, 4 + k, :].rearrange("p (h c) -> p h c", c=P),
                             ACT.Copy).then_inc(s_abs, 1)
            def kernel_exp(k):
                q = slice(16 * k, 16 * k + 16)
                act.wait_ge(s_kprod, k + 1)
                a.activation(kexp[:, q, :], kexp[:, q, :], ACT.Exp).then_inc(s_kexp, 1)

            for c in range(NC):
                xT_out(2, c)
            for k in range(2):
                act.wait_ge(s_g, k + 1)
                a.activation(gram[:, 4 * k:4 * k + 4, :], ps[:, 4 + k, :].rearrange("p (h c) -> p h c", c=P),
                             ACT.Copy).then_inc(s_gs, 1)
            for g in range(BATCH // GB + 1):
                if g < BATCH // GB:
                    for b in range(GB):
                        for j in (0, 2):
                            if g >= 2:
                                act.wait_ge(s_m, g - 1)
                            act.wait_ge(s_gb, (GB * g + b) * 4 + j + 1)
                            a.activation(gbuf[:, g % 2, 4 * j:4 * j + 4, P * b:P * (b + 1)],
                                         ps[:, 4 + j, :].rearrange("p (h c) -> p h c", c=P),
                                         ACT.Copy).then_inc(s_gba, 1)
                        if g < 2:
                            kernel_exp(GB * g + b)
                        if g == 0 and b == 0:
                            act.wait_ge(s_ka, 1)
                            a.activation(kg, ka, ACT.Exp, scale=float(P)).then_inc(s_kg, 1)
                if g >= 1:
                    q = g - 1
                    act.wait_ge(s_m, q + 1)
                    a.activation(l1M[:, GB * q:GB * (q + 1), :],
                                 ps[:, q % 4, 0:GB * P].rearrange("p (b c) -> p b c", c=P),
                                 ACT.Copy, scale=float(HDIM1) ** -0.5).then_inc(s_ms, 1)
            for c in range(NC):
                ln_apply(2, c)
                if c:
                    xT_out(3, c - 1)
            xT_out(3, NC - 1)
            act.wait_ge(s_lsub, 1)
            a.activation(r_pr, r_lg, ACT.Exp).then_inc(s_lexp, 1)
            def combT_out(t):
                act.wait_ge(s_ctp, t + 1)
                a.activation(combT[:, t, :], pair_of_banks(2 * (t % 2)), ACT.Copy).then_inc(s_cT, 1)

            for b in range(BATCH):
                act.wait_ge(s_xdp, 2 * b + 1)
                a.activation(xd[:, 0:4, b, :], ps[:, 4 + 2 * (b % 2), 0:HALF_SLOTS].rearrange("p (e s) -> p e s", s=CAP),
                             ACT.Copy).then_inc(s_xda, 1)
                if b == 0:
                    act.wait_ge(s_kfp, 1)
                    a.activation(kf, ps[:, 6, :].rearrange("p (m c) -> p m c", c=P), ACT.Copy).then_inc(s_kf, 1)
                if b:
                    combT_out(2 * b - 2)
                    combT_out(2 * b - 1)

            def outT(e):
                for hb in range(2):
                    act.wait_ge(s_eop, 2 * e + hb + 1)
                    a.activation(eoT[:, 4 * hb:4 * hb + 4, e, :],
                                 ps[:, 2 * (e % 2) + hb, 0:HALF_SLOTS].rearrange("p (b s) -> p b s", s=CAP),
                                 ACT.Copy).then_inc(s_eoT, 1)

            for n in range(EXPERTS * 2 * NFB):
                e, u = divmod(n, 2 * NFB)
                act.wait_ge(s_eh1, n + 1)
                if n >= 2:
                    act.wait_ge(s_eh, n - 1)
                full = u >= 2
                src, dst = (slice(0, P), slice(0, P)) if full else (slice(0, TAIL), slice(P - TAIL, P))
                a.activation(esil[dst, n % 2, :], ps[src, 4 + n % 2, 0:HALF_SLOTS], ACT.Silu).then_inc(s_sil, 1)
                if e == 0 and u == 1:
                    combT_out(NT - 2)
                    combT_out(NT - 1)
                if e and u == 2:
                    outT(e - 1)
            outT(EXPERTS - 1)
            for b in range(BATCH):
                act.wait_ge(s_eot, b + 1)
                a.activation(eo[:, b].rearrange("p k c -> p (k c)"), pair_of_banks(4 + 2 * (b % 2)),
                             ACT.Copy).then_inc(s_eo, 1)
            for c in range(NC):
                xT_out(4, c)
            def yT2_out(c):
                act.wait_ge(s_y, c + 1)
                a.activation(yT[:, CHUNK * c:CHUNK * (c + 1)], ps[:, c, :], ACT.Copy).then_inc(s_yT, 1)

            def bit_apply(c):
                act.wait_ge(s_rstd2, c + 1)
                normalise(xh, rstd2, nmr2, c, s_xh)

            yT2_out(0)
            yT2_out(1)
            ln_apply(4, 0)
            yT2_out(2)
            ln_apply(4, 1)
            yT2_out(3)
            bit_apply(0)
            bit_apply(1)
            ln_apply(4, 2)
            ln_apply(4, 3)
            act.wait_ge(s_cols, 16 * N_COLS)

            def xnT_out(c):
                act.wait_ge(s_tp, NC * 5 + c + 1)
                a.activation(xnT[:, CHUNK * c:CHUNK * (c + 1)], ps[:, c, :], ACT.Identity,
                             bias=cols[:, 2:3], scale=cols[:, 1:2]).then_inc(s_xT, 1)

            xnT_out(0)
            xnT_out(1)
            bit_apply(2)
            bit_apply(3)
            xnT_out(2)
            xnT_out(3)
            for c in range(NC):
                ln_apply(5, c)
            act.wait_ge(s_hd, 80)
            a.activation(hd[:, 2, :], hd[:, 0, :], ACT.Exp).then_inc(s_ea, 1)
            for c in range(NC):
                xT_out(6, c)

            def z_out(c):
                for k in range(2):
                    act.wait_ge(s_z, 2 * c + k + 1)
                    i = CT * c + 2 * k
                    a.activation(sz[:, i:i + 2, :], ps[:, z_bank(2 * c + k), :].rearrange("p (t c) -> p t c", t=2),
                                 ACT.Silu).then_inc(s_sz, 1)

            def convolved(c):
                t = slice(CHUNK * c, CHUNK * (c + 1))
                for k in range(2):
                    act.wait_ge(s_conv, 3 * c + k + 1)
                    a.activation(xc[:, k, t], xc[:, k, t], ACT.Silu).then_inc(s_xc, 1)
                act.wait_ge(s_conv, 3 * c + 3)
                a.activation(xc[0:NSTATE, 2, t], xc[0:NSTATE, 2, t], ACT.Silu).then_inc(s_xc, 1)
                a.activation(cT[0:NSTATE, t], xc[NSTATE:P, 2, t], ACT.Silu).then_inc(s_xc, 1)

            for c in range(NC):
                t = slice(CHUNK * c, CHUNK * (c + 1))
                for k in range(3):
                    n = 3 * c + k
                    act.wait_ge(s_xbc, n + 1)
                    a.activation(xraw[:, k, t], ps[:, xbc_bank(n), :], ACT.Copy).then_inc(s_raw, 1)
                if c == 0:
                    act.wait_ge(s_sp1, 1)
                    a.activation(d_n, d_n, ACT.Exp).then_inc(s_actc, 1)
                    act.wait_ge(s_actc, 1)
                    a.activation(d_l, d_n, ACT.Ln, bias=1.0).then_inc(s_sp2, 1)
                if c == 1:
                    act.wait_ge(s_cum, 1)
                    a.activation(dexp, ps[:, 7, 64:128].rearrange("p (k b h) -> p k b h", k=2, b=BATCH),
                                 ACT.Exp).then_inc(s_dexp, 1)
            convolved(0)
            for c in range(NC):
                z_out(c)
            convolved(1)
            convolved(2)

            def squares(b):
                act.wait_ge(s_yg, b + 1)
                if b:
                    act.wait_ge(s_sq, b)
                for i in range(2):
                    t = 2 * b + i
                    ins = a.activation(sqj[:, i], ygt[:, b % 2, i, :], ACT.Square, accum_out=ssv[:, t:t + 1])
                ins.then_inc(s_sq, 1)

            def yT_out(b):
                act.wait_ge(s_yt, b + 1)
                a.activation(ygT[:, :, SEQ * b:SEQ * (b + 1)], ps[:, 3, :].rearrange("p (k t) -> p k t", k=2),
                             ACT.Copy).then_inc(s_ygT, 1)

            def decays_out(p):
                act.wait_ge(s_lp, p + 1)
                if p >= 3:
                    act.wait_ge(s_yq, p - 2)
                a.activation(mring[:, p % 3], ps[:, 4 + p % 2, :].rearrange("p (h k t) -> p h k t", h=2, k=2),
                             ACT.Exp).then_inc(s_le, 1)

            decays_out(0)
            decays_out(1)
            for p in range(2 * BATCH):
                b, half = divmod(p, 2)
                if half == 0:
                    act.wait_ge(s_stp, b + 1)
                    a.activation(state[0:NSTATE, b % 2], ps[0:NSTATE, 6, 0:D_INNER], ACT.Copy).then_inc(s_st, 1)
                if p + 2 < 2 * BATCH:
                    decays_out(p + 2)
                if p == 8:
                    convolved(3)
                if half and b:
                    squares(b - 1)
                if half == 0 and b >= 2:
                    yT_out(b - 2)

            def padded_out(c):
                act.wait_ge(s_tp, NC * 7 + c + 1)
                a.activation(xpad[:, 2 * c:2 * c + 2, 1:SEQ + 1], ps[:, c, :].rearrange("p (b t) -> p b t", b=2),
                             ACT.Copy).then_inc(s_xT, 1)

            def relu_sigmoid(c):
                act.wait_ge(s_kp, c + 1)
                a.activation(kact[:, CHUNK * c:CHUNK * (c + 1)], ps[:, 4 + c % 2, :], ACT.Relu).then_inc(s_kr, 1)
                act.wait_ge(s_rp, c + 1)
                a.activation(gate_r[:, CT * c:CT * (c + 1), :], ps[:, 6 + c % 2, :].rearrange("p (t c) -> p t c", c=P),
                             ACT.Sigmoid).then_inc(s_rs, 1)

            yT_out(BATCH - 2)
            padded_out(0)
            squares(BATCH - 1)
            yT_out(BATCH - 1)
            padded_out(1)
            relu_sigmoid(0)
            relu_sigmoid(1)
            padded_out(2)
            padded_out(3)
            relu_sigmoid(2)
            ln_apply(7, 0)
            relu_sigmoid(3)
            for c in range(1, NC):
                ln_apply(7, c)

        @block.vector
        def _(dve):
            v = nc.vector
            n = [0]

            def link(ins):
                n[0] += 1
                ins.then_inc(s_dve, 1)
                dve.wait_ge(s_dve, n[0])

            def ln_stats(layer, c, bias_count=None):
                t = slice(CT * c, CT * (c + 1))
                if bias_count is not None:
                    dve.wait_ge(s_xb, bias_count)
                dve.wait_ge(s_out, NC * layer + c + 1)
                out = ps[:, out3_bank(c) if layer == 6 else c, :].rearrange("p (t c) -> p t c", c=P)
                xc_tok = x_tok[:, t, :]
                if layer == 5:
                    link(v.scalar_tensor_tensor(out=xc_tok, in0=out, scalar=cols[:, 38:39], in1=xc_tok,
                                                op0=ALU.mult, op1=ALU.add))
                elif layer == 6:
                    dve.wait_ge(s_rms, c + 1)
                    for i in range(CT):
                        k = CT * c + i
                        ins = v.scalar_tensor_tensor(out=x_tok[:, k, :], in0=out[:, i, :], scalar=rms[:, k:k + 1],
                                                     in1=x_tok[:, k, :], op0=ALU.mult, op1=ALU.add)
                    link(ins)
                elif layer == 7:
                    dve.wait_ge(s_rs, c + 1)
                    link(v.tensor_tensor(gate_r[:, t, :], out, gate_r[:, t, :], ALU.mult))
                    link(v.tensor_tensor(xc_tok, gate_r[:, t, :], xc_tok, ALU.add))
                else:
                    link(v.tensor_tensor(xc_tok, out, xc_tok, ALU.add))
                for i in range(CT * c, CT * (c + 1)):
                    ins = v.bn_stats(bn[:, i, :], x_tok[:, i, :])
                link(ins)
                for i in range(CT * c, CT * (c + 1)):
                    ins = v.bn_aggr(mv[:, i, :], bn[:, i, :])
                ins.then_inc(s_mv, 1)

            def normalise(dst, stats, scale, tiles):
                for i in tiles:
                    ins = v.tensor_scalar(dst[:, i, :], x_tok[:, i, :], stats[:, i, 0:1], scale[:, i:i + 1],
                                          ALU.subtract, ALU.mult)
                return ins

            def ln_apply(layer, c):
                dve.wait_ge(s_rstd, NC * layer + c + 1)
                normalise(x_tok, mv, rstd, range(CT * c, CT * (c + 1))).then_inc(s_xtok, 2)

            def layer_norm(layer, bias_from=None):
                for c in range(NC):
                    ln_stats(layer, c, None if bias_from is None else bias_from + c + 1)
                    if c and layer not in BURST:
                        ln_apply(layer, c - 1)
                if layer in BURST:
                    dve.wait_ge(s_rstd, NC * layer + NC)
                    normalise(x_tok, mv, rstd, (NT - 2, NT - 1)).then_inc(s_xtok, 1)
                else:
                    ln_apply(layer, NC - 1)

            def square_k(c):
                t = slice(CHUNK * c, CHUNK * (c + 1))
                dve.wait_ge(s_kr, c + 1)
                v.tensor_tensor(kact[:, t], kact[:, t], kact[:, t], ALU.mult).then_inc(s_ka2, 1)

            dve.wait_ge(s_b0, 64)
            dve.wait_ge(s_const, 3)
            for s in range(BATCH + 8):
                if s < BATCH:
                    b = s
                    t = slice(2 * b, 2 * b + 2)
                    dve.wait_ge(s_qkv, b + 1)
                    ins = v.tensor_tensor(qkv[:, t, 0:384], ps[:, 4:6, 0:384],
                                          bqkv.unsqueeze(1).broadcast_to([P, 2, 384]), ALU.add)
                    ins.then_inc(s_qevac, 1)
                if 1 <= s <= BATCH:
                    b = s - 1
                    t = slice(2 * b, 2 * b + 2)
                    dve.wait_ge(s_qexp, b + 1)
                    v.tensor_reduce(gsum[:, t, :], qkv[:, t, 0:256].rearrange("p t (g e) -> p t g e", e=HDIM0),
                                    AX.X, ALU.add).then_inc(s_qsum, 1)
                if s < BATCH:
                    b = s
                    t = slice(2 * b, 2 * b + 2)
                    dve.wait_ge(s_qevac, b + 1)
                    v.tensor_reduce(gmax[:, t, :], qkv[:, t, 0:256].rearrange("p t (g e) -> p t g e", e=HDIM0),
                                    AX.X, ALU.max).then_inc(s_qmax, 1)
                if 1 <= s <= BATCH:
                    b = s - 1
                    t = slice(2 * b, 2 * b + 2)
                    dve.wait_ge(s_qsum, b + 1)
                    v.reciprocal(grec[:, t, :], gsum[:, t, :]).then_inc(s_qrec, 1)
                if 3 <= s < BATCH + 3:
                    b = s - 3
                    dve.wait_ge(s_num, b + 1)
                    nd = ps[:, 3, 0:288].rearrange("p (t c) -> p t c", c=144)
                    v.reciprocal(den0[:, 2 * b:2 * b + 2, :], nd[:, :, P:144]).then_inc(s_den, 1)
                if 2 <= s < BATCH + 2:
                    b = s - 2
                    dve.wait_ge(s_ctx, b + 1)
                    v.tensor_tensor(ctxs[:, b, :], ps[:, 6, 0:144], mask144[:], ALU.mult).then_inc(s_ctxs, 1)
                if 3 <= s < BATCH + 3:
                    b = s - 3
                    t = slice(2 * b, 2 * b + 2)
                    dve.wait_ge(s_den, b + 1)
                    v.tensor_tensor(o0[:, t, :].rearrange("p t (h e) -> p t h e", e=HDIM0),
                                    nd[:, :, 0:P].rearrange("p t (h e) -> p t h e", e=HDIM0),
                                    den0[:, t, :].unsqueeze(3).broadcast_to([P, 2, HEADS0, HDIM0]),
                                    ALU.mult).then_inc(s_onum, 1)
                if s in (8, 10, 11, 13):
                    c = {8: 0, 10: 1, 11: 2, 13: 3}[s]
                    ln_stats(0, c, c + 1)
                if s in (9, 12, 14, 15):
                    ln_apply(0, {9: 0, 12: 1, 14: 2, 15: 3}[s])
                if s == 11:
                    dve.wait_ge(s_kw, 16 * 5)
                    dve.wait_ge(s_ke, 1)
                    v.tensor_scalar(ka, kE, cols[:, 0:1], -1.0, ALU.mult, ALU.mult)
                    v.scalar_tensor_tensor(out=kW[:, 0], in0=kB, scalar=cols[:, 0:1], in1=kC,
                                           op0=ALU.mult, op1=ALU.mult).then_inc(s_ka, 1)
            layer_norm(1, NC)
            def kernel_terms(q):
                dve.wait_ge(s_kexp, q // 16 + 1)
                for i in range(2):
                    if q == 0:
                        ins = v.tensor_scalar(kT[:, i], kexp[:, q, :], kW[:, i, q:q + 1], None, ALU.mult)
                    else:
                        dve.wait_ge(s_kacc, 2 * q + i - 1)
                        ins = v.scalar_tensor_tensor(out=kT[:, i], in0=kexp[:, q, :], scalar=kW[:, i, q:q + 1],
                                                     in1=kT[:, i], op0=ALU.mult, op1=ALU.add)
                    ins.then_inc(s_kacc, 1)

            for g in range(BATCH // GB):
                for b in range(GB):
                    for j in (1, 3):
                        if g >= 2:
                            dve.wait_ge(s_m, g - 1)
                        dve.wait_ge(s_gb, (GB * g + b) * 4 + j + 1)
                        v.tensor_copy(gbuf[:, g % 2, 4 * j:4 * j + 4, P * b:P * (b + 1)],
                                      ps[:, 4 + j, :].rearrange("p (h c) -> p h c", c=P)).then_inc(s_gbv, 1)
                    done = 10 * (GB * g + b - 1)
                    if done == 0:
                        dve.wait_ge(s_kg, 1)
                        dve.wait_ge(s_ka, 1)
                        link(v.tensor_tensor(kW[:, 1], kW[:, 0], kg, ALU.mult))
                    if done >= 0:
                        for q in range(done, min(done + 10, NSTATE)):
                            kernel_terms(q)
            dve.wait_ge(s_kacc, 2 * NSTATE)
            v.tensor_scalar(kT[:, 0, 0:1], kT[:, 0, 0:1], cols[:, 18:19], None, ALU.add).then_inc(s_kacc, 1)
            layer_norm(2)
            wide = lambda x: x.unsqueeze(2).broadcast_to([P, NT, EXPERTS])
            tiew = tie[:].unsqueeze(1).broadcast_to([P, NT, EXPERTS])
            dve.wait_ge(s_lg, 1)
            lg = ps[:, 4, 0:NT * EXPERTS].rearrange("p (t e) -> p t e", e=EXPERTS)
            link(v.tensor_reduce(r_mx, lg, AX.X, ALU.max))
            v.tensor_tensor(r_lg, lg, wide(r_mx), ALU.subtract).then_inc(s_lsub, 1)
            dve.wait_ge(s_lexp, 1)
            link(v.tensor_reduce(r_sum, r_pr, AX.X, ALU.add))
            link(v.reciprocal(r_rec, r_sum))
            link(v.tensor_tensor(r_pr, r_pr, wide(r_rec), ALU.mult))
            link(v.tensor_reduce(r_mx, r_pr, AX.X, ALU.max))
            link(v.tensor_tensor(r_s, r_pr, wide(r_mx), ALU.is_ge))
            link(v.tensor_tensor(r_s, r_s, tiew, ALU.mult))
            link(v.tensor_reduce(r_t, r_s, AX.X, ALU.max))
            link(v.tensor_tensor(r_oh, r_s, wide(r_t), ALU.is_ge))
            link(v.scalar_tensor_tensor(out=r_p2, in0=r_oh, scalar=-2.0, in1=r_pr, op0=ALU.mult, op1=ALU.add))
            link(v.tensor_reduce(r_mx, r_p2, AX.X, ALU.max))
            link(v.tensor_tensor(r_s, r_p2, wide(r_mx), ALU.is_ge))
            link(v.tensor_tensor(r_s, r_s, tiew, ALU.mult))
            link(v.tensor_reduce(r_t, r_s, AX.X, ALU.max))
            link(v.tensor_tensor(r_s, r_s, wide(r_t), ALU.is_ge))
            v.tensor_tensor(r_mask, r_oh, r_s, ALU.add).then_inc(s_mask, 1)
            dve.wait_ge(s_mask, 1)
            dve.wait_ge(s_cnt, 1)
            pair = lambda x: x.rearrange("p (b two) e -> p b two e", two=2)
            v.tensor_tensor(pair(r_pos), ps[:, 5, 0:NT * EXPERTS].rearrange("p (two b e) -> p b two e", two=2, e=EXPERTS),
                            pair(r_mask), ALU.mult).then_inc(s_pos, 1)

            def dispatch(t):
                if t >= 4:
                    dve.wait_ge(s_xdp, t - 2 if t % 2 == 0 else t - 3)
                    dve.wait_ge(s_comb, t - 3)
                v.tensor_tensor(disp[:, t % 4], iota_slot[:].unsqueeze(1).broadcast_to([P, EXPERTS, CAP]),
                                r_pos[:, t, :].unsqueeze(2).broadcast_to([P, EXPERTS, CAP]),
                                ALU.is_equal).then_inc(s_disp, 1)

            dve.wait_ge(s_pos, 1)
            for t in range(4):
                dispatch(t)
            dve.wait_ge(s_kps, 1)
            v.tensor_copy(ktok, ps[:, 7, 0:2 * P].rearrange("p (i c) -> p i c", c=P)).then_inc(s_kt, 1)
            for b in range(BATCH):
                dve.wait_ge(s_xdp, 2 * b + 2)
                v.tensor_copy(xd[:, 4:8, b, :], ps[:, 5 + 2 * (b % 2), 0:HALF_SLOTS].rearrange("p (e s) -> p e s", s=CAP)
                              ).then_inc(s_xdv, 1)
                if b + 2 < BATCH:
                    dispatch(2 * b + 4)
                    dispatch(2 * b + 5)
            for m in range(EXPERTS * 2 * NFB):
                e, u = divmod(m, 2 * NFB)
                hb = u % 2
                j, full = expert_block(u), u >= 2
                if full:
                    dve.wait_ge(s_eh3, 2 * (NFB - 1) * e + u - 1)
                dve.wait_ge(s_sil, m + 1)
                if e >= 2:
                    dve.wait_ge(s_eop, 2 * (e - 1))
                r = slice(0, P) if full else slice(P - TAIL, P)
                v.tensor_tensor(eh[r, e % 2, j, HALF_SLOTS * hb:HALF_SLOTS * (hb + 1)],
                                ps[r, (6 if full else 4) + m % 2, 0:HALF_SLOTS], esil[r, m % 2, :],
                                ALU.mult).then_inc(s_eh, 1)
            layer_norm(3)
            dve.wait_ge(s_hd, 80)

            def u_out(c):
                dve.wait_ge(s_u, c + 1)
                v.tensor_tensor(u_tok[:, CT * c:CT * (c + 1), :], ps[:, c, :].rearrange("p (t c) -> p t c", c=P),
                                bin_tok.unsqueeze(1).broadcast_to([P, CT, P]), ALU.add).then_inc(s_us, 1)

            for c in range(3):
                u_out(c)
            for hb in range(2):
                for k, (um, km) in enumerate([(0, 0), (0, 2), (2, 2), (2, 0)]):
                    dve.wait_ge(s_uf, 2 * hb + k // 2 + 1)
                    dve.wait_ge(s_kf, 1)
                    v.tensor_tensor(prod[:, 4 * hb + k], ps[:, 4 + um:6 + um, :].rearrange("p m (b c) -> p m b c", c=P),
                                    kf[:, km:km + 2, :].unsqueeze(2).broadcast_to([P, 2, 4, P]),
                                    ALU.mult).then_inc(s_prod, 1)
                    if hb == 0 and k == 1:
                        u_out(3)

            def bit_stats(c):
                dve.wait_ge(s_xtok, normalised(4, c))
                for i in range(CT * c, CT * (c + 1)):
                    ins = v.bn_stats(bn[:, i, :], x_tok[:, i, :])
                link(ins)
                for i in range(CT * c, CT * (c + 1)):
                    ins = v.bn_aggr(mv2[:, i, :], bn[:, i, :])
                ins.then_inc(s_mv2, 1)

            def bit_max(c):
                dve.wait_ge(s_xT, 5 * NC + c + 1)
                return v.tensor_reduce(cols[:, 25 + c:26 + c], xnT[:, CHUNK * c:CHUNK * (c + 1)], AX.X, ALU.max,
                                       apply_absolute_value=True)

            gam, beta, thr, nthr = cols[:, 30:31], cols[:, 34:35], cols[:, 35:36], cols[:, 37:38]

            def ternary_weights():
                dve.wait_ge(s_bws, 1)
                link(v.tensor_scalar(beta, ps[:, 6, 0:1], 1.0 / (P * P), None, ALU.mult))
                link(v.tensor_scalar(thr, beta, 1e-5, 0.5, ALU.add, ALU.mult))
                link(v.tensor_scalar(nthr, thr, -1.0, None, ALU.mult))
                link(v.tensor_scalar(bwt, bw, nthr, None, ALU.is_lt))
                v.scalar_tensor_tensor(out=bwq, in0=bw, scalar=thr, in1=bwt, op0=ALU.is_gt,
                                       op1=ALU.subtract).then_inc(s_bwq, 1)

            v.tensor_reduce(cols[:, 24:25], bw, AX.X, ALU.add, apply_absolute_value=True).then_inc(s_bsum, 1)
            ln_stats(4, 0, 2 * NC + 1)
            ln_stats(4, 1, 2 * NC + 2)
            bit_stats(0)
            bit_stats(1)
            ln_stats(4, 2, 2 * NC + 3)
            ln_stats(4, 3, 2 * NC + 4)
            dve.wait_ge(s_rstd, NC * 4 + NC)
            normalise(x_tok, mv, rstd, (NT - 2, NT - 1)).then_inc(s_xtok, 1)
            bit_stats(2)
            bit_stats(3)
            bit_max(0)
            dve.wait_ge(s_rstd2, NC)
            normalise(xh, mv2, rstd2, (NT - 2, NT - 1)).then_inc(s_xh, 1)
            bit_max(1)
            ternary_weights()
            bit_max(2)
            link(bit_max(3))
            v.tensor_reduce(cols[:, 29:30], cols[:, 25:29], AX.X, ALU.max).then_inc(s_gmx, 1)
            dve.wait_ge(s_gt, 1)
            v.tensor_reduce(cols[0:1, 36:37], ps[0:1, 4, 0:P], AX.X, ALU.max).then_inc(s_gm1, 1)
            dve.wait_ge(s_gb2, 1)
            link(v.tensor_copy(gam, ps[:, 5, 0:1]))
            link(v.reciprocal(cols[:, 32:33], gam))
            link(v.tensor_scalar(cols[:, 33:34], cols[:, 32:33], 128.0, None, ALU.mult))
            v.tensor_scalar(cols[:, 38:39], gam, beta, 1.0 / 128.0, ALU.mult, ALU.mult)
            for c in range(NC):
                t = slice(CHUNK * c, CHUNK * (c + 1))
                link(v.tensor_scalar(xqT[:, t], xnT[:, t], cols[:, 33:34], QCLIP, ALU.mult, ALU.min))
                v.tensor_scalar(xqT[:, t], xqT[:, t], -QCLIP, None, ALU.max).then_inc(s_xq, 1)
            layer_norm(5)
            for k in range(2):
                w = wT[:, W3OUT + P * k:W3OUT + P * (k + 1)]
                ins = v.tensor_scalar(w, w, cols[:, 20 + k:21 + k], None, ALU.mult)
            ins.then_inc(s_nw, 1)
            def taps(c, k):
                dve.wait_ge(s_raw, 3 * c + k + 1)
                src = xraw[:, k, CHUNK * c:CHUNK * (c + 1)].rearrange("p (b t) -> p b t", b=2)
                acc = xc[:, k, CHUNK * c:CHUNK * (c + 1)].rearrange("p (b t) -> p b t", b=2)
                link(v.tensor_scalar(acc, src, cols[:, 9 + 4 * k:10 + 4 * k], cols[:, 3 + k:4 + k], ALU.mult, ALU.add))
                for j in range(1, 4):
                    ins = v.scalar_tensor_tensor(out=acc[:, :, j:SEQ], in0=src[:, :, 0:SEQ - j],
                                                 scalar=cols[:, 9 + 4 * k - j:10 + 4 * k - j],
                                                 in1=acc[:, :, j:SEQ], op0=ALU.mult, op1=ALU.add)
                    if j < 3:
                        link(ins)
                ins.then_inc(s_conv, 1)

            taps(0, 0)
            taps(0, 1)
            head4 = lambda x: x.unsqueeze(1).broadcast_to([P, NT, N_HEADS3])
            dve.wait_ge(s_dtp, 1)
            link(v.tensor_tensor(d_v, ps[:, 7, 0:64].rearrange("p (t h) -> p t h", h=N_HEADS3), head4(hd[:, 1, :]), ALU.add))
            v.scalar_tensor_tensor(out=d_n, in0=d_v, scalar=-1.0, in1=d_v, op0=ALU.mult, op1=ALU.min).then_inc(s_sp1, 1)
            dve.wait_ge(s_ea, 1)
            v.tensor_scalar(hd[:, 2, :], hd[:, 2, :], -1.0, None, ALU.mult)
            dve.wait_ge(s_sp2, 1)
            link(v.scalar_tensor_tensor(out=d_dt, in0=d_v, scalar=0.0, in1=d_l, op0=ALU.max, op1=ALU.add))
            v.tensor_tensor(d_a, d_dt, head4(hd[:, 2, :]), ALU.mult).then_inc(s_a, 1)
            taps(0, 2)
            for c in (1, 2):
                for k in range(3):
                    taps(c, k)

            def xs_out(b):
                dve.wait_ge(s_xsp, b + 1)
                if b >= 2:
                    dve.wait_ge(s_yd, b - 1)
                t = slice(2 * b, 2 * b + 2)
                src = ps[:, 2, :].rearrange("p (t h e) -> p t h e", t=2, h=N_HEADS3)
                v.tensor_tensor(xs[:, t, :, :], src, d_dt[:, t, :].unsqueeze(3).broadcast_to([P, 2, N_HEADS3, HEAD3]),
                                ALU.mult)
                v.tensor_tensor(xdd[:, b % 2], src,
                                dsk.unsqueeze(1).unsqueeze(3).broadcast_to([P, 2, N_HEADS3, HEAD3]),
                                ALU.mult).then_inc(s_xs, 1)

            def scores_out(b):
                dve.wait_ge(s_gtp, b + 1)
                v.tensor_tensor(gts[:, b % 2], ps[:, 6, 0:256].rearrange("p (k t) -> p k t", k=2),
                                tri[:].unsqueeze(1).broadcast_to([P, 2, P]), ALU.mult)
                v.tensor_copy(b_tok[:, b % 2], ps[:, 6, 256:256 + NSTATE]).then_inc(s_gts, 1)

            def state_y_out(b):
                dve.wait_ge(s_yip, b + 1)
                if b >= 2:
                    dve.wait_ge(s_yd2, b - 1)
                v.tensor_tensor(yst[:, b % 2], ps[:, 6, 0:D_INNER].rearrange("p (h e) -> p h e", e=HEAD3),
                                dexp[:, 1, b, :].unsqueeze(2).broadcast_to([P, N_HEADS3, HEAD3]),
                                ALU.mult).then_inc(s_yi, 1)

            def add_d(b):
                dve.wait_ge(s_yq, 2 * b + 2)
                dve.wait_ge(s_yd2, b + 1)
                if b >= 2:
                    dve.wait_ge(s_yt, b - 1)
                    dve.wait_ge(s_sq, b - 1)
                v.tensor_tensor(ygt[:, b % 2], ps[:, ssd_bank(b), :].rearrange("p (t c) -> p t c", t=2),
                                xdd[:, b % 2].rearrange("p t h e -> p t (h e)"), ALU.add).then_inc(s_yd, 1)

            def mean_square(c):
                dve.wait_ge(s_sq, 2 * c + 2)
                t = slice(CT * c, CT * (c + 1))
                v.tensor_scalar(ssv[:, t], ssv[:, t], 1.0 / D_INNER, 1e-5, ALU.mult, ALU.add).then_inc(s_ssv, 1)

            xs_out(0)
            scores_out(0)
            dve.wait_ge(s_dexp, 1)
            for p in range(2 * BATCH):
                b, half = divmod(p, 2)
                dve.wait_ge(s_le, p + 1)
                dve.wait_ge(s_gts, b + 1)
                v.tensor_tensor(mring[:, p % 3], mring[:, p % 3], gts[:, b % 2].unsqueeze(1).broadcast_to([P, 2, 2, P]),
                                ALU.mult).then_inc(s_mm, 1)
                if half == 0:
                    if b:
                        add_d(b - 1)
                    if b in (3, 5, 7):
                        mean_square((b - 3) // 2)
                    if b in (5, 7):
                        ln_stats(6, (b - 5) // 2)
                    if b == 6:
                        ln_apply(6, 0)
                else:
                    state_y_out(b)
                    if b + 1 < BATCH:
                        xs_out(b + 1)
                        scores_out(b + 1)
                    if b == 7:
                        ln_apply(6, 1)
                if p in (0, 2, 4):
                    taps(3, p // 2)

            def mix(c):
                b = slice(2 * c, 2 * c + 2)
                dve.wait_ge(s_dif, c + 1)
                v.scalar_tensor_tensor(out=xk[:, b, :], in0=xdif[:, b, :], scalar=cols[:, 23:24],
                                       in1=xpad[:, b, 0:SEQ], op0=ALU.mult, op1=ALU.add).then_inc(s_xk, 1)
                v.scalar_tensor_tensor(out=xr[:, b, :], in0=xdif[:, b, :], scalar=cols[:, 22:23],
                                       in1=xpad[:, b, 0:SEQ], op0=ALU.mult, op1=ALU.add).then_inc(s_xr, 1)

            add_d(BATCH - 1)
            ln_stats(6, 2)
            mean_square(3)
            mix(0)
            ln_apply(6, 2)
            mix(1)
            ln_stats(6, 3)
            square_k(0)
            ln_apply(6, 3)
            square_k(1)
            mix(2)
            ln_stats(7, 0)
            mix(3)
            square_k(2)
            ln_stats(7, 1)
            square_k(3)
            ln_stats(7, 2)
            ln_stats(7, 3)
            dve.wait_ge(s_rstd, NC * 7 + NC)
            normalise(x_tok, mv, rstd, (NT - 2, NT - 1)).then_inc(s_xtok, 1)

        @block.tensor
        def _(pe):
            te = nc.tensor

            def weights_in(k):
                blocks, _, sm, val = wgroups[k]
                pe.wait_ge(sm, val)
                at = 0
                if k >= 3:
                    pe.wait_ge(s_wev, k - 1)
                elif k:
                    pe.wait_ge(s_qevac, BATCH)
                for i, src in enumerate(blocks):
                    r = src.shape[0]
                    mm = te.transpose(ps[:, weights_bank(k), at:at + r], src, ident[0:r, 0:r])
                    at += r
                mm.then_inc(s_wtp, 1)

            def x_transpose(level, c):
                if level == 5:
                    pe.wait_ge(s_xh, 2 * (c + 1))
                elif level:
                    pe.wait_ge(s_xtok, normalised(level - 1, c))
                else:
                    pe.wait_ge(s_x[c], 16)
                for i in range(CT):
                    src = xh if level == 5 else x_tok
                    mm = te.transpose(ps[:, c, P * i:P * (i + 1)], src[:, CT * c + i, :], ident[:])
                mm.then_inc(s_tp, 1)

            def xTt(t):
                return xT[:, P * t:P * (t + 1)]

            def half_rows(k):
                return slice(HDIM1 * (k // 2), HDIM1 * (k // 2) + HDIM1)

            pe.wait_ge(s_const, 2)
            weights_in(0)
            x_transpose(0, 0)
            pe.wait_ge(s_ones, 1)
            def qkv_product(b):
                pe.wait_ge(s_xT, b // 2 + 1)
                if b == 0:
                    pe.wait_ge(s_wev, 1)
                else:
                    pe.wait_ge(s_qevac, b)
                for i in range(2):
                    mm = te.matmul(ps[:, 4 + i, 0:384], xTt(2 * b + i), wT[:, WQKV:WQKV + 384],
                                   start=True, stop=True)
                mm.then_inc(s_qkv, 1)

            qkv_product(0)
            for s in range(BATCH + 6):
                if s + 1 < NC:
                    x_transpose(0, s + 1)
                if 3 <= s < BATCH + 3:
                    b = s - 3
                    pe.wait_ge(s_ctxs, b + 1)
                    pe.wait_ge(s_q0T, b + 1)
                    if b >= 1:
                        pe.wait_ge(s_onum, b)
                    else:
                        pe.wait_ge(s_xT, NC)
                    for i in range(2):
                        mm = te.matmul(ps[:, 3, 144 * i:144 * (i + 1)], q0T[:, P * (2 * b + i):P * (2 * b + i + 1)],
                                       ctxs[:, b, :], start=True, stop=True)
                    mm.then_inc(s_num, 1)
                if 5 <= s < BATCH + 5:
                    b = s - 5
                    pe.wait_ge(s_o0, b + 1)
                    if b >= 1:
                        pe.wait_ge(s_o0T, b)
                    for i in range(2):
                        mm = te.transpose(ps[:, 2, P * i:P * (i + 1)], o0[:, 2 * b + i, :], ident[:])
                    mm.then_inc(s_otp, 1)
                if 2 <= s < BATCH + 2:
                    b = s - 2
                    pe.wait_ge(s_qk, b + 1)
                    if b >= 1:
                        pe.wait_ge(s_ctxs, b)
                    for i in range(2):
                        t = 2 * b + i
                        mm = te.matmul(ps[:, 6, 0:144], qkv[:, t, P:2 * P], qkv[:, t, 256:400],
                                       start=(i == 0), stop=(i == 1))
                    mm.then_inc(s_ctx, 1)
                    if b >= 1:
                        pe.wait_ge(s_q0T, b)
                    for i in range(2):
                        mm = te.transpose(ps[:, 7, P * i:P * (i + 1)], qkv[:, 2 * b + i, 0:P], ident[:])
                    mm.then_inc(s_qtp, 1)
                if s + 1 < BATCH:
                    qkv_product(s + 1)
                if s >= BATCH:
                    for k in (2 * (s - BATCH) + 1, 2 * (s - BATCH) + 2):
                        if k < len(wgroups):
                            weights_in(k)
                if s == BATCH + 5:
                    x_transpose(1, 0)
                for c in {7: [0], 9: [1], 13: [2, 3]}.get(s, []):
                    pe.wait_ge(s_o0T, 2 * c + 2 if c < 2 else BATCH)
                    pe.wait_ge(s_onum, 2 * c + 2)
                    for i in range(CT):
                        t = CT * c + i
                        mm = te.matmul(ps[:, c, P * i:P * (i + 1)], o0T[:, P * t:P * (t + 1)], wT[:, WP:WP + P],
                                       start=True, stop=True)
                    mm.then_inc(s_out, 1)
            pe.wait_ge(s_wev, len(wgroups))
            pe.wait_ge(s_q0T, BATCH)
            pe.wait_ge(s_ctxs, BATCH)
            for k in range(4):
                r = half_rows(k)
                for i in range(4):
                    pair = 4 * (k % 2) + i
                    mm = te.matmul(ps[:, 4 + k, P * i:P * (i + 1)], l1w[r, 1, pair, :], l1w[r, 0, pair, :],
                                   start=True, stop=True)
                mm.then_inc(s_ab, 1)
            pe.wait_ge(s_wf, 64)

            def hidden0(c):
                if c:
                    x_transpose(1, c)
                pe.wait_ge(s_xT, NC + c + 1)
                for j in range(4):
                    if c:
                        pe.wait_ge(s_g0, 4 * (c - 1) + j + 1)
                    else:
                        pe.wait_ge(s_abs, j + 1)
                    te.matmul(ps[:, 4 + j, :], w1s[:, P * j:P * (j + 1)], xT[:, CHUNK * c:CHUNK * (c + 1)],
                              start=True, stop=True).then_inc(s_h0, 1)

            def out0(c):
                pe.wait_ge(s_g0, 4 * c + 4)
                for i in range(CT):
                    for j in range(4):
                        mm = te.matmul(ps[:, c, P * i:P * (i + 1)], h0T[:, c % 2, j, P * i:P * (i + 1)],
                                       w2s[:, j, :], start=(j == 0), stop=(j == 3))
                mm.then_inc(s_out, 1)

            for c in range(NC + 1):
                if c < NC:
                    hidden0(c)
                if c >= 1:
                    out0(c - 1)
            pe.wait_ge(s_g0, 16)
            for k in range(4):
                r = half_rows(k)
                for i in range(4):
                    pair = 4 * (k % 2) + i
                    mm = te.matmul(ps[:, 4 + k, P * i:P * (i + 1)], l1w[r, 2, pair, :],
                                   wT[r, WO1 + P * pair:WO1 + P * (pair + 1)], start=True, stop=True)
                mm.then_inc(s_ab, 1)
            for c in range(NC):
                x_transpose(2, c)
                if c % 2 == 0:
                    pe.wait_ge(s_abs, 8)
                for b in (2 * c, 2 * c + 1):
                    for i in range(2):
                        mm = te.matmul(ps[:, 4 + b // 4, P * (b % 4):P * (b % 4 + 1)], x_tok[:, 2 * b + i, :],
                                       x_tok[:, 2 * b + i, :], start=(i == 0), stop=(i == 1))
                if c % 2:
                    mm.then_inc(s_g, 1)
            pe.wait_ge(s_gs, 2)

            def sum_heads(g):
                pe.wait_ge(s_gba, 2 * GB * (g + 1))
                pe.wait_ge(s_gbv, 2 * GB * (g + 1))
                pe.wait_ge(s_xT, 2 * NC + g + 1)
                for h in range(HEADS1):
                    mm = te.matmul(ps[:, g, 0:GB * P], l1A[:, h, :], gbuf[:, g % 2, h, :],
                                   start=(h == 0), stop=(h == HEADS1 - 1))
                mm.then_inc(s_m, 1)

            for g in range(BATCH // GB):
                for b in range(GB * g, GB * (g + 1)):
                    for j in range(4):
                        if b:
                            pe.wait_ge(s_gbv if j % 2 else s_gba, 2 * (b - 1) + j // 2 + 1)
                        te.matmul(ps[:, 4 + j, :], gram[:, b, :],
                                  l1B[:, 4 * j:4 * j + 4, :], start=True, stop=True).then_inc(s_gb, 1)
                if g:
                    sum_heads(g - 1)
            sum_heads(BATCH // GB - 1)
            for c in range(NC):
                pe.wait_ge(s_ms, c + 1)
                for i in range(CT):
                    t = CT * c + i
                    mm = te.matmul(ps[:, c, P * i:P * (i + 1)], xTt(t), l1M[:, t // 2, :], start=True, stop=True)
                mm.then_inc(s_out, 1)
            def ssm_spectrum():
                pe.wait_ge(s_kt, 1)
                pe.wait_ge(s_four, 48)
                for m in range(4):
                    for k in range(2):
                        mm = te.matmul(ps[:, 6, P * m:P * (m + 1)], four[:, k, P * m:P * (m + 1)], ktok[:, k, :],
                                       start=(k == 0), stop=(k == 1))
                mm.then_inc(s_kfp, 1)

            def router(c):
                pe.wait_ge(s_xT, 3 * NC + c + 1)
                for t in range(CT * c, CT * (c + 1)):
                    mm = te.matmul(ps[:, 4, EXPERTS * t:EXPERTS * (t + 1)], xTt(t), wT[:, GATE:GATE + EXPERTS],
                                   start=True, stop=True)
                if c == NC - 1:
                    mm.then_inc(s_lg, 1)

            pe.wait_ge(s_gba, BATCH * 2)
            for c in range(NC):
                x_transpose(3, c)
                if c:
                    router(c - 1)
            pe.wait_ge(s_kacc, 2 * NSTATE + 1)
            pe.wait_ge(s_gbv, BATCH * 2)
            te.transpose(ps[:, 7, 0:P], kT[:, 0], ident[:])
            te.transpose(ps[:, 7, P:2 * P], kT[:, 1], ident[:]).then_inc(s_kps, 1)
            router(NC - 1)
            pe.wait_ge(s_mask, 1)
            mpair = r_mask.rearrange("p (b two) e -> p b two e", two=2)
            te.matmul(ps[:, 5, 0:64], tri[:], mpair[:, :, 0, :], start=True, stop=True)
            te.matmul(ps[:, 5, 64:128], tri[:], mpair[:, :, 1, :], start=True, stop=False)
            te.matmul(ps[:, 5, 64:128], ones[:], mpair[:, :, 0, :], start=False, stop=True).then_inc(s_cnt, 1)
            pe.wait_ge(s_pos, 1)

            def gather(b):
                pe.wait_ge(s_disp, 2 * b + 2)
                if b >= 2:
                    pe.wait_ge(s_xda, b - 1)
                    pe.wait_ge(s_xdv, b - 1)
                for h in range(2):
                    for k in range(2):
                        t = 2 * b + k
                        mm = te.matmul(ps[:, 4 + 2 * (b % 2) + h, 0:HALF_SLOTS], x_tok[:, t, :],
                                       disp[:, t % 4, 4 * h:4 * h + 4, :], start=(k == 0), stop=(k == 1))
                    mm.then_inc(s_xdp, 1)

            def comb_transpose(b):
                for t in (2 * b, 2 * b + 1):
                    pe.wait_ge(s_comb, t + 1)
                    if t >= 2:
                        pe.wait_ge(s_cT, t - 1)
                    for k in range(ST):
                        mm = te.transpose(ps[:, 2 * (t % 2) + k // 4, P * (k % 4):P * (k % 4 + 1)],
                                          comb[:, t % 4, P * k:P * (k + 1)], ident[:])
                    mm.then_inc(s_ctp, 1)

            def expert_out(e):
                pe.wait_ge(s_eh, 8 * e + 8)
                if e >= 2:
                    pe.wait_ge(s_eoT, 2 * (e - 1))
                elif e == 0:
                    pe.wait_ge(s_cT, NT)
                    pe.wait_ge(s_zero, 4)
                for hb in range(2):
                    for j in range(NFB):
                        mm = te.matmul(ps[:, 2 * (e % 2) + hb, 0:HALF_SLOTS], ew2[e % 2][:, j, :],
                                       eh[:, e % 2, j, HALF_SLOTS * hb:HALF_SLOTS * (hb + 1)],
                                       start=(j == 0), stop=(j == NFB - 1))
                    mm.then_inc(s_eop, 1)

            for b in range(BATCH):
                if b == 1:
                    ssm_spectrum()
                    pe.wait_ge(s_kf, 1)
                gather(b)
                if b:
                    comb_transpose(b - 1)
            for n in range(EXPERTS * 2 * NFB):
                e, u = divmod(n, 2 * NFB)
                j, hb = expert_block(u), u % 2
                if u == 0:
                    pe.wait_ge(s_ew[e % 2], 80 * (e // 2 + 1))
                rhs = xd[:, e, 4 * hb:4 * hb + 4, :]
                if n >= 2:
                    pe.wait_ge(s_sil, n - 1)
                    pe.wait_ge(s_eh, n - 1)
                else:
                    pe.wait_ge(s_xda, BATCH)
                    pe.wait_ge(s_xdv, BATCH)
                te.matmul(ps[:, 4 + n % 2, 0:HALF_SLOTS], ew13[e % 2][:, P * j:P * (j + 1)], rhs,
                          start=True, stop=True).then_inc(s_eh1, 1)
                if j < NFB - 1:
                    te.matmul(ps[:, 6 + n % 2, 0:HALF_SLOTS], ew13[e % 2][:, P * (NFB + j):P * (NFB + j + 1)], rhs,
                              start=True, stop=True).then_inc(s_eh3, 1)
                if n == 0:
                    comb_transpose(BATCH - 1)
                if e and u == 1:
                    expert_out(e - 1)
            expert_out(EXPERTS - 1)

            def out_transpose(b):
                pe.wait_ge(s_eoT, 2 * EXPERTS)
                if b >= 2:
                    pe.wait_ge(s_eo, b - 1)
                slots = eoT[:, b].rearrange("p e s -> p (e s)")
                for k in range(ST):
                    mm = te.transpose(ps[:, 4 + 2 * (b % 2) + k // 4, P * (k % 4):P * (k % 4 + 1)],
                                      slots[:, P * k:P * (k + 1)], ident[:])
                mm.then_inc(s_eot, 1)

            out_transpose(0)
            for b in range(BATCH):
                if b + 1 < BATCH:
                    out_transpose(b + 1)
                pe.wait_ge(s_eo, b + 1)
                for t in (2 * b, 2 * b + 1):
                    for k in range(ST):
                        mm = te.matmul(ps[:, t // CT, P * (t % CT):P * (t % CT + 1)], combT[:, t, P * k:P * (k + 1)],
                                       eo[:, b, k, :], start=(k == 0), stop=(k == ST - 1))
                if b % 2:
                    mm.then_inc(s_out, 1)
            upair = u_tok.rearrange("p (b two) c -> p b two c", two=2)

            def u_in(c):
                pe.wait_ge(s_xT, 4 * NC + c + 1)
                for i in range(CT):
                    mm = te.matmul(ps[:, c, P * i:P * (i + 1)], xTt(CT * c + i), wT[:, WIN:WIN + P],
                                   start=True, stop=True)
                mm.then_inc(s_u, 1)

            def transform(hb):
                pe.wait_ge(s_us, 2 * hb + 2)
                if hb == 0:
                    pe.wait_ge(s_eo, BATCH)
                for m in range(4):
                    if hb:
                        pe.wait_ge(s_prod, 2 * (m // 2) + 2)
                    for k in range(2):
                        mm = te.matmul(ps[:, 4 + m, :], four[:, k, P * m:P * (m + 1)],
                                       upair[:, 4 * hb:4 * hb + 4, k, :], start=(k == 0), stop=(k == 1))
                    if m % 2:
                        mm.then_inc(s_uf, 1)

            x_transpose(4, 0)
            x_transpose(4, 1)
            u_in(0)
            u_in(1)
            x_transpose(4, 2)
            u_in(2)
            x_transpose(4, 3)
            transform(0)
            u_in(3)
            transform(1)
            for hb in range(2):
                for c in (2 * hb, 2 * hb + 1):
                    pe.wait_ge(s_yf, 2 * hb + 2)
                    for i in range(2):
                        for m in range(4):
                            mm = te.matmul(ps[:, c, SEQ * i:SEQ * (i + 1)], yf[:, m, 2 * c + i, :], finv[:, m, :],
                                           start=(m == 0), stop=(m == 3))
                    mm.then_inc(s_y, 1)
                for c in (2 * hb, 2 * hb + 1):
                    pe.wait_ge(s_yT, c + 1)
                    for i in range(CT):
                        t = CT * c + i
                        mm = te.matmul(ps[:, c, P * i:P * (i + 1)], yT[:, P * t:P * (t + 1)], wT[:, WOUT:WOUT + P],
                                       start=True, stop=True)
                    mm.then_inc(s_out, 1)
            pe.wait_ge(s_bsum, 1)
            te.matmul(ps[:, 6, 0:1], ones[:], cols[:, 24:25], start=True, stop=True).then_inc(s_bws, 1)
            for c in range(NC):
                x_transpose(5, c)
            pe.wait_ge(s_gmx, 1)
            te.transpose(ps[0:1, 4, 0:P], cols[:, 29:30], ident[:]).then_inc(s_gt, 1)
            pe.wait_ge(s_gm1, 1)
            te.matmul(ps[:, 5, 0:1], ones[0:1, :], cols[0:1, 36:37], start=True, stop=True).then_inc(s_gb2, 1)
            pe.wait_ge(s_bwq, 1)
            for c in range(NC):
                pe.wait_ge(s_xq, c + 1)
                for i in range(CT):
                    t = CT * c + i
                    mm = te.matmul(ps[:, c, P * i:P * (i + 1)], xqT[:, P * t:P * (t + 1)], bwq, start=True, stop=True)
                mm.then_inc(s_out, 1)
            for c in range(NC):
                x_transpose(6, c)
            for c in range(NC):
                xcs = xT[:, CHUNK * c:CHUNK * (c + 1)]
                pe.wait_ge(s_xT, 6 * NC + c + 1)
                for k in range(3):
                    n = 3 * c + k
                    if n >= 5:
                        pe.wait_ge(s_raw, n - 4)
                    te.matmul(ps[:, xbc_bank(n), :], wT[:, W3IN + P * (2 + k):W3IN + P * (3 + k)], xcs,
                              start=True, stop=True).then_inc(s_xbc, 1)
                if c == 0:
                    for t in range(NT):
                        pe.wait_ge(s_xT, 6 * NC + t // CT + 1)
                        mm = te.matmul(ps[:, 7, N_HEADS3 * t:N_HEADS3 * (t + 1)], xTt(t), wT[:, W3IN + 640:W3IN + 644],
                                       start=True, stop=True)
                    mm.then_inc(s_dtp, 1)
                if c == 1:
                    pe.wait_ge(s_a, 1)
                    apair = d_a.rearrange("p (b two) h -> p b two h", two=2)
                    te.matmul(ps[:, 7, 64:96], below[:], apair[:, :, 0, :], start=True, stop=True)
                    te.matmul(ps[:, 7, 96:128], tri[:], apair[:, :, 1, :], start=True, stop=True).then_inc(s_cum, 1)
            for c in range(NC):
                for k in range(2):
                    n = 2 * c + k
                    if n == 2:
                        pe.wait_ge(s_dexp, 1)
                    if n >= 3:
                        pe.wait_ge(s_raw, n + 5)
                    for i in range(2):
                        mm = te.matmul(ps[:, z_bank(n), D_INNER * i:D_INNER * (i + 1)], xTt(CT * c + 2 * k + i),
                                       wT[:, W3IN:W3IN + D_INNER], start=True, stop=True)
                    mm.then_inc(s_z, 1)

            def x_tokens(b):
                pe.wait_ge(s_xc, 4 * (b // 2) + 2)
                if b:
                    pe.wait_ge(s_xs, b)
                else:
                    pe.wait_ge(s_sz, 2 * NC)
                for i in range(2):
                    for k in range(2):
                        t = 2 * b + i
                        mm = te.transpose(ps[:, 2, 256 * i + P * k:256 * i + P * (k + 1)],
                                          xc[:, k, P * t:P * (t + 1)], ident[:])
                mm.then_inc(s_xsp, 1)

            def scores(b):
                pe.wait_ge(s_xc, 4 * (b // 2) + 4)
                if b:
                    pe.wait_ge(s_yi, b)
                for i in range(2):
                    t = slice(SEQ * b + P * i, SEQ * b + P * (i + 1))
                    te.matmul(ps[:, 6, P * i:P * (i + 1)], xc[0:NSTATE, 2, t], cT[0:NSTATE, t], start=True, stop=True)
                te.transpose(ps[:, 6, 256:256 + NSTATE], xc[0:NSTATE, 2, SEQ * b:SEQ * b + P],
                             ident[0:NSTATE, 0:NSTATE]).then_inc(s_gtp, 1)

            def decays(p):
                b, half = divmod(p, 2)
                pe.wait_ge(s_lm, b + 1)
                if p >= 2:
                    pe.wait_ge(s_le, p - 1)
                for h in range(2):
                    for i in range(2):
                        mm = te.matmul(ps[:, 4 + p % 2, P * (2 * h + i):P * (2 * h + i + 1)],
                                       lmat[:, b % 2, i, 2 * half + h, :], tri[:], start=True, stop=True)
                mm.then_inc(s_lp, 1)

            def first_state(b):
                pe.wait_ge(s_xe, b + 1)
                pe.wait_ge(s_gts, b + 1)
                te.matmul(ps[0:NSTATE, 6, 0:D_INNER], b_tok[:, b % 2], xend[:, b % 2], start=True, stop=True
                          ).then_inc(s_stp, 1)

            def state_y(b):
                pe.wait_ge(s_st, b + 1)
                te.matmul(ps[:, 6, 0:D_INNER], cT[0:NSTATE, SEQ * b + P:SEQ * (b + 1)], state[0:NSTATE, b % 2],
                          start=True, stop=True).then_inc(s_yip, 1)

            def y_transpose(b):
                pe.wait_ge(s_yg, b + 1)
                if b:
                    pe.wait_ge(s_ygT, b)
                for k in range(2):
                    for i in range(2):
                        mm = te.transpose(ps[:, 3, SEQ * k + P * i:SEQ * k + P * (i + 1)],
                                          ygt[:, b % 2, i, P * k:P * (k + 1)], ident[:])
                mm.then_inc(s_yt, 1)

            def out3(c):
                pe.wait_ge(s_ygT, 2 * c + 2)
                if c == 1:
                    pe.wait_ge(s_mv, 6 * NC + c)
                if c == 2:
                    pe.wait_ge(s_xs, BATCH)
                for i in range(CT):
                    t = CT * c + i
                    for k in range(2):
                        mm = te.matmul(ps[:, out3_bank(c), P * i:P * (i + 1)], ygT[:, k, P * t:P * (t + 1)],
                                       wT[:, W3OUT + P * k:W3OUT + P * (k + 1)], start=(k == 0), stop=(k == 1))
                mm.then_inc(s_out, 1)

            x_tokens(0)
            scores(0)
            decays(0)
            decays(1)
            pe.wait_ge(s_nw, 1)
            for p in range(2 * BATCH):
                b, half = divmod(p, 2)
                if half == 0:
                    first_state(b)
                if p + 2 < 2 * BATCH:
                    decays(p + 2)
                if half and b + 1 < BATCH:
                    scores(b + 1)
                if half == 0:
                    pe.wait_ge(s_xs, b + 1)
                    if b >= 2:
                        pe.wait_ge(s_yd, b - 1)
                pe.wait_ge(s_mm, p + 1)
                for h in range(2):
                    for i in range(2):
                        at = D_INNER * i + HEAD3 * (2 * half + h)
                        mm = te.matmul(ps[:, ssd_bank(b), at:at + HEAD3], mring[:, p % 3, h, i, :],
                                       xs[:, 2 * b + i, 2 * half + h, :], start=True, stop=True)
                mm.then_inc(s_yq, 1)
                if half == 0:
                    if b + 1 < BATCH:
                        x_tokens(b + 1)
                    state_y(b)
                else:
                    if b:
                        y_transpose(b - 1)
                    if b in (3, 5, 7):
                        out3((b - 3) // 2)

            def key_receptance(c):
                b = slice(2 * c, 2 * c + 2)
                pe.wait_ge(s_xk, c + 1)
                if c >= 2:
                    pe.wait_ge(s_kr, c - 1)
                te.matmul(ps[:, 4 + c % 2, :], wT[:, WK:WK + P], xk[:, b, :], start=True, stop=True).then_inc(s_kp, 1)
                pe.wait_ge(s_xr, c + 1)
                if c >= 2:
                    pe.wait_ge(s_rs, c - 1)
                xrf = xr.rearrange("p b t -> p (b t)")
                for i in range(CT):
                    t = CT * c + i
                    mm = te.matmul(ps[:, 6 + c % 2, P * i:P * (i + 1)], xrf[:, P * t:P * (t + 1)],
                                   wT[:, WR:WR + P], start=True, stop=True)
                mm.then_inc(s_rp, 1)

            def value(c):
                pe.wait_ge(s_ka2, c + 1)
                for i in range(CT):
                    t = CT * c + i
                    mm = te.matmul(ps[:, c, P * i:P * (i + 1)], kact[:, P * t:P * (t + 1)],
                                   wT[:, WV:WV + P], start=True, stop=True)
                mm.then_inc(s_out, 1)

            pe.wait_ge(s_mv, 6 * NC + 2)
            x_transpose(7, 0)
            y_transpose(BATCH - 1)
            x_transpose(7, 1)
            out3(3)
            key_receptance(0)
            key_receptance(1)
            value(0)
            x_transpose(7, 2)
            value(1)
            x_transpose(7, 3)
            key_receptance(2)
            key_receptance(3)
            value(2)
            value(3)


def kernel(**inputs):
    import concourse.bacc as _bacc
    from concourse.bass_utils import run_bass_kernel_spmd as _run

    nc = _bacc.Bacc("TRN2", target_bir_lowering=False, num_devices=1)
    arrays, aps = {}, {}
    for name in inputs:
        a = np.ascontiguousarray(inputs[name])
        arrays["in_" + name] = a
        aps[name] = nc.dram_tensor("in_" + name, a.shape, mybir.dt.from_np(a.dtype), kind="ExternalInput").ap()
    fwd, inv = fourier_constants()
    arrays["fourier_fwd"], arrays["fourier_inv"] = fwd, inv
    fwd_ap = nc.dram_tensor("fourier_fwd", fwd.shape, F32, kind="ExternalInput").ap()
    inv_ap = nc.dram_tensor("fourier_inv", inv.shape, F32, kind="ExternalInput").ap()
    out = nc.dram_tensor("out", (BATCH, SEQ, P), F32, kind="ExternalOutput").ap()
    build(nc, aps, fwd_ap, inv_ap, out)
    r = _run(nc, [arrays], core_ids=[0])
    return r.results[0]["out"]
```
